# Optimizing a Trainium2 kernel written in Bass

```python
import numpy as np
import jax
import jax.numpy as jnp

def _softmax(x, axis=-1):
    return jax.nn.softmax(x, axis=axis)

def _gelu(x):
    return jax.nn.gelu(x, approximate=True)

def _silu(x):
    return jax.nn.silu(x)

def _sigmoid(x):
    return jax.nn.sigmoid(x)

def _layernorm(x, axis=-1, eps=1e-05):
    m = jnp.mean(x, axis=axis, keepdims=True)
    v = jnp.var(x, axis=axis, keepdims=True)
    return (x - m) / jnp.sqrt(v + eps)

def _scatter_add(tgt, idx, src, axis=0):
    return tgt.at[idx].add(src)

def _segment_sum(src, seg, n):
    return jax.ops.segment_sum(src, seg, n)
kernel_name = 'mk_gnn_ffn_d1_gnn_r32_a9129f'

def setup_inputs(seed: int=0):
    np.random.seed(seed)
    _w = jnp.asarray

    def _rec_inputs():
        import jax
        import jax.numpy as jnp
        _gk = jax.random.key(seed)
        x = -0.0001126 + 1 * jax.random.normal(jax.random.fold_in(_gk, 1), (3125, 256), jnp.float32)
        src = jax.random.randint(jax.random.fold_in(_gk, 2), (50000,), 0, 3125, jnp.int32)
        dst = jnp.minimum((3125 * jax.random.uniform(jax.random.fold_in(_gk, 3), (50000,)) ** 2.0).astype(jnp.int32), 99999)
        _o = jnp.argsort(dst, stable=True)
        src = src[_o]
        dst = dst[_o]
        edge_type_8 = jax.random.randint(jax.random.fold_in(_gk, 12), (50000,), 0, 8, jnp.int32)
        return (x, src, dst, edge_type_8)
    x, src, dst, edge_type_8 = _rec_inputs()

    def _L0_gnn_setup():
        import jax, jax.numpy as jnp
        import numpy as np
        N = 30000
        E = 18750
        FIN = 256
        FOUT = 256
        R = 8
        key = jax.random.key(seed)
        ks = jax.random.split(key, 6)
        x = jax.random.normal(ks[0], (N, FIN), dtype=jnp.float32)
        W = jax.random.normal(ks[1], (R, FIN, FOUT), dtype=jnp.float32) * (1.0 / np.sqrt(FIN))
        W_root = jax.random.normal(ks[2], (FIN, FOUT), dtype=jnp.float32) * (1.0 / np.sqrt(FIN))
        bias = jax.random.normal(ks[3], (FOUT,), dtype=jnp.float32) * 0.01
        edge_index = jax.random.randint(ks[4], (2, E), 0, N, dtype=jnp.int64)
        edge_type = jax.random.randint(ks[5], (E,), 0, R, dtype=jnp.int64)
        return {'x': x, 'W': W, 'W_root': W_root, 'bias': bias, 'edge_index': edge_index, 'edge_type': edge_type}
    _L0_gnn_all = _L0_gnn_setup()
    _L0_gnn_in = {k: v for k, v in _L0_gnn_all.items() if k in ('W', 'W_root', 'bias')}
    del _L0_gnn_all

    def _L0_ffn_setup():
        import jax, jax.numpy as jnp
        import numpy as np
        TOP_K = 2
        LN_EPS = 1e-05
        key = jax.random.key(seed)
        ks = jax.random.split(key, 8)
        B, S, D, E, H = (16, 1024, 256, 8, 1024)
        x = jax.random.normal(ks[0], (B, S, D), dtype=jnp.float32)
        Wr = jax.random.normal(ks[1], (D, E), dtype=jnp.float32) * 0.1
        br = jnp.zeros((E,), dtype=jnp.float32)
        ln_g = jnp.ones((E, D), dtype=jnp.float32)
        ln_b = jnp.zeros((E, D), dtype=jnp.float32)
        W1 = jax.random.normal(ks[2], (E, D, H), dtype=jnp.float32) * (1.0 / np.sqrt(D))
        b1 = jnp.zeros((E, H), dtype=jnp.float32)
        W2 = jax.random.normal(ks[3], (E, H, D), dtype=jnp.float32) * (1.0 / np.sqrt(H))
        b2 = jnp.zeros((E, D), dtype=jnp.float32)
        return {'x': x, 'Wr': Wr, 'br': br, 'ln_g': ln_g, 'ln_b': ln_b, 'W1': W1, 'b1': b1, 'W2': W2, 'b2': b2}
    _L0_ffn_all = _L0_ffn_setup()
    _L0_ffn_in = {k: v for k, v in _L0_ffn_all.items() if k in ('Wr', 'br', 'ln_g', 'ln_b', 'W1', 'b1', 'W2', 'b2')}
    del _L0_ffn_all
    return {'x': x, 'src': src, 'dst': dst, 'edge_type_8': edge_type_8, 'L0_gnn_W': _L0_gnn_in['W'], 'L0_gnn_W_root': _L0_gnn_in['W_root'], 'L0_gnn_bias': _L0_gnn_in['bias'], 'L0_ffn_Wr': _L0_ffn_in['Wr'], 'L0_ffn_br': _L0_ffn_in['br'], 'L0_ffn_ln_g': _L0_ffn_in['ln_g'], 'L0_ffn_ln_b': _L0_ffn_in['ln_b'], 'L0_ffn_W1': _L0_ffn_in['W1'], 'L0_ffn_b1': _L0_ffn_in['b1'], 'L0_ffn_W2': _L0_ffn_in['W2'], 'L0_ffn_b2': _L0_ffn_in['b2']}

def reference(x, src, dst, edge_type_8, L0_gnn_W, L0_gnn_W_root, L0_gnn_bias, L0_ffn_Wr, L0_ffn_br, L0_ffn_ln_g, L0_ffn_ln_b, L0_ffn_W1, L0_ffn_b1, L0_ffn_W2, L0_ffn_b2):
    import jax
    import jax.numpy as jnp

    def _L0_gnn_ref(x, W, W_root, bias, edge_index, edge_type):
        import jax, jax.numpy as jnp
        import numpy as np
        N = 30000
        E = 18750
        FIN = 256
        FOUT = 256
        R = 8
        n, fin = x.shape
        r = W.shape[0]
        src, dst = (edge_index[0], edge_index[1])
        seg = dst * r + edge_type
        sums = jax.ops.segment_sum(x[src], seg, num_segments=n * r)
        cnt = jax.ops.segment_sum(jnp.ones_like(src, dtype=x.dtype), seg, num_segments=n * r)
        mean = (sums / jnp.maximum(cnt, 1.0)[:, None]).reshape(n, r, fin)
        out = jnp.einsum('nri,rio->no', mean, W) + x @ W_root + bias
        return jax.nn.relu(out)

    def _L0_ffn_ref(x, Wr, br, ln_g, ln_b, W1, b1, W2, b2):
        import jax, jax.numpy as jnp
        import numpy as np
        TOP_K = 2
        LN_EPS = 1e-05
        B, S, D = x.shape
        N = B * S
        xt = x.reshape(N, D)
        logits = xt @ Wr + br
        probs = jax.nn.softmax(logits, axis=-1)
        top_p, top_idx = jax.lax.top_k(probs, TOP_K)
        weights = top_p / top_p.sum(axis=-1, keepdims=True)
        mu = xt.mean(axis=-1, keepdims=True)
        var = ((xt - mu) ** 2).mean(axis=-1, keepdims=True)
        xn = (xt - mu) * jax.lax.rsqrt(var + LN_EPS)
        xe = xn[None, :, :] * ln_g[:, None, :] + ln_b[:, None, :]
        h = jax.nn.gelu(jnp.einsum('end,edh->enh', xe, W1) + b1[:, None, :], approximate=False)
        y = jnp.einsum('enh,ehd->end', h, W2) + b2[:, None, :]
        y_tok = jnp.transpose(y, (1, 0, 2))
        sel = jnp.take_along_axis(y_tok, top_idx[:, :, None], axis=1)
        out = (weights[:, :, None] * sel).sum(axis=1)
        return out.reshape(B, S, D)
    edge_index = jnp.stack([src, dst])
    x = x + _L0_gnn_ref(_layernorm(x, axis=-1), L0_gnn_W, L0_gnn_W_root, L0_gnn_bias, edge_index, edge_type_8)
    x = x + _L0_ffn_ref(_layernorm(x, axis=-1)[None], L0_ffn_Wr, L0_ffn_br, L0_ffn_ln_g, L0_ffn_ln_b, L0_ffn_W1, L0_ffn_b1, L0_ffn_W2, L0_ffn_b2)[0]
    return x

_drawn_inputs = setup_inputs


def setup_inputs(seed=0):
    import zlib

    import numpy as np

    out = dict(_drawn_inputs(seed))
    spreads = {'L0_ffn_br': (0.0, 0.1),
     'L0_ffn_ln_g': (1.0, 0.2),
     'L0_ffn_ln_b': (0.0, 0.287),
     'L0_ffn_b1': (0.0, 0.282),
     'L0_ffn_b2': (0.0, 0.1)}
    factors = {'L0_gnn_bias': 5.334}
    for name, (base, spread) in spreads.items():
        noise = np.random.default_rng([zlib.crc32(name.encode()), seed]).standard_normal(out[name].shape)
        drawn = base * np.exp(spread * noise) if base else spread * noise
        out[name] = jnp.asarray(drawn.astype(out[name].dtype))
    for name, factor in factors.items():
        out[name] = (out[name] * factor).astype(out[name].dtype)
    return out
```

```python
from contextlib import ExitStack

import concourse.bass as bass
from concourse import mybir

P = 128
F32, F16 = mybir.dt.float32, mybir.dt.float16
I32, U32 = mybir.dt.int32, mybir.dt.uint32
ALU = mybir.AluOpType
ACT = mybir.ActivationFunctionType
AX = mybir.AxisListType
ENG = mybir.EngineType
ds = bass.ds

W_SCALE = 64.0
EPS = 1e-5
FAR = 1.0e6


def ceil_div(a, b):
    return -(-a // b)


def wait_from_first(eng, sem, value):
    if not (isinstance(value, int) and value <= 0):
        eng.wait_ge(sem, value)


def build(nc, a, out):
    N, D = a["x"].shape
    E = a["src"].shape[0]
    R = a["L0_gnn_W"].shape[0]
    NX = a["L0_ffn_Wr"].shape[1]
    H = a["L0_ffn_W1"].shape[2]
    NT = ceil_div(N, P)
    LAST = N - (NT - 1) * P
    ET = ceil_div(E, P)
    EC = ceil_div(ET, P)
    KC = D // P
    HC = H // P
    UNROLL = 8
    COUNT_STEPS = ceil_div(ET + NT - 1, NT)
    GROUPS = ceil_div(ET + NT - 1, UNROLL)
    PAIRS = GROUPS * UNROLL
    PW = max(COUNT_STEPS * NT, PAIRS + UNROLL)
    PW = ceil_div(PW, UNROLL) * UNROLL
    DUMMY = NT
    ST = (2 * N) // P + NX
    assert PW <= 512 and ST % 2 == 0 and KC == 2 and NT % 2 == 1 and D == 256

    x, src, dst, typ = a["x"], a["src"], a["dst"], a["edge_type_8"]
    y_table = nc.dram_tensor("y_table", (NT * P * R, D), F32).ap()
    xn_table = nc.dram_tensor("xn_table", (NT * P, D), F32).ap()

    with ExitStack() as whole:
        def sem(name):
            return whole.enter_context(nc.semaphore(name))

        def sb(name, shape, dt, ctx=whole):
            return ctx.enter_context(nc.sbuf_tensor(name, shape, dt))

        def ps(name, ctx, shape=(P, 512), dt=F32):
            return ctx.enter_context(nc.psum_tensor(name, list(shape), dt))

        ident = sb("ident", [P, P], F32)
        lower = sb("lower", [P, P], F32)
        ones = sb("ones", [P, P], F32)
        iota_row = sb("iota_row", [P, P], F32)
        iota_col = sb("iota_col", [P, NT], F32)
        params = sb("params", [P, 2 * KC * NX + HC * NX], F32)
        b2_rows = sb("b2_rows", [P, NX, D], F32)
        br_row = sb("br_row", [P, NX], F32)
        wr = sb("wr", [P, KC, NX], F32)
        acc = sb("acc", [P, NT + 1, D], F32)
        G0, B0, B10 = 0, KC * NX, 2 * KC * NX

        rows_loaded = sem("rows_loaded")
        consts_ready, steps = sem("consts_ready"), sem("dve_steps")
        done_steps = [0]

        def link(dve, ins):
            done_steps[0] += 1
            ins.then_inc(steps, 1)
            dve.wait_ge(steps, done_steps[0])

        def inverse_of_root(dve, result, root, value):
            link(dve, nc.vector.reciprocal(result[:], root[:]))
            link(dve, nc.vector.tensor_tensor(result[:], result[:], value[:], ALU.mult))
            link(dve, nc.vector.tensor_tensor(root[:], root[:], result[:], ALU.add))
            link(dve, nc.vector.tensor_scalar(root[:], root[:], 0.5, None, ALU.mult))
            link(dve, nc.vector.reciprocal(result[:], root[:]))

        dst_rel = sb("dst_rel", [P, PW], F32)
        row_idx = sb("row_idx", [P, PW], U32)
        blk_f = sb("blk_f", [P, PW], F32)
        blk = sb("blk", [P, PW], I32)
        rel_hot = sb("rel_hot", [P, PW, R], F16)
        iota_h = sb("iota_h", [P, P], F16)
        ident_h = sb("ident_h", [P, P], F16)
        cnt = sb("cnt", [P, NT + 1, R], F32)
        inv = sb("inv", [P, NT + 1, R], F32)

        with ExitStack() as to2:
            xs = sb("xs", [P, NT, D], F32, to2)
            wg32 = sb("wg32", [P, KC, R + 1, D], F32, to2)
            wgh = sb("wgh", [P, KC, (R + 1) * D], F16, to2)
            wgl = sb("wgl", [P, KC, (R + 1) * D], F16, to2)
            bias_row = sb("bias_row", [P, D], F32, to2)

            with ExitStack() as s1:
                dst_i = sb("dst_i", [P, EC, P], I32, s1)
                src_i = sb("src_i", [P, EC, P], I32, s1)
                typ_i = sb("typ_i", [P, EC, P], I32, s1)
                dst_f = sb("dst_f", [P, EC, P], F32, s1)
                seg_f = sb("seg_f", [P, EC, P], F32, s1)
                typ_f = sb("typ_f", [P, EC, P], F32, s1)
                off_f = sb("off_f", [P, EC, P], F32, s1)
                pair_hot = sb("pair_hot", [P, EC, PW], F32, s1)
                before_end = sb("before_end", [P, EC, PW], F32, s1)
                iota_pair = sb("iota_pair", [P, PW], F32, s1)
                tile_no = sb("tile_no", [P, EC], F32, s1)
                first_i = sb("first_i", [P, EC], I32, s1)
                last_i = sb("last_i", [P, EC], I32, s1)
                last_s = sb("last_s", [P, EC], I32, s1)
                last_m = sb("last_m", [P, EC], F32, s1)
                first = sb("first", [P, EC], F32, s1)
                last = sb("last", [P, EC], F32, s1)
                span = sb("span", [P, EC], F32, s1)
                totals = sb("totals", [P, EC], F32, s1)
                carry = sb("carry", [P, EC], F32, s1)
                begin = sb("begin", [P, EC], F32, s1)
                end = sb("end", [P, EC], F32, s1)
                is_last = sb("is_last", [P, EC], F32, s1)
                beyond = sb("beyond", [P, EC], F32, s1)
                begin_v = sb("begin_v", [P, EC], F32, s1)
                end_v = sb("end_v", [P, EC], F32, s1)
                offset = sb("offset", [P, EC], F32, s1)
                blk_raw = sb("blk_raw", [P, PW], F32, s1)
                iota_rel = sb("iota_rel", [P, R], F32, s1)
                stats = sb("stats", [P, NT, 6], F32, s1)
                mv = sb("mv", [P, NT, 2], F32, s1)
                var_eps = sb("var_eps", [P, NT], F32, s1)
                std = sb("std", [P, NT], F32, s1)
                rstd = sb("rstd", [P, NT], F32, s1)
                var_ready, root_ready = sem("var_ready"), sem("root_ready")
                raw = sb("raw", [2 * KC * NX + HC * NX, P], F32, s1)
                p_prefix, p_total = ps("p_prefix", s1), ps("p_total", s1)
                p_dst, p_seg = ps("p_dst", s1), ps("p_seg", s1)
                p_typ, p_off = ps("p_typ", s1), ps("p_off", s1)
                p_par = ps("p_par", s1)

                pads_set, edges_loaded = sem("pads_set"), sem("edges_loaded")
                x_loaded, params_loaded = sem("x_loaded"), sem("params_loaded")
                wg_loaded, wgh_ready = sem("wg_loaded"), sem("wgh_ready")
                spans_ready, prefix_ready = sem("spans_ready"), sem("prefix_ready")
                hot_ready, pair_cols_ready = sem("hot_ready"), sem("pair_cols_ready")
                par_turned, ident_base = sem("par_turned"), sem("ident_base")

                FULL_C = E // (P * P)
                FULL_T = E // P - FULL_C * P
                TAIL = E - (E // P) * P

                with nc.Block() as block:
                    @block.sync
                    def _(sp):
                        sp.wait_ge(pads_set, 4)
                        for t, i in ((dst_i, dst), (src_i, src), (typ_i, typ)):
                            sp.dma_start(t[:, 0:FULL_C, :], i[0:FULL_C * P * P].rearrange(
                                "(c p e) -> p c e", c=FULL_C, p=P)).then_inc(edges_loaded, 16)
                            sp.dma_start(t[0:FULL_T, FULL_C, :], i[FULL_C * P * P:(E // P) * P].rearrange(
                                "(p e) -> p e", e=P)).then_inc(edges_loaded, 16)
                            sp.dma_start(t[FULL_T:FULL_T + 1, FULL_C, 0:TAIL], i[(E // P) * P:E].rearrange(
                                "(p e) -> p e", p=1)).then_inc(edges_loaded, 16)
                        sp.dma_start(xs[:, 0:NT - 1, :], x[0:(NT - 1) * P, :].rearrange(
                            "(t p) d -> p t d", p=P)).then_inc(x_loaded, 16)
                        sp.dma_start(xs[0:LAST, NT - 1, :], x[(NT - 1) * P:N, :]).then_inc(x_loaded, 16)

                    @block.scalar
                    def _(act):
                        for c in range(KC):
                            act.dma_start(wg32[:, c, 0:R, :], a["L0_gnn_W"][:, c * P:(c + 1) * P, :].rearrange(
                                "r k o -> k r o")).then_inc(wg_loaded, 16)
                            act.dma_start(wg32[:, c, R, :], a["L0_gnn_W_root"][c * P:(c + 1) * P, :]
                                          ).then_inc(wg_loaded, 16)
                        GB = KC * NX
                        act.dma_start(raw[0:GB, :], a["L0_ffn_ln_g"].rearrange("e (c k) -> (e c) k", k=P)
                                      ).then_inc(params_loaded, 16)
                        act.dma_start(raw[GB:2 * GB, :], a["L0_ffn_ln_b"].rearrange("e (c k) -> (e c) k", k=P)
                                      ).then_inc(params_loaded, 16)
                        act.dma_start(raw[2 * GB:, :], a["L0_ffn_b1"].rearrange("e (c k) -> (e c) k", k=P)
                                      ).then_inc(params_loaded, 16)
                        act.dma_start(bias_row[:], a["L0_gnn_bias"].partition_broadcast(P)).then_inc(rows_loaded, 16)
                        act.dma_start(br_row[:], a["L0_ffn_br"].partition_broadcast(P)).then_inc(rows_loaded, 16)
                        act.dma_start(b2_rows[:], a["L0_ffn_b2"].partition_broadcast(P)).then_inc(rows_loaded, 16)
                        act.dma_start(wr[:], a["L0_ffn_Wr"].rearrange("(c k) e -> k c e", k=P)
                                      ).then_inc(rows_loaded, 16)
                        act.wait_ge(wg_loaded, 16 * 2 * KC)
                        for c in range(KC):
                            nc.scalar.activation(wgh[:, c, :], wg32[:, c, :, :].rearrange("p r o -> p (r o)"),
                                                 ACT.Copy, scale=W_SCALE).then_inc(wgh_ready, 1)
                        act.wait_ge(var_ready, 1)
                        nc.scalar.activation(std[:], var_eps[:], ACT.Sqrt).then_inc(root_ready, 1)

                    @block.gpsimd
                    def _(pool):
                        pool.memset(dst_i[:, EC - 1, :], -1).then_inc(pads_set, 1)
                        pool.memset(src_i[:, EC - 1, :], 0).then_inc(pads_set, 1)
                        pool.memset(typ_i[:, EC - 1, :], 0).then_inc(pads_set, 1)
                        pool.memset(xs[:, NT - 1, :], 0.0).then_inc(pads_set, 1)
                        pool.memset(ones[:], 1.0).then_inc(ident_base, 1)
                        imp = dict(allow_small_or_imprecise_dtypes=True)
                        pool.iota(iota_row[:], [[1, P]], base=0, channel_multiplier=0, **imp).then_inc(consts_ready, 1)
                        pool.iota(iota_h[:], [[1, P]], base=0, channel_multiplier=0, **imp).then_inc(consts_ready, 1)
                        pool.iota(iota_col[:], [[P, NT]], base=0, channel_multiplier=1, **imp).then_inc(consts_ready, 1)
                        pool.iota(iota_pair[:], [[1, PW]], base=0, channel_multiplier=0, **imp).then_inc(consts_ready, 1)
                        pool.iota(iota_rel[:], [[1, R]], base=0, channel_multiplier=0, **imp).then_inc(consts_ready, 1)
                        pool.iota(tile_no[:], [[P, EC]], base=0, channel_multiplier=1, **imp).then_inc(consts_ready, 1)
                        pool.wait_ge(ident_base, 1)
                        pool.affine_select(out=ident[:], in_=ones[:], compare_op=ALU.is_equal, fill=0.0,
                                           base=0, pattern=[[-1, P]], channel_multiplier=1).then_inc(consts_ready, 1)
                        pool.affine_select(out=ident_h[:], in_=ones[:], compare_op=ALU.is_equal, fill=0.0,
                                           base=0, pattern=[[-1, P]], channel_multiplier=1).then_inc(consts_ready, 1)
                        pool.affine_select(out=lower[:], in_=ones[:], compare_op=ALU.is_gt, fill=0.0,
                                           base=0, pattern=[[1, P]], channel_multiplier=-1).then_inc(consts_ready, 1)

                    @block.vector
                    def _(dve):
                        V = nc.vector
                        V.memset(cnt[:], 0.0)
                        V.memset(acc[:, NT, :], 0.0)
                        dve.wait_ge(edges_loaded, 16 * 9)
                        dve.wait_ge(consts_ready, 9)
                        V.tensor_copy(dst_f[:], dst_i[:])
                        V.scalar_tensor_tensor(seg_f[:], src_i[:], float(R), typ_i[:], ALU.mult, ALU.add)
                        V.tensor_copy(typ_f[:], typ_i[:])
                        V.tensor_scalar(first_i[:], dst_i[:, :, 0], 7, None, ALU.arith_shift_right)
                        V.tensor_scalar(is_last[:], tile_no[:], float(ET - 1), FAR, ALU.is_equal, ALU.mult)
                        link(dve, V.tensor_scalar(beyond[:], tile_no[:], float(ET - 1), FAR, ALU.is_gt, ALU.mult))
                        link(dve, V.tensor_reduce(last_m[:], dst_f[:], AX.X, ALU.max))
                        link(dve, V.tensor_copy(last_i[:], last_m[:]))
                        link(dve, V.tensor_scalar(last_s[:], last_i[:], 7, None, ALU.arith_shift_right))
                        V.tensor_copy(first[:], first_i[:])
                        link(dve, V.tensor_copy(last[:], last_s[:]))
                        link(dve, V.scalar_tensor_tensor(span[:], last[:], 1.0, first[:], ALU.add, ALU.subtract))
                        V.engine_nop().then_inc(spans_ready, 1)
                        dve.wait_ge(prefix_ready, 1)
                        V.memset(carry[:, 0:1], 0.0)
                        link(dve, V.tensor_copy(totals[:], p_total[:, 0:EC]))
                        for c in range(1, EC):
                            link(dve, V.tensor_tensor(carry[:, c:c + 1], carry[:, c - 1:c], totals[:, c - 1:c], ALU.add))
                        link(dve, V.tensor_tensor(begin[:], p_prefix[:, 0:EC], carry[:], ALU.add))
                        V.tensor_tensor(begin_v[:], begin[:], beyond[:], ALU.add)
                        V.tensor_tensor(offset[:], first[:], begin[:], ALU.subtract)
                        link(dve, V.tensor_tensor(end[:], begin[:], span[:], ALU.add))
                        link(dve, V.tensor_tensor(end_v[:], end[:], is_last[:], ALU.add))
                        for c in range(EC):
                            V.tensor_scalar(off_f[:, c, :], ones[:], offset[:, c:c + 1], None, ALU.mult)
                            ins = V.tensor_scalar(before_end[:, c, :], iota_pair[:], end_v[:, c:c + 1], None, ALU.is_lt)
                        link(dve, ins)
                        for c in range(EC):
                            V.scalar_tensor_tensor(pair_hot[:, c, :], iota_pair[:], begin_v[:, c:c + 1],
                                                   before_end[:, c, :], ALU.is_ge, ALU.mult).then_inc(hot_ready, 1)
                        dve.wait_ge(x_loaded, 32)
                        for t in range(NT):
                            ins = V.bn_stats(stats[:, t, :], xs[:, t, :])
                        link(dve, ins)
                        for t in range(NT):
                            ins = V.bn_aggr(mv[:, t, :], stats[:, t, :])
                        link(dve, ins)
                        V.tensor_scalar(var_eps[:], mv[:, :, 1], EPS, None, ALU.add).then_inc(var_ready, 1)
                        dve.wait_ge(root_ready, 1)
                        inverse_of_root(dve, rstd, std, var_eps)
                        for t in range(NT):
                            V.tensor_scalar(xs[:, t, :], xs[:, t, :], mv[:, t, 0:1], rstd[:, t:t + 1],
                                            ALU.subtract, ALU.mult)
                        for c in range(KC):
                            dve.wait_ge(wgh_ready, c + 1)
                            V.scalar_tensor_tensor(wgl[:, c, :], wg32[:, c, :, :].rearrange("p r o -> p (r o)"),
                                                   W_SCALE, wgh[:, c, :], ALU.mult, ALU.subtract)
                        dve.wait_ge(par_turned, 1)
                        V.tensor_copy(params[:], p_par[:, 0:params.shape[1]])
                        dve.wait_ge(pair_cols_ready, 4)
                        link(dve, V.tensor_tensor(blk_raw[:], p_off[:, 0:PW], iota_pair[:], ALU.add))
                        link(dve, V.tensor_scalar(blk_f[:], blk_raw[:], float(DUMMY), None, ALU.min))
                        V.tensor_copy(blk[:], blk_f[:])
                        V.scalar_tensor_tensor(dst_rel[:], blk_f[:], -float(P), p_dst[:, 0:PW], ALU.mult, ALU.add)
                        V.tensor_copy(row_idx[:], p_seg[:, 0:PW])
                        V.tensor_tensor(rel_hot[:], p_typ[:, 0:PW].unsqueeze(2).to_broadcast([P, PW, R]),
                                        iota_rel[:].unsqueeze(1).to_broadcast([P, PW, R]), ALU.is_equal)

                    @block.tensor
                    def _(pe):
                        pe.wait_ge(consts_ready, 9)
                        pe.wait_ge(params_loaded, 48)
                        nr = raw.shape[0]
                        pe.transpose(p_par[:, 0:nr], raw[:], ident[0:nr, 0:nr]).then_inc(par_turned, 1)
                        pe.wait_ge(spans_ready, 1)
                        pe.matmul(p_prefix[:, 0:EC], lower[:], span[:], start=True, stop=True)
                        pe.matmul(p_total[:, 0:EC], ones[:], span[:], start=True, stop=True).then_inc(prefix_ready, 1)
                        pe.wait_ge(hot_ready, EC)
                        for t, p in ((off_f, p_off), (dst_f, p_dst), (seg_f, p_seg), (typ_f, p_typ)):
                            for c in range(EC):
                                mm = pe.matmul(p[:, 0:PW], t[:, c, :], pair_hot[:, c, :],
                                               start=(c == 0), stop=(c == EC - 1))
                            mm.then_inc(pair_cols_ready, 1)

            with ExitStack() as s2:
                CS, NY = COUNT_STEPS, R * D // 512
                parts = sb("parts", [P, 2, 2, D], F16, s2)
                xt = sb("xt", [P, 2, 2 * KC * P], F16, s2)
                ystage = sb("ystage", [P, 2, R * D], F32, s2)
                hot = sb("hot", [P, 2, CS, P], F16, s2)
                cnt_max = sb("cnt_max", [P, NT + 1, R], F32, s2)
                p_turn = ps("p_turn", s2, (P, 1024), F16)
                p_y = [ps("p_y0", s2), ps("p_y1", s2)]
                p_root = ps("p_root", s2)
                p_cnt = [ps("p_cnt0", s2), ps("p_cnt1", s2)]
                hi_split, lo_split = sem("hi_split"), sem("lo_split")
                turned, xt_ready = sem("turned"), sem("xt_ready")
                y_made, y_staged = sem("y_made"), sem("y_staged")
                y_stored = [sem("y_stored0"), sem("y_stored1")]
                root_made, root_kept = sem("root_made"), sem("root_kept")
                hots_made, counts_made, count_added = sem("hots_made"), sem("counts_made"), sem("count_added")
                y_rows = y_table.rearrange("(t p r) d -> t p (r d)", p=P, r=R)

                def tile_of(ap, t):
                    return ap[:, t, :] if isinstance(t, int) else ap[:, ds(t, 1), :].rearrange("p a d -> p (a d)")

                def over_tiles(eng, tick):
                    tick(0, 0, 0)
                    tick(1, 0, 1)
                    with eng.Fori(0, (NT - 5) // 2) as i:
                        tick(2 * i + 2, i + 1, 0)
                        tick(2 * i + 3, i + 1, 1)
                    for t in range(NT - 3, NT):
                        tick(t, t // 2, t % 2)

                def is_tile(t):
                    return not (isinstance(t, int) and t >= NT)

                with nc.Block() as block:
                    @block.tensor
                    def _(pe):
                        def turn(t, par):
                            pe.wait_ge(lo_split, t + 1)
                            wait_from_first(pe, xt_ready, t)
                            for n in range(2 * KC):
                                part, c = divmod(n, KC)
                                mm = pe.transpose(p_turn[:, n * P:(n + 1) * P],
                                                  parts[:, par, part, c * P:(c + 1) * P], ident_h[:])
                            mm.then_inc(turned, 1)

                        def tick(t, half, par):
                            if is_tile(t + 1):
                                turn(t + 1, 1 - par)
                            pe.wait_ge(xt_ready, t + 1)
                            for q in range(NY + 1):
                                lo, hi = q * 512, min((q + 1) * 512, (R + 1) * D)
                                if q < NY:
                                    o = p_y[q % 2][:, :]
                                    wait_from_first(pe, y_staged, NY * t + (q - 1))
                                else:
                                    o = p_root[:, 0:D]
                                    wait_from_first(pe, root_kept, t)
                                terms = [(xp, wp, c) for c in range(KC) for xp, wp in ((0, wgh), (0, wgl), (1, wgh))]
                                for n, (xp, wp, c) in enumerate(terms):
                                    mm = pe.matmul(o, xt[:, par, (xp * KC + c) * P:(xp * KC + c + 1) * P], wp[:, c, lo:hi],
                                                   start=(n == 0), stop=(n == len(terms) - 1))
                                mm.then_inc(y_made if q < NY else root_made, 1)
                            pe.wait_ge(hots_made, t + 1)
                            wait_from_first(pe, count_added, CS * (t - 1))
                            for j in range(CS):
                                mm = pe.matmul(p_cnt[par][:, j * R:(j + 1) * R], hot[:, par, j, :],
                                               tile_of(rel_hot, t * CS + j), start=True, stop=True)
                            mm.then_inc(counts_made, 1)

                        turn(0, 0)
                        over_tiles(pe, tick)

                    @block.scalar
                    def _(act):
                        def split_hi(t, par):
                            wait_from_first(act, turned, t - 1)
                            nc.scalar.activation(parts[:, par, 0, :], tile_of(xs, t), ACT.Copy).then_inc(hi_split, 1)

                        def keep_turned(t, par):
                            act.wait_ge(turned, t + 1)
                            wait_from_first(act, root_made, t - 1)
                            nc.scalar.activation(xt[:, par, :], p_turn[:, 0:2 * KC * P], ACT.Copy).then_inc(xt_ready, 1)

                        def tick(t, half, par):
                            if is_tile(t + 2):
                                split_hi(t + 2, par)
                            if is_tile(t + 1):
                                keep_turned(t + 1, 1 - par)
                            wait_from_first(act, y_stored[par], 16 * half)
                            for q in range(NY):
                                act.wait_ge(y_made, NY * t + (q + 1))
                                nc.scalar.activation(ystage[:, par, q * 512:(q + 1) * 512], p_y[q % 2][:, :],
                                                     ACT.Copy, scale=1.0 / W_SCALE).then_inc(y_staged, 1)

                        split_hi(0, 0)
                        split_hi(1, 1)
                        keep_turned(0, 0)
                        over_tiles(act, tick)

                    @block.sync
                    def _(sp):
                        def tick(t, half, par):
                            sp.wait_ge(y_staged, NY * t + NY)
                            row = y_rows[t, :, :] if isinstance(t, int) else \
                                y_rows[ds(t, 1), :, :].rearrange("a p d -> (a p) d")
                            sp.dma_start(row, ystage[:, par, :]).then_inc(y_stored[par], 16)

                        over_tiles(sp, tick)
                        sp.wait_ge(y_stored[0], 16 * ((NT + 1) // 2))
                        sp.wait_ge(y_stored[1], 16 * (NT // 2))

                    @block.vector
                    def _(dve):
                        V = nc.vector

                        def split_lo(t, par):
                            dve.wait_ge(hi_split, t + 1)
                            wait_from_first(dve, turned, t - 1)
                            V.tensor_tensor(parts[:, par, 1, :], tile_of(xs, t), parts[:, par, 0, :],
                                            ALU.subtract).then_inc(lo_split, 1)

                        def one_hot(t, par, j):
                            ins = V.tensor_scalar(hot[:, par, j, :], iota_h[:],
                                                  dst_rel[:, ds(t * CS + j, 1)], None, ALU.is_equal)
                            if j == CS - 1:
                                ins.then_inc(hots_made, 1)

                        def add_count(t, par, j, block_no):
                            if j == 0:
                                dve.wait_ge(counts_made, t + 1)
                            wait_from_first(dve, count_added, CS * t + j)
                            here = cnt[:, ds(block_no, 1), :].rearrange("p a r -> p (a r)")
                            V.tensor_tensor(here, p_cnt[par][:, j * R:(j + 1) * R], here, ALU.add).then_inc(count_added, 1)

                        def blocks_of(t):
                            return nc.values_load_multi_w_load_instructions(
                                blk[0:1, ds(t * CS, CS)], engines=(ENG.DVE,), min_val=0, max_val=DUMMY,
                                skip_runtime_bounds_check_because="clamped to DUMMY on chip")[1]

                        def tick(t, half, par):
                            if is_tile(t + 2):
                                split_lo(t + 2, par)
                            before = not (isinstance(t, int) and t == 0)
                            wait_from_first(dve, counts_made, t - 1)
                            nos = blocks_of(t - 1) if before else []
                            for j in range(CS):
                                one_hot(t, par, j)
                                if before:
                                    add_count(t - 1, 1 - par, j, nos[j])
                            dve.wait_ge(root_made, t + 1)
                            V.scalar_tensor_tensor(tile_of(acc, t), p_root[:, 0:D], 1.0 / W_SCALE, bias_row[:],
                                                   ALU.mult, ALU.add).then_inc(root_kept, 1)

                        dve.wait_ge(rows_loaded, 64)
                        split_lo(0, 0)
                        split_lo(1, 1)
                        over_tiles(dve, tick)
                        nos = blocks_of(NT - 1)
                        for j in range(CS):
                            add_count(NT - 1, (NT - 1) % 2, j, nos[j])
                        dve.wait_ge(count_added, CS * NT)
                        link(dve, V.tensor_scalar(cnt_max[:], cnt[:], 1.0, None, ALU.max))
                        V.reciprocal(inv[:], cnt_max[:])
        w1h = sb("w1h", [P, KC * NX, H], F16)
        w1l = sb("w1l", [P, KC * NX, H], F16)
        w2h = sb("w2h", [P, 2 * NX, HC // 2 * D], F16)
        w2l = sb("w2l", [P, 2 * NX, HC // 2 * D], F16)
        with ExitStack() as s3:
            U = UNROLL
            LOOKUP, WEIGH, SCALE, SUM, ADD = 1, 2, 3, 4, 6
            AHEAD = 5
            wstage = [sb(f"wstage{k}", [P, H], F32, s3) for k in range(2)]
            gathered = sb("gathered", [P, U, D], F32, s3)
            idx_now = sb("idx_now", [P, U], U32, s3)
            hot = sb("hot3", [P, 4, P], F16, s3)
            hot_t = sb("hot_t", [P, 2, P], F32, s3)
            hot_w = sb("hot_w", [P, 4, P], F32, s3)
            picked = sb("picked", [P, 2, R], F32, s3)
            weight = sb("weight", [P, 4], F32, s3)
            p_hot = [ps(f"p_hot{k}", s3, (P, 1024), F16) for k in range(2)]
            p_inv = [ps(f"p_inv{k}", s3) for k in range(2)]
            p_sum = [ps(f"p_sum{k}", s3) for k in range(4)]
            idx_set, hots3, hots_turned, hots_kept = sem("idx_set"), sem("hots3"), sem("hots_turned"), sem("hots_kept")
            inv_found, weighed, scaled = sem("inv_found"), sem("weighed"), sem("scaled")
            summed, added = sem("summed"), sem("added")
            rows_in = [sem(f"rows_in{k}") for k in range(U)]
            w_loaded = [sem("w1_loaded"), sem("w2_loaded")]
            w_hi, w_lo = sem("w_hi"), sem("w_lo")
            gather_clear = sem("gather_clear")
            w1_src = a["L0_ffn_W1"].rearrange("e (c k) h -> (e c) k h", k=P)
            w2_src = a["L0_ffn_W2"].rearrange("e (f q k) d -> (e f) k q d", f=2, k=P)
            PIECE = H // 2

            def col(ap, n):
                return ap[:, ds(n, 1)]

            def group(tick, g, units=None):
                for j in range(U):
                    tick(g * U + j, j, g, units)

            def over_groups(eng, group_of):
                group_of(0, None)
                with eng.Fori(0, KC * NX) as i:
                    group_of(i + 1, i)
                with eng.Fori(KC * NX + 1, GROUPS) as i:
                    group_of(i, None)

            def live(m):
                return not isinstance(m, int) or 0 <= m < PAIRS

            def blocks(g, lag, engine, n=U):
                if isinstance(g, int) and g == 0:
                    lo, n, skip = 0, U - lag, lag
                else:
                    lo, n, skip = g * U - lag, n, 0
                nos = nc.values_load_multi_w_load_instructions(
                    blk[0:1, ds(lo, n)], engines=(engine,), min_val=0, max_val=DUMMY,
                    skip_runtime_bounds_check_because="clamped to DUMMY on chip")[1]
                return [None] * skip + list(nos)

            with nc.Block() as block:
                @block.sync
                def _(sp):
                    def unit(i):
                        for k, source in enumerate((w1_src, w2_src)):
                            wait_from_first(sp, w_lo, 4 * i - (2 if k == 0 else 0))
                            if k == 0:
                                sp.dma_start(wstage[0][:], source[ds(i, 1), :, :].rearrange("a k h -> (a k) h")
                                             ).then_inc(w_loaded[0], 16)
                            else:
                                sp.dma_start(wstage[1][:].rearrange("p (q d) -> p q d", d=D),
                                             source[ds(i, 1), :, :, :].rearrange("a k q d -> (a k) q d")
                                             ).then_inc(w_loaded[1], 16)

                    unit(0)
                    with sp.Fori(1, KC * NX) as i:
                        unit(i)

                @block.gpsimd
                def _(pool):
                    def tick(m, j, g, units):
                        pool.wait_ge(idx_set, m + 1)
                        wait_from_first(pool, summed, m - U + 1)
                        pool.sem_inc(gather_clear)
                        pool.indirect_dma_start(
                            out=gathered[:, j, :], out_offset=None, in_=y_table[:, :],
                            in_offset=bass.IndirectOffsetOnAxis(ap=idx_now[:, j:j + 1], axis=0),
                        ).then_inc(rows_in[j], 16)

                    over_groups(pool, lambda g, units: group(tick, g, units))

                @block.scalar
                def _(act):
                    def set_idx(m, j):
                        if live(m):
                            if not (isinstance(m, int) and m < U):
                                act.wait_ge(rows_in[j], 16 * (m // U) if isinstance(m, int) else m_rows[0])
                            nc.scalar.activation(idx_now[:, j:j + 1], col(row_idx, m), ACT.Copy).then_inc(idx_set, 1)

                    m_rows = [None]

                    def tick(n, j, g, units):
                        late = (j + AHEAD) // U
                        if not isinstance(n, int):
                            m_rows[0] = 16 * (g + late)
                        set_idx(n + AHEAD, (j + AHEAD) % U)
                        act.wait_ge(hots_turned, n + 1)
                        wait_from_first(act, inv_found, n - 1)
                        nc.scalar.activation(hot_t[:, j % 2, :], p_hot[j % 2][:, 0:P], ACT.Copy).then_inc(hots_kept, 1)
                        if units is not None and j % 2:
                            k, piece = divmod(j // 2, 2)
                            act.wait_ge(w_loaded[k], 16 * units + 16)
                            to = (w1h, w2h)[k][:, ds(units, 1), piece * PIECE:(piece + 1) * PIECE].rearrange("p a n -> p (a n)")
                            nc.scalar.activation(to, wstage[k][:, piece * PIECE:(piece + 1) * PIECE],
                                                 ACT.Copy, scale=W_SCALE).then_inc(w_hi, 1)

                    for m in range(AHEAD):
                        set_idx(m, m)
                    over_groups(act, lambda g, units: group(tick, g, units))

                @block.tensor
                def _(pe):
                    def sum_pair(m, j, g_of):
                        if live(m):
                            pe.wait_ge(scaled, m + 1)
                            pe.wait_ge(rows_in[j % U], 16 * (g_of + 1))
                            wait_from_first(pe, added, m - 3)
                            pe.matmul(p_sum[j % 4][:, 0:D], hot_w[:, j % 4, :], gathered[:, j % U, :],
                                      start=True, stop=True).then_inc(summed, 1)

                    def lookup(m, j, block_no):
                        if live(m):
                            pe.wait_ge(hots_kept, m + 1)
                            wait_from_first(pe, weighed, m - 1)
                            pe.matmul(p_inv[j % 2][:, 0:R], hot_t[:, j % 2, :],
                                      inv[:, ds(block_no, 1), :].rearrange("p a r -> p (a r)"),
                                      start=True, stop=True).then_inc(inv_found, 1)

                    def group_of(g, units):
                        nos = blocks(g, LOOKUP, ENG.PE)
                        for j in range(U):
                            n = g * U + j
                            pe.wait_ge(hots3, n + 1)
                            wait_from_first(pe, hots_kept, n - 1)
                            pe.transpose(p_hot[j % 2][:, 0:P], hot[:, j % 4, :], ident_h[:]).then_inc(hots_turned, 1)
                            lookup(n - LOOKUP, (j - LOOKUP) % U, nos[j])
                            sum_pair(n - SUM, (j - SUM) % U, g if j >= SUM else g - 1)

                    over_groups(pe, group_of)
                    nos = blocks(GROUPS, LOOKUP, ENG.PE, LOOKUP)
                    for j in range(SUM):
                        if j < LOOKUP:
                            lookup(PAIRS + j - LOOKUP, (j - LOOKUP) % U, nos[j])
                        sum_pair(PAIRS + j - SUM, (j - SUM) % U, GROUPS - 1)

                @block.vector
                def _(dve):
                    V = nc.vector

                    def weigh(m, j):
                        if live(m):
                            dve.wait_ge(inv_found, m + 1)
                            wait_from_first(dve, scaled, m - 3)
                            V.scalar_tensor_tensor(picked[:, j % 2, :], p_inv[j % 2][:, 0:R], 1.0,
                                                   rel_hot[:, ds(m, 1), :].rearrange("p a r -> p (a r)"),
                                                   ALU.mult, ALU.mult, accum_out=weight[:, j % 4:j % 4 + 1]).then_inc(weighed, 1)

                    def scale(m, j):
                        if live(m):
                            dve.wait_ge(weighed, m + 1)
                            wait_from_first(dve, summed, m - 3)
                            V.tensor_scalar(hot_w[:, j % 4, :], iota_row[:], col(dst_rel, m),
                                            weight[:, j % 4:j % 4 + 1], ALU.is_equal, ALU.mult).then_inc(scaled, 1)

                    def add(m, j, block_no):
                        if live(m):
                            dve.wait_ge(summed, m + 1)
                            wait_from_first(dve, added, m)
                            here = acc[:, ds(block_no, 1), :].rearrange("p a d -> p (a d)")
                            V.tensor_tensor(here, p_sum[j % 4][:, 0:D], here, ALU.add).then_inc(added, 1)

                    def group_of(g, units):
                        nos = blocks(g, ADD, ENG.DVE)
                        for j in range(U):
                            n = g * U + j
                            wait_from_first(dve, hots_turned, n - 3)
                            V.tensor_scalar(hot[:, j % 4, :], iota_h[:], col(dst_rel, n), None, ALU.is_equal).then_inc(hots3, 1)
                            weigh(n - WEIGH, (j - WEIGH) % U)
                            scale(n - SCALE, (j - SCALE) % U)
                            add(n - ADD, (j - ADD) % U, nos[j])
                            if units is not None and j % 2:
                                k, piece = divmod(j // 2, 2)
                                dve.wait_ge(w_hi, 4 * units + (j // 2 + 1))
                                at = slice(piece * PIECE, (piece + 1) * PIECE)
                                hi = (w1h, w2h)[k][:, ds(units, 1), at].rearrange("p a n -> p (a n)")
                                lo = (w1l, w2l)[k][:, ds(units, 1), at].rearrange("p a n -> p (a n)")
                                V.scalar_tensor_tensor(lo, wstage[k][:, at], W_SCALE, hi, ALU.mult, ALU.subtract).then_inc(w_lo, 1)

                    over_groups(dve, group_of)
                    nos = blocks(GROUPS, ADD, ENG.DVE, ADD)
                    for j in range(ADD):
                        weigh(PAIRS + j - WEIGH, (j - WEIGH) % U)
                        scale(PAIRS + j - SCALE, (j - SCALE) % U)
                        add(PAIRS + j - ADD, (j - ADD) % U, nos[j])
        logits = sb("logits", [P, NT, NX], F32)
        slot_read = sb("slot_read", [P, ST], F32)
        slot_add = sb("slot_add", [P, ST], F32)
        slot_w = sb("slot_w", [P, ST], F32)
        tile_expert = sb("tile_expert", [P, ST], I32)
        TG = 5
        NG = NT // TG
        assert NT == TG * NG and NG % 2 == 1 and NG >= 3

        def over_pairs(eng, count, tick):
            tail = 2 + count % 2
            tick(0, 0, 0)
            tick(1, 0, 1)
            if count - tail > 2:
                with eng.Fori(0, (count - tail - 2) // 2) as i:
                    tick(2 * i + 2, i + 1, 0)
                    tick(2 * i + 3, i + 1, 1)
            for i in range(max(2, count - tail), count):
                tick(i, i // 2, i % 2)

        def row_group(t, n, ap):
            return ap[ds(t * P, n * P), :].rearrange("(t p) d -> p t d", p=P)

        with ExitStack() as s4:
            xr = sb("xr", [P, 2, TG, D], F32, s4)
            xn = sb("xn", [P, TG, D], F32, s4)
            xr_t = sb("xr_t", [P, 2, D], F32, s4)
            stats = sb("stats4", [P, TG, 6], F32, s4)
            mv = sb("mv4", [P, TG, 2], F32, s4)
            var_eps, std, rstd = (sb(n, [P, TG], F32, s4) for n in ("var_eps4", "std4", "rstd4"))
            p_turn = [ps(f"p_turn4{k}", s4) for k in range(2)]
            p_logit = [ps(f"p_logit{k}", s4) for k in range(2)]
            xr_loaded = [sem("xr_loaded0"), sem("xr_loaded1")]
            x1_ready, x1_stored, xn_ready, xn_stored = sem("x1_ready"), sem("x1_stored"), sem("xn_ready"), sem("xn_stored")
            ln_ready, var_ready, root_ready = sem("ln_ready"), sem("var_ready4"), sem("root_ready4")
            turned, kept, tile_logit, logit_kept = sem("turned4"), sem("kept4"), sem("tile_logit"), sem("logit_kept")

            with nc.Block() as block:
                @block.sync
                def _(sp):
                    def load(g, half, par):
                        if isinstance(g, int) and g == NG - 1:
                            sp.dma_start(xr[:, par, 0:TG - 1, :], row_group(g * TG, TG - 1, x)).then_inc(xr_loaded[par], 16)
                            sp.dma_start(xr[0:LAST, par, TG - 1, :], x[(NT - 1) * P:N, :]).then_inc(xr_loaded[par], 16)
                        else:
                            sp.dma_start(xr[:, par, :, :], row_group(g * TG, TG, x)).then_inc(xr_loaded[par], 16)

                    def tick(g, half, par):
                        sp.wait_ge(x1_ready, g + 1)
                        tiles = acc[:, ds(g * TG, TG), :]
                        sp.dma_start(row_group(g * TG, TG, out), tiles).then_inc(x1_stored, 16)
                        sp.wait_ge(xn_ready, g + 1)
                        sp.dma_start(row_group(g * TG, TG, xn_table), xn[:]).then_inc(xn_stored, 16)
                        if not isinstance(g, int) or g + 2 < NG:
                            sp.wait_ge(turned, TG * g + TG)
                            load(g + 2, half + 1, par)

                    load(0, 0, 0)
                    load(1, 0, 1)
                    over_pairs(sp, NG, tick)
                    sp.dma_start(out[NT * P:N + P, :], acc[0:N + P - NT * P, NT, :]).then_inc(x1_stored, 16)
                    sp.wait_ge(x1_stored, 16 * (NG + 1))
                    sp.wait_ge(xn_stored, 16 * NG)

                @block.vector
                def _(dve):
                    V = nc.vector

                    def norm(g, second, source, result):
                        for t in range(TG):
                            ins = V.bn_stats(stats[:, t, :], source(t))
                        ins.then_inc(ln_steps, 1)
                        dve.wait_ge(ln_steps, 2 * (2 * g + second) + 1)
                        for t in range(TG):
                            ins = V.bn_aggr(mv[:, t, :], stats[:, t, :])
                        ins.then_inc(ln_steps, 1)
                        dve.wait_ge(ln_steps, 2 * (2 * g + second) + 2)
                        V.tensor_scalar(var_eps[:], mv[:, :, 1], EPS, None, ALU.add).then_inc(var_ready, 1)
                        dve.wait_ge(root_ready, 2 * g + second + 1)
                        base = 5 * (2 * g + second)
                        for n, make in enumerate((
                                lambda: V.reciprocal(rstd[:], std[:]),
                                lambda: V.tensor_tensor(rstd[:], rstd[:], var_eps[:], ALU.mult),
                                lambda: V.tensor_tensor(std[:], std[:], rstd[:], ALU.add),
                                lambda: V.tensor_scalar(std[:], std[:], 0.5, None, ALU.mult),
                                lambda: V.reciprocal(rstd[:], std[:]))):
                            make().then_inc(newton_steps, 1)
                            dve.wait_ge(newton_steps, base + n + 1)
                        for t in range(TG):
                            ins = V.tensor_scalar(result(t), source(t), mv[:, t, 0:1], rstd[:, t:t + 1], ALU.subtract, ALU.mult)
                        return ins

                    def tick(g, half, par):
                        final = isinstance(g, int) and g == NG - 1
                        dve.wait_ge(xr_loaded[par], (16 * half + 32) if final else 16 * half + 16)

                        def node(t):
                            return acc[:, ds(g * TG + t, 1), :].rearrange("p a d -> p (a d)")

                        for t in range(TG):
                            ins = V.scalar_tensor_tensor(node(t), node(t), 0.0, xr[:, par, t, :], ALU.max, ALU.add)
                        ins.then_inc(x1_ready, 1)
                        dve.wait_ge(x1_ready, g + 1)
                        norm(g, 0, node, lambda t: xr[:, par, t, :]).then_inc(ln_ready, 1)
                        dve.wait_ge(ln_ready, g + 1)
                        wait_from_first(dve, xn_stored, 16 * g)
                        norm(g, 1, lambda t: xr[:, par, t, :], lambda t: xn[:, t, :]).then_inc(xn_ready, 1)
                        dve.wait_ge(tile_logit, TG * g + TG)
                        V.tensor_tensor(logits[:, ds(g * TG, TG), :],
                                        p_logit[par][:, 0:TG * NX].rearrange("p (t e) -> p t e", e=NX),
                                        br_row[:].unsqueeze(1).to_broadcast([P, TG, NX]), ALU.add).then_inc(logit_kept, 1)

                    ln_steps, newton_steps = sem("ln_steps"), sem("newton_steps")
                    over_pairs(dve, NG, tick)

                @block.scalar
                def _(act):
                    def tick(g, half, par):
                        act.wait_ge(var_ready, 2 * g + 1)
                        nc.scalar.activation(std[:], var_eps[:], ACT.Sqrt).then_inc(root_ready, 1)
                        act.wait_ge(var_ready, 2 * g + 2)
                        nc.scalar.activation(std[:], var_eps[:], ACT.Sqrt).then_inc(root_ready, 1)
                        for t in range(TG):
                            act.wait_ge(turned, TG * g + (t + 1))
                            if t < 2:
                                wait_from_first(act, tile_logit, TG * g)
                            else:
                                act.wait_ge(tile_logit, TG * g + (t - 1))
                            nc.scalar.activation(xr_t[:, t % 2, :], p_turn[t % 2][:, 0:D], ACT.Copy).then_inc(kept, 1)

                    over_pairs(act, NG, tick)

                @block.tensor
                def _(pe):
                    def tick(g, half, par):
                        def turn(t):
                            if t < 2:
                                wait_from_first(pe, kept, TG * g)
                            else:
                                pe.wait_ge(kept, TG * g + (t - 1))
                            for c in range(KC):
                                mm = pe.transpose(p_turn[t % 2][:, c * P:(c + 1) * P], xr[:, par, t, c * P:(c + 1) * P], ident[:])
                            mm.then_inc(turned, 1)

                        pe.wait_ge(ln_ready, g + 1)
                        wait_from_first(pe, logit_kept, g - 1)
                        turn(0)
                        for t in range(TG):
                            if t + 1 < TG:
                                turn(t + 1)
                            pe.wait_ge(kept, TG * g + (t + 1))
                            for c in range(KC):
                                mm = pe.matmul(p_logit[par][:, t * NX:(t + 1) * NX], xr_t[:, t % 2, c * P:(c + 1) * P],
                                               wr[:, c, :], start=(c == 0), stop=(c == KC - 1))
                            mm.then_inc(tile_logit, 1)

                    pe.wait_ge(rows_loaded, 64)
                    over_pairs(pe, NG, tick)

        with ExitStack() as s4b:
            def arr(name, shape, dt=F32):
                return sb(name, [P] + list(shape), dt, s4b)

            iota_e, iota_slot = arr("iota_e", [NX]), arr("iota_slot", [ST])
            hot_k = [arr(f"hot_k{k}", [NT, NX]) for k in range(2)]
            top = [arr(f"top{k}", [NT]) for k in range(2)]
            lower_than, cand, rest = (arr(n, [NT, NX]) for n in ("lower_than", "cand", "rest"))
            which, gap, ratio, one_more = (arr(n, [NT]) for n in ("which", "gap", "ratio", "one_more"))
            wk = arr("wk", [2, NT])
            valid, far, tok1 = (arr(n, [NT]) for n in ("valid", "far", "tok1"))
            chosen, both, scan0, scan1, place = (arr(n, [NT, NX]) for n in ("chosen", "both", "scan0", "scan1", "place"))
            fill, tiles_f, begin_e, end_e, base_e = (arr(n, [NX]) for n in ("fill", "tiles_f", "begin_e", "end_e", "base_e"))
            fill_i, tiles_i = arr("fill_i", [NX], I32), arr("tiles_i", [NX], I32)
            where = [arr(f"where{k}", [NT]) for k in range(2)]
            where_i, tile_i = arr("where_i", [2, NT], I32), arr("tile_i", [2, NT], I32)
            slot_tile, slot_row = arr("slot_tile", [2, NT]), arr("slot_row", [2, NT])
            ended, expert_f = arr("ended", [ST, NX]), arr("expert_f", [ST])
            row_hot, tile_vals = arr("row_hot", [2, P]), arr("tile_vals", [2, 2, ST])
            trash, unused = arr("trash", [1]), arr("unused", [ST])
            p_rank, p_tot, p_slot = ps("p_rank", s4b), ps("p_tot", s4b), ps("p_slot", s4b)
            iotas_ready, gap_ready, ratio_ready = sem("iotas_ready"), sem("gap_ready"), sem("ratio_ready")
            chosen_ready, ranks_ready = sem("chosen_ready"), sem("ranks_ready")
            vals_ready, vals_used = sem("vals_ready"), sem("vals_used")

            with nc.Block() as block:
                @block.gpsimd
                def _(pool):
                    imp = dict(allow_small_or_imprecise_dtypes=True)
                    pool.iota(iota_e[:], [[1, NX]], base=0, channel_multiplier=0, **imp).then_inc(iotas_ready, 1)
                    pool.iota(iota_slot[:], [[1, ST]], base=0, channel_multiplier=0, **imp).then_inc(iotas_ready, 1)
                    pool.iota(trash[:], [[0, 1]], base=N + 1, channel_multiplier=1, **imp).then_inc(iotas_ready, 1)

                @block.scalar
                def _(act):
                    act.wait_ge(gap_ready, 1)
                    nc.scalar.activation(ratio[:], gap[:], ACT.Exp).then_inc(ratio_ready, 1)

                @block.tensor
                def _(pe):
                    pe.wait_ge(chosen_ready, 1)
                    flat = chosen[:].rearrange("p t e -> p (t e)")
                    pe.matmul(p_rank[:, 0:NT * NX], lower[:], flat, start=True, stop=True)
                    pe.matmul(p_tot[:, 0:NT * NX], ones[:], flat, start=True, stop=True).then_inc(ranks_ready, 1)

                    def add_tile(t):
                        for k in range(2):
                            pe.wait_ge(vals_ready, 2 * t + (k + 1))
                            pe.matmul(p_slot[:, 0:2 * ST], row_hot[:, k, :], tile_vals[:, k, :, :].rearrange("p a s -> p (a s)"),
                                      start=(isinstance(t, int) and t + k == 0),
                                      stop=(isinstance(t, int) and t + k == NT)).then_inc(vals_used, 1)

                    add_tile(0)
                    with pe.Fori(1, NT - 1) as t:
                        add_tile(t)
                    add_tile(NT - 1)

                @block.vector
                def _(dve):
                    V = nc.vector
                    grid = [P, NT, NX]

                    def per_tile(ap):
                        return ap.unsqueeze(2).to_broadcast(grid)

                    def per_expert(ap):
                        return ap.unsqueeze(1).to_broadcast(grid)

                    dve.wait_ge(iotas_ready, 3)
                    for k, source in enumerate((logits, rest)):
                        link(dve, V.tensor_reduce(top[k][:], source[:], AX.X, ALU.max))
                        link(dve, V.tensor_tensor(lower_than[:], source[:], per_tile(top[k][:]), ALU.is_lt))
                        link(dve, V.scalar_tensor_tensor(cand[:], lower_than[:], 99.0, per_expert(iota_e[:]), ALU.mult, ALU.add))
                        link(dve, V.tensor_reduce(which[:], cand[:], AX.X, ALU.min))
                        link(dve, V.tensor_tensor(hot_k[k][:], per_expert(iota_e[:]), per_tile(which[:]), ALU.is_equal))
                        if k == 0:
                            link(dve, V.scalar_tensor_tensor(rest[:], hot_k[0][:], -1.0e30, logits[:], ALU.mult, ALU.add))
                    V.tensor_tensor(gap[:], top[1][:], top[0][:], ALU.subtract).then_inc(gap_ready, 1)
                    V.tensor_scalar(valid[:], iota_col[:], float(N), None, ALU.is_lt)
                    V.tensor_scalar(far[:], iota_col[:], float(N), FAR, ALU.is_ge, ALU.mult)
                    V.tensor_scalar(tok1[:], iota_col[:], 1.0, None, ALU.add)
                    link(dve, V.tensor_tensor(both[:], hot_k[0][:], hot_k[1][:], ALU.add))
                    V.tensor_tensor(chosen[:], both[:], per_tile(valid[:]), ALU.mult).then_inc(chosen_ready, 1)
                    dve.wait_ge(ratio_ready, 1)
                    link(dve, V.tensor_scalar(one_more[:], ratio[:], 1.0, None, ALU.add))
                    link(dve, V.reciprocal(wk[:, 0, :], one_more[:]))
                    link(dve, V.tensor_tensor(wk[:, 1, :], wk[:, 0, :], ratio[:], ALU.mult))
                    dve.wait_ge(ranks_ready, 1)
                    link(dve, V.tensor_copy(scan0[:], p_tot[:, 0:NT * NX].rearrange("p (t e) -> p t e", e=NX)))
                    old, new, shift = scan0, scan1, 1
                    while shift < NT:
                        V.tensor_copy(new[:, 0:shift, :], old[:, 0:shift, :])
                        link(dve, V.tensor_tensor(new[:, shift:, :], old[:, shift:, :], old[:, 0:NT - shift, :], ALU.add))
                        old, new, shift = new, old, 2 * shift
                    link(dve, V.tensor_scalar(fill[:], old[:, NT - 1, :], float(P - 1), None, ALU.add))
                    link(dve, V.tensor_copy(fill_i[:], fill[:]))
                    link(dve, V.tensor_scalar(tiles_i[:], fill_i[:], 7, None, ALU.arith_shift_right))
                    link(dve, V.tensor_copy(tiles_f[:], tiles_i[:]))
                    link(dve, V.memset(begin_e[:, 0:1], 0.0))
                    for e in range(1, NX):
                        link(dve, V.tensor_tensor(begin_e[:, e:e + 1], begin_e[:, e - 1:e], tiles_f[:, e - 1:e], ALU.add))
                    V.tensor_scalar(base_e[:], begin_e[:], float(P), None, ALU.mult)
                    link(dve, V.tensor_tensor(end_e[:], begin_e[:], tiles_f[:], ALU.add))
                    link(dve, V.tensor_tensor(ended[:], end_e[:].unsqueeze(1).to_broadcast([P, ST, NX]),
                                              iota_slot[:].unsqueeze(2).to_broadcast([P, ST, NX]), ALU.is_le))
                    link(dve, V.tensor_reduce(expert_f[:], ended[:], AX.X, ALU.add))
                    link(dve, V.tensor_scalar(expert_f[:], expert_f[:], float(NX - 1), None, ALU.min))
                    V.tensor_copy(tile_expert[:], expert_f[:])
                    link(dve, V.tensor_tensor(new[:], old[:], p_tot[:, 0:NT * NX].rearrange("p (t e) -> p t e", e=NX), ALU.subtract))
                    link(dve, V.tensor_tensor(place[:], new[:], p_rank[:, 0:NT * NX].rearrange("p (t e) -> p t e", e=NX), ALU.add))
                    link(dve, V.tensor_tensor(place[:], place[:], per_expert(base_e[:]), ALU.add))
                    for k in range(2):
                        link(dve, V.tensor_tensor(cand[:], place[:], hot_k[k][:], ALU.mult))
                        link(dve, V.tensor_reduce(where[k][:], cand[:], AX.X, ALU.add))
                        link(dve, V.tensor_copy(where_i[:, k, :], where[k][:]))
                        link(dve, V.tensor_scalar(tile_i[:, k, :], where_i[:, k, :], 7, None, ALU.arith_shift_right))
                        link(dve, V.tensor_copy(slot_tile[:, k, :], tile_i[:, k, :]))
                        link(dve, V.scalar_tensor_tensor(slot_row[:, k, :], slot_tile[:, k, :], -float(P), where[k][:], ALU.mult, ALU.add))
                        link(dve, V.tensor_tensor(slot_tile[:, k, :], slot_tile[:, k, :], far[:], ALU.add))

                    def tile_tick(t):
                        for k in range(2):
                            wait_from_first(dve, vals_used, 2 * t + (k - 1))
                            V.tensor_scalar(row_hot[:, k, :], iota_row[:], slot_row[:, k, ds(t, 1)], None, ALU.is_equal)
                            V.tensor_scalar(tile_vals[:, k, 0, :], iota_slot[:], slot_tile[:, k, ds(t, 1)], tok1[:, ds(t, 1)],
                                            ALU.is_equal, ALU.mult)
                            V.tensor_scalar(tile_vals[:, k, 1, :], iota_slot[:], slot_tile[:, k, ds(t, 1)], wk[:, k, ds(t, 1)],
                                            ALU.is_equal, ALU.mult).then_inc(vals_ready, 1)

                    tile_tick(0)
                    with dve.Fori(1, NT) as t:
                        tile_tick(t)
                    dve.wait_ge(vals_used, 2 * NT)
                    V.tensor_scalar(slot_read[:], p_slot[:, 0:ST], -1.0, 0.0, ALU.add, ALU.max)
                    link(dve, V.tensor_scalar(unused[:], p_slot[:, 0:ST], 0.0, trash[:, 0:1], ALU.is_equal, ALU.mult))
                    V.scalar_tensor_tensor(slot_add[:], p_slot[:, 0:ST], -1.0, unused[:], ALU.add, ALU.add)
                    V.tensor_copy(slot_w[:], p_slot[:, ST:2 * ST])

        with ExitStack() as s5:
            HALF = HC // 2
            rows = sb("rows", [P, 2, D], F32, s5)
            xe = sb("xe", [P, KC, P], F32, s5)
            xe_h = sb("xe_h", [P, 2, KC, P], F16, s5)
            xe_l = sb("xe_l", [P, 2, KC, P], F16, s5)
            h32 = sb("h32", [P, 2, HALF * P], F32, s5)
            h_h = sb("h_h", [P, 2, H], F16, s5)
            h_l = sb("h_l", [P, 2, H], F16, s5)
            y0 = sb("y0", [P, D], F32, s5)
            y = sb("y", [P, 2, D], F32, s5)
            read_now = sb("read_now", [P, 2], U32, s5)
            add_now = sb("add_now", [P, 2], U32, s5)
            p_x = ps("p_x", s5)
            p_h = [ps(f"p_h{k}", s5) for k in range(2)]
            p_y = [ps(f"p_y5{k}", s5) for k in range(2)]
            read_set, add_set, issue_clear = sem("read_set"), sem("add_set"), sem("issue_clear")
            rows_in = [sem("slot_rows_in0"), sem("slot_rows_in1")]
            y_added = [sem("y_added0"), sem("y_added1")]
            turned, xe_made, xe_hi, xe_ready = sem("turned5"), sem("xe_made"), sem("xe_hi"), sem("xe_ready")
            hidden_made, gelu_done, h_hi, h_ready = sem("hidden_made"), sem("gelu_done"), sem("h_hi"), sem("h_ready")
            y_made, y_part, y_ready = sem("y_made5"), sem("y_part"), sem("y_ready")
            w1h_f, w1l_f = (w[:].rearrange("p a h -> p (a h)") for w in (w1h, w1l))
            w2h_f, w2l_f = (w[:].rearrange("p a h -> p (a h)") for w in (w2h, w2l))

            def experts_of(engine, lo, n):
                return nc.values_load_multi_w_load_instructions(
                    tile_expert[0:1, ds(lo, n)], engines=(engine,), min_val=0, max_val=NX - 1,
                    skip_runtime_bounds_check_because="clamped on chip")[1]

            def exists(s):
                return not isinstance(s, int) or 0 <= s < ST

            def over_tiles5(eng, engine, tick, lo, n):
                def with_experts(s, half, par):
                    if par == 0:
                        a0 = max(0, s + lo) if isinstance(s, int) else s + lo
                        skip = a0 - (s + lo) if isinstance(s, int) else 0
                        count = n + 1 - skip
                        if isinstance(s, int):
                            count = min(count, ST - a0)
                        nos = [None] * skip + list(experts_of(engine, a0, count))
                        held[0] = nos + [None] * (n + 1 - len(nos))
                    tick(s, half, par, *held[0][par:par + n])

                held = [None]
                over_pairs(eng, ST, with_experts)

            with nc.Block() as block:
                @block.gpsimd
                def _(pool):
                    def gather(s, half, par):
                        if exists(s):
                            pool.wait_ge(read_set, s + 1)
                            wait_from_first(pool, turned, s - 1)
                            pool.sem_inc(issue_clear)
                            pool.indirect_dma_start(
                                out=rows[:, par, :], out_offset=None, in_=xn_table[:, :],
                                in_offset=bass.IndirectOffsetOnAxis(ap=read_now[:, par:par + 1], axis=0),
                            ).then_inc(rows_in[par], 16)

                    def add_out(s, half, par):
                        if exists(s):
                            pool.wait_ge(add_set, s + 1)
                            pool.wait_ge(y_ready, s + 1)
                            if not (isinstance(s, int) and s == 0):
                                pool.wait_ge(y_added[1 - par], 16 * (half + par))
                            pool.sem_inc(issue_clear)
                            pool.indirect_dma_start(
                                out=out[:, :], out_offset=bass.IndirectOffsetOnAxis(ap=add_now[:, par:par + 1], axis=0),
                                in_=y[:, par, :], in_offset=None, compute_op=ALU.add,
                            ).then_inc(y_added[par], 16)

                    def tick(s, half, par):
                        gather(s + 2, half + 1, par)
                        add_out(s - 1, half - 1 + par, 1 - par)

                    gather(0, 0, 0)
                    gather(1, 0, 1)
                    over_pairs(pool, ST, tick)
                    add_out(ST - 1, (ST - 1) // 2, (ST - 1) % 2)
                    pool.wait_ge(y_added[0], 16 * (ST // 2))
                    pool.wait_ge(y_added[1], 16 * (ST // 2))

                @block.scalar
                def _(act):
                    def set_read(s, half, par):
                        if exists(s):
                            wait_from_first(act, rows_in[par], 16 * half)
                            nc.scalar.activation(read_now[:, par:par + 1], slot_read[:, ds(s, 1)], ACT.Copy).then_inc(read_set, 1)

                    def set_add(s, half, par):
                        if exists(s):
                            wait_from_first(act, y_added[par], 16 * half)
                            nc.scalar.activation(add_now[:, par:par + 1], slot_add[:, ds(s, 1)], ACT.Copy).then_inc(add_set, 1)

                    def x_hi(s, par):
                        if exists(s):
                            act.wait_ge(xe_made, KC * s + KC)
                            nc.scalar.activation(xe_h[:, par, :, :], xe[:], ACT.Copy).then_inc(xe_hi, 1)

                    def tick(s, half, par, expert):
                        set_read(s + 2, half + 1, par)
                        set_add(s - 1, half - 1 + par, 1 - par)
                        x_hi(s + 1, 1 - par)
                        for k in range(2):
                            act.wait_ge(hidden_made, 2 * s + (k + 1))
                            wait_from_first(act, h_ready, 2 * s - (1 - k))
                            for q in range(HALF):
                                ins = nc.scalar.activation(
                                    h32[:, k, q * P:(q + 1) * P], p_h[k][:, q * P:(q + 1) * P], ACT.Gelu,
                                    bias=params[:, ds(expert * HC + (B10 + k * HALF + q), 1)], scale=1.0 / W_SCALE)
                            ins.then_inc(gelu_done, 1)

                    set_read(0, 0, 0)
                    set_read(1, 0, 1)
                    x_hi(0, 0)
                    over_tiles5(act, ENG.Activation, tick, 0, 1)
                    set_add(ST - 1, (ST - 1) // 2, (ST - 1) % 2)

                @block.tensor
                def _(pe):
                    def turn(s, half, par):
                        if exists(s):
                            pe.wait_ge(rows_in[par], 16 * half + 16)
                            wait_from_first(pe, xe_made, KC * s)
                            for c in range(KC):
                                mm = pe.transpose(p_x[:, c * P:(c + 1) * P], rows[:, par, c * P:(c + 1) * P], ident[:])
                            mm.then_inc(turned, 1)

                    def down(s, half, par, expert):
                        if exists(s):
                            pe.wait_ge(h_ready, 2 * s + 2)
                            wait_from_first(pe, y_part, s - 1)
                            n = 0
                            for hc in range(HC):
                                at = ds(expert * (HC * D) + hc * D, D)
                                for hp, wp in ((h_h, w2h_f), (h_h, w2l_f), (h_l, w2h_f)):
                                    mm = pe.matmul(p_y[par][:, 0:D], hp[:, par, hc * P:(hc + 1) * P], wp[:, at],
                                                   start=(n == 0), stop=(n == 3 * HC - 1))
                                    n += 1
                            mm.then_inc(y_made, 1)

                    def tick(s, half, par, before, expert):
                        turn(s + 1, half + par, 1 - par)
                        pe.wait_ge(xe_ready, s + 1)
                        for k in range(2):
                            wait_from_first(pe, gelu_done, 2 * s + (k - 1))
                            for q in range(HALF):
                                n = 0
                                for c in range(KC):
                                    at = ds(expert * (KC * H) + (c * H + (k * HALF + q) * P), P)
                                    for wp, xp in ((w1h_f, xe_h), (w1h_f, xe_l), (w1l_f, xe_h)):
                                        mm = pe.matmul(p_h[k][:, q * P:(q + 1) * P], wp[:, at], xp[:, par, c, :],
                                                       start=(n == 0), stop=(n == 3 * KC - 1))
                                        n += 1
                            mm.then_inc(hidden_made, 1)
                        down(s - 1, half - 1 + par, 1 - par, before)

                    turn(0, 0, 0)
                    over_tiles5(pe, ENG.PE, tick, -1, 2)
                    last = experts_of(ENG.PE, ST - 1, 1)
                    down(ST - 1, (ST - 1) // 2, (ST - 1) % 2, last[0])

                @block.vector
                def _(dve):
                    V = nc.vector

                    def apply_ln(s, par, expert):
                        if exists(s):
                            dve.wait_ge(turned, s + 1)
                            wait_from_first(dve, xe_ready, s)
                            for c in range(KC):
                                V.tensor_scalar(xe[:, c, :], p_x[:, c * P:(c + 1) * P], params[:, ds(expert * KC + (G0 + c), 1)],
                                                params[:, ds(expert * KC + (B0 + c), 1)], ALU.mult, ALU.add).then_inc(xe_made, 1)

                    def x_lo(s, par):
                        if exists(s):
                            dve.wait_ge(xe_hi, s + 1)
                            V.tensor_tensor(xe_l[:, par, :, :], xe[:], xe_h[:, par, :, :], ALU.subtract).then_inc(xe_ready, 1)

                    def weigh(s, half, par, expert):
                        if exists(s):
                            dve.wait_ge(y_made, s + 1)
                            wait_from_first(dve, y_ready, s)
                            V.scalar_tensor_tensor(y0[:], p_y[par][:, 0:D], 1.0 / W_SCALE,
                                                   b2_rows[:, ds(expert, 1), :].rearrange("p a d -> p (a d)"),
                                                   ALU.mult, ALU.add).then_inc(y_part, 1)
                            dve.wait_ge(y_part, s + 1)
                            wait_from_first(dve, y_added[par], 16 * half)
                            V.tensor_scalar(y[:, par, :], y0[:], slot_w[:, ds(s, 1)], None, ALU.mult).then_inc(y_ready, 1)

                    def tick(s, half, par, before, expert, after):
                        apply_ln(s + 1, 1 - par, after)
                        x_lo(s + 1, 1 - par)
                        for k in range(2):
                            dve.wait_ge(gelu_done, 2 * s + (k + 1))
                            wait_from_first(dve, y_made, s - 1)
                            at = slice(k * HALF * P, (k + 1) * HALF * P)
                            V.tensor_copy(h_h[:, par, at], h32[:, k, :]).then_inc(h_hi, 1)
                            dve.wait_ge(h_hi, 2 * s + (k + 1))
                            V.tensor_tensor(h_l[:, par, at], h32[:, k, :], h_h[:, par, at], ALU.subtract).then_inc(h_ready, 1)
                        weigh(s - 1, half - 1 + par, 1 - par, before)

                    first = experts_of(ENG.DVE, 0, 1)
                    apply_ln(0, 0, first[0])
                    x_lo(0, 0)
                    over_tiles5(dve, ENG.DVE, tick, -1, 3)
                    last = experts_of(ENG.DVE, ST - 1, 1)
                    weigh(ST - 1, (ST - 1) // 2, (ST - 1) % 2, last[0])

def kernel(**inputs):
    import numpy as np
    import concourse.bacc as bacc
    from concourse.bass_utils import run_bass_kernel_spmd as run

    nc = bacc.Bacc("TRN2", target_bir_lowering=False, num_devices=1)
    arrays, aps = {}, {}
    for name, value in inputs.items():
        value = np.ascontiguousarray(value)
        arrays[f"in_{name}"] = value
        aps[name] = nc.dram_tensor(f"in_{name}", value.shape, mybir.dt.from_np(value.dtype), kind="ExternalInput").ap()
    n, d = inputs["x"].shape
    out = nc.dram_tensor("out_0", (n + P, d), F32, kind="ExternalOutput").ap()
    build(nc, aps, out)
    result = run(nc, [arrays], core_ids=[0]).results[0]["out_0"]
    return result[:n]
```

```python
from contextlib import ExitStack

import concourse.bass as bass
from concourse import mybir

P = 128
F32, F16 = mybir.dt.float32, mybir.dt.float16
I32, U32 = mybir.dt.int32, mybir.dt.uint32
ALU = mybir.AluOpType
ACT = mybir.ActivationFunctionType
AX = mybir.AxisListType
ENG = mybir.EngineType
ds = bass.ds

W_SCALE = 64.0
Y_SCALE = 16.0
INV_SCALE = 16384.0
EPS = 1e-5
FAR = 1.0e6


def ceil_div(a, b):
    return -(-a // b)


def wait_from_first(eng, sem, value):
    if not (isinstance(value, int) and value <= 0):
        eng.wait_ge(sem, value)


def build(nc, a, out):
    N, D = a["x"].shape
    E = a["src"].shape[0]
    R = a["L0_gnn_W"].shape[0]
    NX = a["L0_ffn_Wr"].shape[1]
    H = a["L0_ffn_W1"].shape[2]
    NT = ceil_div(N, P)
    LAST = N - (NT - 1) * P
    ET = ceil_div(E, P)
    EC = ceil_div(ET, P)
    KC = D // P
    HC = H // P
    UNROLL = 8
    COUNT_STEPS = ceil_div(ET + NT - 1, NT)
    GROUPS = ceil_div(ET + NT - 1, UNROLL)
    PAIRS = GROUPS * UNROLL
    PW = max(COUNT_STEPS * NT, PAIRS + UNROLL)
    PW = ceil_div(PW, UNROLL) * UNROLL
    DUMMY = NT
    ST = (2 * N) // P + NX
    assert PW <= 512 and ST % 2 == 0 and KC == 2 and NT % 2 == 1 and D == 256

    x, src, dst, typ = a["x"], a["src"], a["dst"], a["edge_type_8"]
    y_table = nc.dram_tensor("y_table", (NT * P * R, 2 * D), F16).ap()
    xn_table = nc.dram_tensor("xn_table", (NT * P, D), F32).ap()

    with ExitStack() as whole:
        def sem(name):
            return whole.enter_context(nc.semaphore(name))

        def sb(name, shape, dt, ctx=whole):
            return ctx.enter_context(nc.sbuf_tensor(name, shape, dt))

        def ps(name, ctx, shape=(P, 512), dt=F32):
            return ctx.enter_context(nc.psum_tensor(name, list(shape), dt))

        ident = sb("ident", [P, P], F32)
        lower = sb("lower", [P, P], F32)
        ones = sb("ones", [P, P], F32)
        iota_row = sb("iota_row", [P, P], F32)
        iota_col = sb("iota_col", [P, NT], F32)
        params = sb("params", [P, 2 * KC * NX + HC * NX], F32)
        br_row = sb("br_row", [P, NX], F32)
        wr = sb("wr", [P, KC, NX], F32)
        acc = sb("acc", [P, NT + 1, D], F32)
        G0, B0, B10 = 0, KC * NX, 2 * KC * NX

        rows_loaded = sem("rows_loaded")
        consts_ready, steps = sem("consts_ready"), sem("dve_steps")
        done_steps = [0]

        def link(dve, ins):
            done_steps[0] += 1
            ins.then_inc(steps, 1)
            dve.wait_ge(steps, done_steps[0])

        def inverse_of_root(dve, result, root, value):
            link(dve, nc.vector.reciprocal(result[:], root[:]))
            link(dve, nc.vector.tensor_tensor(result[:], result[:], value[:], ALU.mult))
            link(dve, nc.vector.tensor_tensor(root[:], root[:], result[:], ALU.add))
            link(dve, nc.vector.tensor_scalar(root[:], root[:], 0.5, None, ALU.mult))
            link(dve, nc.vector.reciprocal(result[:], root[:]))

        dst_rel = sb("dst_rel", [P, PW], F32)
        row_idx = sb("row_idx", [P, PW], U32)
        blk = sb("blk", [P, PW], I32)
        rel_hot = sb("rel_hot", [P, PW, R], F16)
        iota_h = sb("iota_h", [P, P], F16)
        ident_h = sb("ident_h", [P, P], F16)
        inv_parts = sb("inv_parts", [P, NT + 1, 2, R], F16)

        with ExitStack() as to2:
            xs = sb("xs", [P, NT, D], F32, to2)
            wg32 = sb("wg32", [P, KC, R + 1, D], F32, to2)
            wgh = sb("wgh", [P, KC, (R + 1) * D], F16, to2)
            wgl = sb("wgl", [P, KC, (R + 1) * D], F16, to2)
            bias_row = sb("bias_row", [P, D], F32, to2)
            zeros_h = sb("zeros_h", [P, (NT + 1) * R], F16, to2)

            with ExitStack() as s1:
                dst_i = sb("dst_i", [P, EC, P], I32, s1)
                src_i = sb("src_i", [P, EC, P], I32, s1)
                typ_i = sb("typ_i", [P, EC, P], I32, s1)
                dst_f = sb("dst_f", [P, EC, P], F32, s1)
                seg_f = sb("seg_f", [P, EC, P], F32, s1)
                typ_f = sb("typ_f", [P, EC, P], F32, s1)
                off_f = sb("off_f", [P, EC, P], F32, s1)
                pair_hot = sb("pair_hot", [P, EC, PW], F32, s1)
                before_end = sb("before_end", [P, EC, PW], F32, s1)
                iota_pair = sb("iota_pair", [P, PW], F32, s1)
                tile_no = sb("tile_no", [P, EC], F32, s1)
                first_i = sb("first_i", [P, EC], I32, s1)
                last_i = sb("last_i", [P, EC], I32, s1)
                last_s = sb("last_s", [P, EC], I32, s1)
                last_m = sb("last_m", [P, EC], F32, s1)
                first = sb("first", [P, EC], F32, s1)
                last = sb("last", [P, EC], F32, s1)
                span = sb("span", [P, EC], F32, s1)
                totals = sb("totals", [P, EC], F32, s1)
                carry = sb("carry", [P, EC], F32, s1)
                begin = sb("begin", [P, EC], F32, s1)
                end = sb("end", [P, EC], F32, s1)
                is_last = sb("is_last", [P, EC], F32, s1)
                beyond = sb("beyond", [P, EC], F32, s1)
                begin_v = sb("begin_v", [P, EC], F32, s1)
                end_v = sb("end_v", [P, EC], F32, s1)
                offset = sb("offset", [P, EC], F32, s1)
                blk_f = sb("blk_f", [P, PW], F32, s1)
                blk_raw = sb("blk_raw", [P, PW], F32, s1)
                iota_rel = sb("iota_rel", [P, R], F32, s1)
                stats = sb("stats", [P, NT, 6], F32, s1)
                mv = sb("mv", [P, NT, 2], F32, s1)
                var_eps = sb("var_eps", [P, NT], F32, s1)
                std = sb("std", [P, NT], F32, s1)
                rstd = sb("rstd", [P, NT], F32, s1)
                var_ready, root_ready = sem("var_ready"), sem("root_ready")
                raw = sb("raw", [2 * KC * NX + HC * NX, P], F32, s1)
                p_prefix, p_total = ps("p_prefix", s1), ps("p_total", s1)
                p_dst, p_seg = ps("p_dst", s1), ps("p_seg", s1)
                p_typ, p_off = ps("p_typ", s1), ps("p_off", s1)
                p_par = ps("p_par", s1)

                pads_set, edges_loaded = sem("pads_set"), sem("edges_loaded")
                x_loaded, params_loaded = sem("x_loaded"), sem("params_loaded")
                wg_loaded, wgh_ready = sem("wg_loaded"), sem("wgh_ready")
                spans_ready, prefix_ready = sem("spans_ready"), sem("prefix_ready")
                hot_ready, pair_cols_ready = sem("hot_ready"), sem("pair_cols_ready")
                par_turned, ident_base = sem("par_turned"), sem("ident_base")

                FULL_C = E // (P * P)
                FULL_T = E // P - FULL_C * P
                TAIL = E - (E // P) * P

                with nc.Block() as block:
                    @block.sync
                    def _(sp):
                        sp.wait_ge(pads_set, 4)
                        for t, i in ((dst_i, dst), (src_i, src), (typ_i, typ)):
                            sp.dma_start(t[:, 0:FULL_C, :], i[0:FULL_C * P * P].rearrange(
                                "(c p e) -> p c e", c=FULL_C, p=P)).then_inc(edges_loaded, 16)
                            sp.dma_start(t[0:FULL_T, FULL_C, :], i[FULL_C * P * P:(E // P) * P].rearrange(
                                "(p e) -> p e", e=P)).then_inc(edges_loaded, 16)
                            sp.dma_start(t[FULL_T:FULL_T + 1, FULL_C, 0:TAIL], i[(E // P) * P:E].rearrange(
                                "(p e) -> p e", p=1)).then_inc(edges_loaded, 16)
                        sp.dma_start(xs[:, 0:NT - 1, :], x[0:(NT - 1) * P, :].rearrange(
                            "(t p) d -> p t d", p=P)).then_inc(x_loaded, 16)
                        sp.dma_start(xs[0:LAST, NT - 1, :], x[(NT - 1) * P:N, :]).then_inc(x_loaded, 16)

                    @block.scalar
                    def _(act):
                        for c in range(KC):
                            act.dma_start(wg32[:, c, 0:R, :], a["L0_gnn_W"][:, c * P:(c + 1) * P, :].rearrange(
                                "r k o -> k r o")).then_inc(wg_loaded, 16)
                            act.dma_start(wg32[:, c, R, :], a["L0_gnn_W_root"][c * P:(c + 1) * P, :]
                                          ).then_inc(wg_loaded, 16)
                        GB = KC * NX
                        act.dma_start(raw[0:GB, :], a["L0_ffn_ln_g"].rearrange("e (c k) -> (e c) k", k=P)
                                      ).then_inc(params_loaded, 16)
                        act.dma_start(raw[GB:2 * GB, :], a["L0_ffn_ln_b"].rearrange("e (c k) -> (e c) k", k=P)
                                      ).then_inc(params_loaded, 16)
                        act.dma_start(raw[2 * GB:, :], a["L0_ffn_b1"].rearrange("e (c k) -> (e c) k", k=P)
                                      ).then_inc(params_loaded, 16)
                        act.dma_start(bias_row[:], a["L0_gnn_bias"].partition_broadcast(P)).then_inc(rows_loaded, 16)
                        act.dma_start(br_row[:], a["L0_ffn_br"].partition_broadcast(P)).then_inc(rows_loaded, 16)
                        act.dma_start(wr[:], a["L0_ffn_Wr"].rearrange("(c k) e -> k c e", k=P)
                                      ).then_inc(rows_loaded, 16)
                        act.wait_ge(wg_loaded, 16 * 2 * KC)
                        for c in range(KC):
                            nc.scalar.activation(wgh[:, c, :], wg32[:, c, :, :].rearrange("p r o -> p (r o)"),
                                                 ACT.Copy, scale=W_SCALE).then_inc(wgh_ready, 1)
                        act.wait_ge(var_ready, 1)
                        nc.scalar.activation(std[:], var_eps[:], ACT.Sqrt).then_inc(root_ready, 1)

                    @block.gpsimd
                    def _(pool):
                        pool.memset(dst_i[:, EC - 1, :], -1).then_inc(pads_set, 1)
                        pool.memset(src_i[:, EC - 1, :], 0).then_inc(pads_set, 1)
                        pool.memset(typ_i[:, EC - 1, :], 0).then_inc(pads_set, 1)
                        pool.memset(xs[:, NT - 1, :], 0.0).then_inc(pads_set, 1)
                        pool.memset(zeros_h[:], 0.0)
                        pool.memset(ones[:], 1.0).then_inc(ident_base, 1)
                        imp = dict(allow_small_or_imprecise_dtypes=True)
                        pool.iota(iota_row[:], [[1, P]], base=0, channel_multiplier=0, **imp).then_inc(consts_ready, 1)
                        pool.iota(iota_h[:], [[1, P]], base=0, channel_multiplier=0, **imp).then_inc(consts_ready, 1)
                        pool.iota(iota_col[:], [[P, NT]], base=0, channel_multiplier=1, **imp).then_inc(consts_ready, 1)
                        pool.iota(iota_pair[:], [[1, PW]], base=0, channel_multiplier=0, **imp).then_inc(consts_ready, 1)
                        pool.iota(iota_rel[:], [[1, R]], base=0, channel_multiplier=0, **imp).then_inc(consts_ready, 1)
                        pool.iota(tile_no[:], [[P, EC]], base=0, channel_multiplier=1, **imp).then_inc(consts_ready, 1)
                        pool.wait_ge(ident_base, 1)
                        pool.affine_select(out=ident[:], in_=ones[:], compare_op=ALU.is_equal, fill=0.0,
                                           base=0, pattern=[[-1, P]], channel_multiplier=1).then_inc(consts_ready, 1)
                        pool.affine_select(out=ident_h[:], in_=ones[:], compare_op=ALU.is_equal, fill=0.0,
                                           base=0, pattern=[[-1, P]], channel_multiplier=1).then_inc(consts_ready, 1)
                        pool.affine_select(out=lower[:], in_=ones[:], compare_op=ALU.is_gt, fill=0.0,
                                           base=0, pattern=[[1, P]], channel_multiplier=-1).then_inc(consts_ready, 1)

                    @block.vector
                    def _(dve):
                        V = nc.vector
                        V.memset(acc[:, NT, :], 0.0)
                        dve.wait_ge(edges_loaded, 16 * 9)
                        dve.wait_ge(consts_ready, 9)
                        V.tensor_copy(dst_f[:], dst_i[:])
                        V.scalar_tensor_tensor(seg_f[:], src_i[:], float(R), typ_i[:], ALU.mult, ALU.add)
                        V.tensor_copy(typ_f[:], typ_i[:])
                        V.tensor_scalar(first_i[:], dst_i[:, :, 0], 7, None, ALU.arith_shift_right)
                        V.tensor_scalar(is_last[:], tile_no[:], float(ET - 1), FAR, ALU.is_equal, ALU.mult)
                        link(dve, V.tensor_scalar(beyond[:], tile_no[:], float(ET - 1), FAR, ALU.is_gt, ALU.mult))
                        link(dve, V.tensor_reduce(last_m[:], dst_f[:], AX.X, ALU.max))
                        link(dve, V.tensor_copy(last_i[:], last_m[:]))
                        link(dve, V.tensor_scalar(last_s[:], last_i[:], 7, None, ALU.arith_shift_right))
                        V.tensor_copy(first[:], first_i[:])
                        link(dve, V.tensor_copy(last[:], last_s[:]))
                        link(dve, V.scalar_tensor_tensor(span[:], last[:], 1.0, first[:], ALU.add, ALU.subtract))
                        V.engine_nop().then_inc(spans_ready, 1)
                        dve.wait_ge(prefix_ready, 1)
                        V.memset(carry[:, 0:1], 0.0)
                        link(dve, V.tensor_copy(totals[:], p_total[:, 0:EC]))
                        for c in range(1, EC):
                            link(dve, V.tensor_tensor(carry[:, c:c + 1], carry[:, c - 1:c], totals[:, c - 1:c], ALU.add))
                        link(dve, V.tensor_tensor(begin[:], p_prefix[:, 0:EC], carry[:], ALU.add))
                        V.tensor_tensor(begin_v[:], begin[:], beyond[:], ALU.add)
                        V.tensor_tensor(offset[:], first[:], begin[:], ALU.subtract)
                        link(dve, V.tensor_tensor(end[:], begin[:], span[:], ALU.add))
                        link(dve, V.tensor_tensor(end_v[:], end[:], is_last[:], ALU.add))
                        for c in range(EC):
                            V.tensor_scalar(off_f[:, c, :], ones[:], offset[:, c:c + 1], None, ALU.mult)
                            ins = V.tensor_scalar(before_end[:, c, :], iota_pair[:], end_v[:, c:c + 1], None, ALU.is_lt)
                        link(dve, ins)
                        for c in range(EC):
                            V.scalar_tensor_tensor(pair_hot[:, c, :], iota_pair[:], begin_v[:, c:c + 1],
                                                   before_end[:, c, :], ALU.is_ge, ALU.mult).then_inc(hot_ready, 1)
                        dve.wait_ge(x_loaded, 32)
                        for t in range(NT):
                            ins = V.bn_stats(stats[:, t, :], xs[:, t, :])
                        link(dve, ins)
                        for t in range(NT):
                            ins = V.bn_aggr(mv[:, t, :], stats[:, t, :])
                        link(dve, ins)
                        V.tensor_scalar(var_eps[:], mv[:, :, 1], EPS, None, ALU.add).then_inc(var_ready, 1)
                        dve.wait_ge(root_ready, 1)
                        inverse_of_root(dve, rstd, std, var_eps)
                        for t in range(NT):
                            V.tensor_scalar(xs[:, t, :], xs[:, t, :], mv[:, t, 0:1], rstd[:, t:t + 1],
                                            ALU.subtract, ALU.mult)
                        for c in range(KC):
                            dve.wait_ge(wgh_ready, c + 1)
                            V.scalar_tensor_tensor(wgl[:, c, :], wg32[:, c, :, :].rearrange("p r o -> p (r o)"),
                                                   W_SCALE, wgh[:, c, :], ALU.mult, ALU.subtract)
                        dve.wait_ge(par_turned, 1)
                        V.tensor_copy(params[:], p_par[:, 0:params.shape[1]])
                        dve.wait_ge(pair_cols_ready, 4)
                        link(dve, V.tensor_tensor(blk_raw[:], p_off[:, 0:PW], iota_pair[:], ALU.add))
                        link(dve, V.tensor_scalar(blk_f[:], blk_raw[:], float(DUMMY), None, ALU.min))
                        V.tensor_copy(blk[:], blk_f[:])
                        V.scalar_tensor_tensor(dst_rel[:], blk_f[:], -float(P), p_dst[:, 0:PW], ALU.mult, ALU.add)
                        V.tensor_copy(row_idx[:], p_seg[:, 0:PW])
                        V.tensor_tensor(rel_hot[:], p_typ[:, 0:PW].unsqueeze(2).to_broadcast([P, PW, R]),
                                        iota_rel[:].unsqueeze(1).to_broadcast([P, PW, R]), ALU.is_equal)

                    @block.tensor
                    def _(pe):
                        pe.wait_ge(consts_ready, 9)
                        pe.wait_ge(params_loaded, 48)
                        nr = raw.shape[0]
                        pe.transpose(p_par[:, 0:nr], raw[:], ident[0:nr, 0:nr]).then_inc(par_turned, 1)
                        pe.wait_ge(spans_ready, 1)
                        pe.matmul(p_prefix[:, 0:EC], lower[:], span[:], start=True, stop=True)
                        pe.matmul(p_total[:, 0:EC], ones[:], span[:], start=True, stop=True).then_inc(prefix_ready, 1)
                        pe.wait_ge(hot_ready, EC)
                        for t, p in ((off_f, p_off), (dst_f, p_dst), (seg_f, p_seg), (typ_f, p_typ)):
                            for c in range(EC):
                                mm = pe.matmul(p[:, 0:PW], t[:, c, :], pair_hot[:, c, :],
                                               start=(c == 0), stop=(c == EC - 1))
                            mm.then_inc(pair_cols_ready, 1)

            with ExitStack() as s2:
                CS, NY = COUNT_STEPS, R * D // 512
                parts = sb("parts", [P, 2, 2, D], F16, s2)
                xt = sb("xt", [P, 2, 2 * KC * P], F16, s2)
                ystage = sb("ystage", [P, 2, R, 2, D], F16, s2)
                hot = sb("hot", [P, 2, CS, P], F16, s2)
                rel_now = sb("rel_now", [P, 2, CS, R], F16, s2)
                cnt_max = sb("cnt_max", [P, NT + 1, R], F32, s2)
                inv = sb("inv", [P, NT + 1, R], F32, s2)
                p_turn = ps("p_turn", s2, (P, 1024), F16)
                p_y = [ps(f"p_y{q}", s2) for q in range(NY)]
                p_root = ps("p_root", s2)
                p_cnt = ps("p_cnt", s2)
                hi_split, lo_split = sem("hi_split"), sem("lo_split")
                turned, xt_ready = sem("turned"), sem("xt_ready")
                y_made, y_hi, y_lo = sem("y_made"), sem("y_hi"), sem("y_lo")
                y_stored = [sem("y_stored0"), sem("y_stored1")]
                root_made, root_kept = sem("root_made"), sem("root_kept")
                hots_made, rels_set, counts_made = sem("hots_made"), sem("rels_set"), sem("counts_made")
                y_rows = y_table.rearrange("(t p r) d -> t p (r d)", p=P, r=R)

                def tile_of(ap, t):
                    return ap[:, t, :] if isinstance(t, int) else ap[:, ds(t, 1), :].rearrange("p a d -> p (a d)")

                def over_tiles(eng, tick):
                    tick(0, 0, 0)
                    tick(1, 0, 1)
                    with eng.Fori(0, (NT - 5) // 2) as i:
                        tick(2 * i + 2, i + 1, 0)
                        tick(2 * i + 3, i + 1, 1)
                    for t in range(NT - 3, NT):
                        tick(t, t // 2, t % 2)

                def is_tile(t):
                    return not (isinstance(t, int) and t >= NT)

                with nc.Block() as block:
                    @block.tensor
                    def _(pe):
                        def turn(t, par):
                            pe.wait_ge(lo_split, t + 1)
                            wait_from_first(pe, xt_ready, t)
                            for n in range(2 * KC):
                                part, c = divmod(n, KC)
                                mm = pe.transpose(p_turn[:, n * P:(n + 1) * P],
                                                  parts[:, par, part, c * P:(c + 1) * P], ident_h[:])
                            mm.then_inc(turned, 1)

                        def tick(t, half, par):
                            if is_tile(t + 1):
                                turn(t + 1, 1 - par)
                            pe.wait_ge(xt_ready, t + 1)
                            for q in range(NY + 1):
                                lo, hi = q * 512, min((q + 1) * 512, (R + 1) * D)
                                if q < NY:
                                    o = p_y[q][:, :]
                                    wait_from_first(pe, y_lo, NY * t + (q + 1 - NY))
                                else:
                                    o = p_root[:, 0:D]
                                    wait_from_first(pe, root_kept, t)
                                terms = [(xp, wp, c) for c in range(KC) for xp, wp in ((0, wgh), (0, wgl), (1, wgh))]
                                for n, (xp, wp, c) in enumerate(terms):
                                    mm = pe.matmul(o, xt[:, par, (xp * KC + c) * P:(xp * KC + c + 1) * P], wp[:, c, lo:hi],
                                                   start=(n == 0), stop=(n == len(terms) - 1))
                                mm.then_inc(y_made if q < NY else root_made, 1)
                            nos = nc.values_load_multi_w_load_instructions(
                                blk[0:1, ds(t * CS, CS)], engines=(ENG.PE,), min_val=0, max_val=DUMMY,
                                skip_runtime_bounds_check_because="clamped to DUMMY on chip")[1]
                            pe.wait_ge(rels_set, t + 1)
                            pe.wait_ge(hots_made, t + 1)
                            for j in range(CS):
                                mm = pe.matmul(p_cnt[:, ds(nos[j] * R, R)], hot[:, par, j, :], rel_now[:, par, j, :],
                                               start=False, stop=isinstance(t, int) and t * CS + j == NT * CS - 1)
                            mm.then_inc(counts_made, 1)

                        pe.matmul(p_cnt[:, 0:(NT + 1) * R], ident_h[:], zeros_h[:], start=True, stop=False)
                        turn(0, 0)
                        over_tiles(pe, tick)

                    @block.scalar
                    def _(act):
                        def split_hi(t, par):
                            wait_from_first(act, turned, t - 1)
                            nc.scalar.activation(parts[:, par, 0, :], tile_of(xs, t), ACT.Copy).then_inc(hi_split, 1)

                        def keep_turned(t, par):
                            act.wait_ge(turned, t + 1)
                            wait_from_first(act, root_made, t - 1)
                            nc.scalar.activation(xt[:, par, :], p_turn[:, 0:2 * KC * P], ACT.Copy).then_inc(xt_ready, 1)

                        def tick(t, half, par):
                            if is_tile(t + 2):
                                split_hi(t + 2, par)
                            if is_tile(t + 1):
                                keep_turned(t + 1, 1 - par)
                            wait_from_first(act, counts_made, t - 1)
                            nc.scalar.activation(rel_now[:, par, :, :], rel_hot[:, ds(t * CS, CS), :], ACT.Copy
                                                 ).then_inc(rels_set, 1)
                            wait_from_first(act, y_stored[par], 16 * half)
                            for q in range(NY):
                                act.wait_ge(y_made, NY * t + (q + 1))
                                nc.scalar.activation(ystage[:, par, 2 * q:2 * q + 2, 0, :],
                                                     p_y[q][:, :].rearrange("p (r d) -> p r d", d=D),
                                                     ACT.Copy, scale=Y_SCALE / W_SCALE).then_inc(y_hi, 1)

                        split_hi(0, 0)
                        split_hi(1, 1)
                        keep_turned(0, 0)
                        over_tiles(act, tick)

                    @block.sync
                    def _(sp):
                        def tick(t, half, par):
                            sp.wait_ge(y_lo, NY * t + NY)
                            row = y_rows[t, :, :] if isinstance(t, int) else \
                                y_rows[ds(t, 1), :, :].rearrange("a p d -> (a p) d")
                            sp.dma_start(row, ystage[:, par, :, :, :].rearrange("p r i d -> p (r i d)")
                                         ).then_inc(y_stored[par], 16)

                        over_tiles(sp, tick)
                        sp.wait_ge(y_stored[0], 16 * ((NT + 1) // 2))
                        sp.wait_ge(y_stored[1], 16 * (NT // 2))

                    @block.vector
                    def _(dve):
                        V = nc.vector

                        def split_lo(t, par):
                            dve.wait_ge(hi_split, t + 1)
                            wait_from_first(dve, turned, t - 1)
                            V.tensor_tensor(parts[:, par, 1, :], tile_of(xs, t), parts[:, par, 0, :],
                                            ALU.subtract).then_inc(lo_split, 1)

                        def tick(t, half, par):
                            if is_tile(t + 2):
                                split_lo(t + 2, par)
                            wait_from_first(dve, counts_made, t - 1)
                            V.tensor_tensor(hot[:, par, :, :], iota_h[:].unsqueeze(1).to_broadcast([P, CS, P]),
                                            dst_rel[:, ds(t * CS, CS)].unsqueeze(2).to_broadcast([P, CS, P]),
                                            ALU.is_equal).then_inc(hots_made, 1)
                            for q in range(NY):
                                dve.wait_ge(y_hi, NY * t + (q + 1))
                                V.scalar_tensor_tensor(ystage[:, par, 2 * q:2 * q + 2, 1, :],
                                                       p_y[q][:, :].rearrange("p (r d) -> p r d", d=D), Y_SCALE / W_SCALE,
                                                       ystage[:, par, 2 * q:2 * q + 2, 0, :],
                                                       ALU.mult, ALU.subtract).then_inc(y_lo, 1)
                            dve.wait_ge(root_made, t + 1)
                            V.scalar_tensor_tensor(tile_of(acc, t), p_root[:, 0:D], 1.0 / W_SCALE, bias_row[:],
                                                   ALU.mult, ALU.add).then_inc(root_kept, 1)

                        dve.wait_ge(rows_loaded, 48)
                        split_lo(0, 0)
                        split_lo(1, 1)
                        over_tiles(dve, tick)
                        dve.wait_ge(counts_made, NT)
                        link(dve, V.tensor_scalar(cnt_max[:], p_cnt[:, 0:(NT + 1) * R].rearrange("p (t r) -> p t r", r=R),
                                                  1.0, 1.0 / INV_SCALE, ALU.max, ALU.mult))
                        link(dve, V.reciprocal(inv[:], cnt_max[:]))
                        link(dve, V.tensor_copy(inv_parts[:, :, 0, :], inv[:]))
                        V.tensor_tensor(inv_parts[:, :, 1, :], inv[:], inv_parts[:, :, 0, :], ALU.subtract)
        w1h = sb("w1h", [P, KC * NX, H], F16)
        w1l = sb("w1l", [P, KC * NX, H], F16)
        w2 = sb("w2", [P, 2 * NX, HC // 2, 2, D], F16)
        with ExitStack() as s3:
            U = UNROLL
            PIECE = H // 2
            wstage = [sb(f"wstage{k}", [P, PIECE], F32, s3) for k in range(2)]
            gathered = sb("gathered", [P, 2, U, 2, D], F16, s3)
            idx_now = sb("idx_now", [P, 2, U], U32, s3)
            hot = sb("hot3", [P, 2, U, P], F16, s3)
            hot_t = sb("hot_t", [P, 2, U * P], F16, s3)
            hot_w = sb("hot_w", [P, 2, 2, U, P], F16, s3)
            picked = sb("picked", [P, U, 2, R], F32, s3)
            weight = sb("weight", [P, 2, U, 2], F32, s3)
            p_hot = [ps(f"p_hot{k}", s3, (P, 1024), F16) for k in range(2)]
            p_inv = [ps(f"p_inv{k}", s3) for k in range(2)]
            p_sum = [ps(f"p_sum{k}", s3) for k in range(4)]
            idx_set, hots3, hots_turned, hots_kept = sem("idx_set"), sem("hots3"), sem("hots_turned"), sem("hots_kept")
            inv_found, picks_made, weighed = sem("inv_found"), sem("picks_made"), sem("weighed")
            hots_hi, hots_lo = sem("hots_hi"), sem("hots_lo")
            summed, added = sem("summed"), sem("added")
            rows_in = [sem("edge_rows_in0"), sem("edge_rows_in1")]
            w_loaded = [sem("w_piece0_loaded"), sem("w_piece1_loaded")]
            w_hi, w_lo = sem("w_hi"), sem("w_lo")
            gather_clear = sem("gather_clear")
            w1_src = a["L0_ffn_W1"].rearrange("e (c k) h -> (e c) k h", k=P)
            w2_src = a["L0_ffn_W2"].rearrange("e (f q k) d -> (e f) k q d", f=2, k=P)
            UNITS = KC * NX

            def over_groups(eng, tick):
                for g in range(4):
                    tick(g, g // 2, g % 2, None, None)
                for kind in range(2):
                    with eng.Fori(0, UNITS // 2) as i:
                        for par in range(2):
                            tick(2 * i + (4 + kind * UNITS + par), i + (2 + kind * UNITS // 2), par, kind, 2 * i + par)
                with eng.Fori(2 + UNITS, GROUPS // 2) as i:
                    for par in range(2):
                        tick(2 * i + par, i, par, None, None)
                for g in range(GROUPS, GROUPS + 2):
                    tick(g, g // 2, g % 2, None, None)

            def is_group(g):
                return not isinstance(g, int) or 0 <= g < GROUPS

            def blocks(g, engine):
                return nc.values_load_multi_w_load_instructions(
                    blk[0:1, ds(g * U, U)], engines=(engine,), min_val=0, max_val=DUMMY,
                    skip_runtime_bounds_check_because="clamped to DUMMY on chip")[1]

            def w_part(kind, i, piece, part):
                if kind == 0:
                    return (w1h, w1l)[part][:, ds(i, 1), piece * PIECE:(piece + 1) * PIECE].rearrange("p a n -> p (a n)")
                q = HC // 4
                return w2[:, ds(i, 1), piece * q:(piece + 1) * q, part, :].rearrange("p a q d -> p (a q) d")

            def staged(kind, piece):
                return wstage[piece][:] if kind == 0 else wstage[piece][:].rearrange("p (q d) -> p q d", d=D)

            with nc.Block() as block:
                @block.sync
                def _(sp):
                    def unit(kind, i):
                        for piece in range(2):
                            wait_from_first(sp, w_lo, 2 * (i + kind * UNITS) + (piece - 1))
                            if kind == 0:
                                source = w1_src[ds(i, 1), :, piece * PIECE:(piece + 1) * PIECE].rearrange("a k h -> (a k) h")
                            else:
                                q = HC // 4
                                source = w2_src[ds(i, 1), :, piece * q:(piece + 1) * q, :].rearrange("a k q d -> (a k) q d")
                            sp.dma_start(staged(kind, piece), source).then_inc(w_loaded[piece], 16)

                    unit(0, 0)
                    with sp.Fori(1, UNITS) as i:
                        unit(0, i)
                    with sp.Fori(0, UNITS) as i:
                        unit(1, i)

                @block.gpsimd
                def _(pool):
                    def tick(g, half, par, kind, i):
                        if is_group(g):
                            pool.wait_ge(idx_set, g + 1)
                            for j in range(U):
                                if j % 2 == 0:
                                    wait_from_first(pool, summed, g * U + (j + 2 - 2 * U))
                                    pool.sem_inc(gather_clear)
                                pool.indirect_dma_start(
                                    out=gathered[:, par, j, :, :].rearrange("p i d -> p (i d)"), out_offset=None,
                                    in_=y_table[:, :], in_offset=bass.IndirectOffsetOnAxis(ap=idx_now[:, par, j:j + 1], axis=0),
                                ).then_inc(rows_in[par], 16)

                    over_groups(pool, tick)

                @block.scalar
                def _(act):
                    def set_idx(g, half, par):
                        if is_group(g):
                            wait_from_first(act, rows_in[par], 16 * U * half)
                            nc.scalar.activation(idx_now[:, par, :], row_idx[:, ds(g * U, U)], ACT.Copy).then_inc(idx_set, 1)

                    def keep_turned(g, par):
                        if is_group(g):
                            act.wait_ge(hots_turned, g + 1)
                            wait_from_first(act, inv_found, g - 1)
                            nc.scalar.activation(hot_t[:, par, :], p_hot[par][:, :], ACT.Copy).then_inc(hots_kept, 1)

                    def hot_hi(g, par):
                        if is_group(g):
                            act.wait_ge(weighed, g + 1)
                            wait_from_first(act, summed, g * U - U)
                            for j in range(U):
                                ins = nc.scalar.activation(hot_w[:, par, 0, j, :], hot[:, par, j, :], ACT.Copy,
                                                           scale=weight[:, par, j, 0:1])
                            ins.then_inc(hots_hi, 1)

                    def w_hi_part(kind, i, piece):
                        if kind is not None:
                            act.wait_ge(w_loaded[piece], 16 * (i + kind * UNITS) + 16)
                            nc.scalar.activation(w_part(kind, i, piece, 0), staged(kind, piece),
                                                 ACT.Copy, scale=W_SCALE).then_inc(w_hi, 1)

                    def tick(g, half, par, kind, i):
                        if not isinstance(g, int) or g >= 2:
                            set_idx(g, half, par)
                        w_hi_part(kind, i, 0)
                        hot_hi(g - 1, 1 - par)
                        keep_turned(g, par)
                        w_hi_part(kind, i, 1)

                    set_idx(0, 0, 0)
                    set_idx(1, 0, 1)
                    over_groups(act, tick)

                @block.tensor
                def _(pe):
                    def turn(g, par):
                        if is_group(g):
                            pe.wait_ge(hots3, 4 * g + 4)
                            wait_from_first(pe, hots_kept, g - 1)
                            for j in range(U):
                                mm = pe.transpose(p_hot[par][:, j * P:(j + 1) * P], hot[:, par, j, :], ident_h[:])
                            mm.then_inc(hots_turned, 1)

                    def lookup(g, par):
                        if is_group(g):
                            nos = blocks(g, ENG.PE)
                            pe.wait_ge(hots_kept, g + 1)
                            wait_from_first(pe, picks_made, g - 1)
                            for j in range(U):
                                mm = pe.matmul(p_inv[par][:, j * 2 * R:(j + 1) * 2 * R], hot_t[:, par, j * P:(j + 1) * P],
                                               inv_parts[:, ds(nos[j], 1), :, :].rearrange("p a i r -> p (a i r)"),
                                               start=True, stop=True)
                            mm.then_inc(inv_found, 1)

                    def sum_pairs(g, half, par, js):
                        if is_group(g):
                            if js[0] == 0:
                                pe.wait_ge(hots_hi, g + 1)
                                pe.wait_ge(hots_lo, 4 * g + 4)
                                pe.wait_ge(rows_in[par], 16 * U * half + 16 * U)
                            for j in js:
                                wait_from_first(pe, added, g * U + (j - 3))
                                for n, (hp, yp) in enumerate(((0, 0), (0, 1), (1, 0))):
                                    mm = pe.matmul(p_sum[j % 4][:, 0:D], hot_w[:, par, hp, j, :], gathered[:, par, j, yp, :],
                                                   start=(n == 0), stop=(n == 2))
                                mm.then_inc(summed, 1)

                    def tick(g, half, par, kind, i):
                        sum_pairs(g - 2, half - 1, par, range(0, U // 2))
                        turn(g, par)
                        sum_pairs(g - 2, half - 1, par, range(U // 2, U))
                        lookup(g, par)

                    over_groups(pe, tick)

                @block.vector
                def _(dve):
                    V = nc.vector

                    def add(g, j, nos):
                        if is_group(g):
                            dve.wait_ge(summed, g * U + (j + 1))
                            wait_from_first(dve, added, g * U + j)
                            here = acc[:, ds(nos[j], 1), :].rearrange("p a d -> p (a d)")
                            V.scalar_tensor_tensor(here, p_sum[j % 4][:, 0:D], 1.0 / (Y_SCALE * INV_SCALE), here,
                                                   ALU.mult, ALU.add).then_inc(added, 1)

                    QUARTER = U // 4

                    def one_hots(g, par, quarter):
                        if is_group(g):
                            if quarter == 0:
                                wait_from_first(dve, hots_hi, g - 1)
                                wait_from_first(dve, hots_lo, 4 * g - 4)
                            at = slice(quarter * QUARTER, (quarter + 1) * QUARTER)
                            V.tensor_tensor(hot[:, par, at, :], iota_h[:].unsqueeze(1).to_broadcast([P, QUARTER, P]),
                                            dst_rel[:, ds(g * U + at.start, QUARTER)].unsqueeze(2).to_broadcast([P, QUARTER, P]),
                                            ALU.is_equal).then_inc(hots3, 1)

                    def pick(g, par):
                        if is_group(g):
                            dve.wait_ge(inv_found, g + 1)
                            wait_from_first(dve, weighed, g)
                            V.tensor_tensor(picked[:], p_inv[par][:, 0:U * 2 * R].rearrange("p (u i r) -> p u i r", u=U, r=R),
                                            rel_hot[:, ds(g * U, U), :].unsqueeze(2).to_broadcast([P, U, 2, R]),
                                            ALU.mult).then_inc(picks_made, 1)

                    def weigh(g, par):
                        if is_group(g):
                            dve.wait_ge(picks_made, g + 1)
                            V.tensor_reduce(weight[:, par, :, :], picked[:], AX.X, ALU.add).then_inc(weighed, 1)

                    def hot_lo(g, par, quarter):
                        if is_group(g):
                            if quarter == 0:
                                dve.wait_ge(weighed, g + 1)
                                wait_from_first(dve, summed, g * U - U)
                            at = slice(quarter * QUARTER, (quarter + 1) * QUARTER)
                            V.tensor_tensor(hot_w[:, par, 1, at, :], hot[:, par, at, :],
                                            weight[:, par, at, 1].unsqueeze(2).to_broadcast([P, QUARTER, P]),
                                            ALU.mult).then_inc(hots_lo, 1)

                    def w_lo_part(kind, i, piece):
                        if kind is not None:
                            dve.wait_ge(w_hi, 2 * (i + kind * UNITS) + (piece + 1))
                            V.scalar_tensor_tensor(w_part(kind, i, piece, 1), staged(kind, piece), W_SCALE,
                                                   w_part(kind, i, piece, 0), ALU.mult, ALU.subtract).then_inc(w_lo, 1)

                    def tick(g, half, par, kind, i):
                        nos = blocks(g - 2, ENG.DVE) if is_group(g - 2) else None
                        one_hots(g, par, 0)
                        add(g - 2, 0, nos)
                        pick(g - 1, 1 - par)
                        one_hots(g, par, 1)
                        add(g - 2, 1, nos)
                        weigh(g - 1, 1 - par)
                        one_hots(g, par, 2)
                        add(g - 2, 2, nos)
                        one_hots(g, par, 3)
                        for j in range(3, 7):
                            add(g - 2, j, nos)
                            hot_lo(g - 1, 1 - par, j - 3)
                            if j == 4:
                                w_lo_part(kind, i, 0)
                        add(g - 2, 7, nos)
                        w_lo_part(kind, i, 1)

                    over_groups(dve, tick)

        logits = sb("logits", [P, NT, NX], F32)
        slot_read = sb("slot_read", [P, ST], F32)
        slot_add = sb("slot_add", [P, ST], F32)
        slot_w = sb("slot_w", [P, ST], F32)
        tile_expert = sb("tile_expert", [P, ST], I32)
        b2_rows = sb("b2_rows", [P, NX, D], F32)
        b2_loaded = sem("b2_loaded")
        TG = 5
        NG = NT // TG
        assert NT == TG * NG and NG % 2 == 1 and NG >= 3

        def over_pairs(eng, count, tick):
            tail = 2 + count % 2
            tick(0, 0, 0)
            tick(1, 0, 1)
            if count - tail > 2:
                with eng.Fori(0, (count - tail - 2) // 2) as i:
                    tick(2 * i + 2, i + 1, 0)
                    tick(2 * i + 3, i + 1, 1)
            for i in range(max(2, count - tail), count):
                tick(i, i // 2, i % 2)

        def row_group(t, n, ap):
            return ap[ds(t * P, n * P), :].rearrange("(t p) d -> p t d", p=P)

        with ExitStack() as s4:
            xr = sb("xr", [P, 2, TG, D], F32, s4)
            xn = sb("xn", [P, TG, D], F32, s4)
            xr_t = sb("xr_t", [P, 2, D], F32, s4)
            stats = sb("stats4", [P, TG, 6], F32, s4)
            mv = sb("mv4", [P, TG, 2], F32, s4)
            var_eps, std, rstd = (sb(n, [P, TG], F32, s4) for n in ("var_eps4", "std4", "rstd4"))
            p_turn = [ps(f"p_turn4{k}", s4) for k in range(2)]
            p_logit = [ps(f"p_logit{k}", s4) for k in range(2)]
            xr_loaded = [sem("xr_loaded0"), sem("xr_loaded1")]
            x1_ready, x1_stored, xn_ready, xn_stored = sem("x1_ready"), sem("x1_stored"), sem("xn_ready"), sem("xn_stored")
            ln_ready, var_ready, root_ready = sem("ln_ready"), sem("var_ready4"), sem("root_ready4")
            turned, kept, tile_logit, logit_kept = sem("turned4"), sem("kept4"), sem("tile_logit"), sem("logit_kept")

            with nc.Block() as block:
                @block.sync
                def _(sp):
                    def load(g, half, par):
                        if isinstance(g, int) and g == NG - 1:
                            sp.dma_start(xr[:, par, 0:TG - 1, :], row_group(g * TG, TG - 1, x)).then_inc(xr_loaded[par], 16)
                            sp.dma_start(xr[0:LAST, par, TG - 1, :], x[(NT - 1) * P:N, :]).then_inc(xr_loaded[par], 16)
                        else:
                            sp.dma_start(xr[:, par, :, :], row_group(g * TG, TG, x)).then_inc(xr_loaded[par], 16)

                    def tick(g, half, par):
                        sp.wait_ge(x1_ready, g + 1)
                        tiles = acc[:, ds(g * TG, TG), :]
                        sp.dma_start(row_group(g * TG, TG, out), tiles).then_inc(x1_stored, 16)
                        sp.wait_ge(xn_ready, g + 1)
                        sp.dma_start(row_group(g * TG, TG, xn_table), xn[:]).then_inc(xn_stored, 16)
                        if not isinstance(g, int) or g + 2 < NG:
                            sp.wait_ge(turned, TG * g + TG)
                            load(g + 2, half + 1, par)

                    load(0, 0, 0)
                    load(1, 0, 1)
                    sp.dma_start(b2_rows[:], a["L0_ffn_b2"].partition_broadcast(P)).then_inc(b2_loaded, 16)
                    over_pairs(sp, NG, tick)
                    sp.dma_start(out[NT * P:N + P, :], acc[0:N + P - NT * P, NT, :]).then_inc(x1_stored, 16)
                    sp.wait_ge(x1_stored, 16 * (NG + 1))
                    sp.wait_ge(xn_stored, 16 * NG)

                @block.vector
                def _(dve):
                    V = nc.vector

                    def norm(g, second, source, result):
                        for t in range(TG):
                            ins = V.bn_stats(stats[:, t, :], source(t))
                        ins.then_inc(ln_steps, 1)
                        dve.wait_ge(ln_steps, 2 * (2 * g + second) + 1)
                        for t in range(TG):
                            ins = V.bn_aggr(mv[:, t, :], stats[:, t, :])
                        ins.then_inc(ln_steps, 1)
                        dve.wait_ge(ln_steps, 2 * (2 * g + second) + 2)
                        V.tensor_scalar(var_eps[:], mv[:, :, 1], EPS, None, ALU.add).then_inc(var_ready, 1)
                        dve.wait_ge(root_ready, 2 * g + second + 1)
                        base = 5 * (2 * g + second)
                        for n, make in enumerate((
                                lambda: V.reciprocal(rstd[:], std[:]),
                                lambda: V.tensor_tensor(rstd[:], rstd[:], var_eps[:], ALU.mult),
                                lambda: V.tensor_tensor(std[:], std[:], rstd[:], ALU.add),
                                lambda: V.tensor_scalar(std[:], std[:], 0.5, None, ALU.mult),
                                lambda: V.reciprocal(rstd[:], std[:]))):
                            make().then_inc(newton_steps, 1)
                            dve.wait_ge(newton_steps, base + n + 1)
                        for t in range(TG):
                            ins = V.tensor_scalar(result(t), source(t), mv[:, t, 0:1], rstd[:, t:t + 1], ALU.subtract, ALU.mult)
                        return ins

                    def tick(g, half, par):
                        final = isinstance(g, int) and g == NG - 1
                        dve.wait_ge(xr_loaded[par], (16 * half + 32) if final else 16 * half + 16)

                        def node(t):
                            return acc[:, ds(g * TG + t, 1), :].rearrange("p a d -> p (a d)")

                        for t in range(TG):
                            ins = V.scalar_tensor_tensor(node(t), node(t), 0.0, xr[:, par, t, :], ALU.max, ALU.add)
                        ins.then_inc(x1_ready, 1)
                        dve.wait_ge(x1_ready, g + 1)
                        norm(g, 0, node, lambda t: xr[:, par, t, :]).then_inc(ln_ready, 1)
                        dve.wait_ge(ln_ready, g + 1)
                        wait_from_first(dve, xn_stored, 16 * g)
                        norm(g, 1, lambda t: xr[:, par, t, :], lambda t: xn[:, t, :]).then_inc(xn_ready, 1)
                        dve.wait_ge(tile_logit, TG * g + TG)
                        V.tensor_tensor(logits[:, ds(g * TG, TG), :],
                                        p_logit[par][:, 0:TG * NX].rearrange("p (t e) -> p t e", e=NX),
                                        br_row[:].unsqueeze(1).to_broadcast([P, TG, NX]), ALU.add).then_inc(logit_kept, 1)

                    ln_steps, newton_steps = sem("ln_steps"), sem("newton_steps")
                    over_pairs(dve, NG, tick)

                @block.scalar
                def _(act):
                    def tick(g, half, par):
                        act.wait_ge(var_ready, 2 * g + 1)
                        nc.scalar.activation(std[:], var_eps[:], ACT.Sqrt).then_inc(root_ready, 1)
                        act.wait_ge(var_ready, 2 * g + 2)
                        nc.scalar.activation(std[:], var_eps[:], ACT.Sqrt).then_inc(root_ready, 1)
                        for t in range(TG):
                            act.wait_ge(turned, TG * g + (t + 1))
                            if t < 2:
                                wait_from_first(act, tile_logit, TG * g)
                            else:
                                act.wait_ge(tile_logit, TG * g + (t - 1))
                            nc.scalar.activation(xr_t[:, t % 2, :], p_turn[t % 2][:, 0:D], ACT.Copy).then_inc(kept, 1)

                    over_pairs(act, NG, tick)

                @block.tensor
                def _(pe):
                    def tick(g, half, par):
                        def turn(t):
                            if t < 2:
                                wait_from_first(pe, kept, TG * g)
                            else:
                                pe.wait_ge(kept, TG * g + (t - 1))
                            for c in range(KC):
                                mm = pe.transpose(p_turn[t % 2][:, c * P:(c + 1) * P], xr[:, par, t, c * P:(c + 1) * P], ident[:])
                            mm.then_inc(turned, 1)

                        pe.wait_ge(ln_ready, g + 1)
                        wait_from_first(pe, logit_kept, g - 1)
                        turn(0)
                        for t in range(TG):
                            if t + 1 < TG:
                                turn(t + 1)
                            pe.wait_ge(kept, TG * g + (t + 1))
                            for c in range(KC):
                                mm = pe.matmul(p_logit[par][:, t * NX:(t + 1) * NX], xr_t[:, t % 2, c * P:(c + 1) * P],
                                               wr[:, c, :], start=(c == 0), stop=(c == KC - 1))
                            mm.then_inc(tile_logit, 1)

                    pe.wait_ge(rows_loaded, 48)
                    over_pairs(pe, NG, tick)

        with ExitStack() as s4b:
            def arr(name, shape, dt=F32):
                return sb(name, [P] + list(shape), dt, s4b)

            iota_e, iota_slot = arr("iota_e", [NX]), arr("iota_slot", [ST])
            hot_k = [arr(f"hot_k{k}", [NT, NX]) for k in range(2)]
            top = [arr(f"top{k}", [NT]) for k in range(2)]
            lower_than, cand, rest = (arr(n, [NT, NX]) for n in ("lower_than", "cand", "rest"))
            which, gap, ratio, one_more = (arr(n, [NT]) for n in ("which", "gap", "ratio", "one_more"))
            wk = arr("wk", [2, NT])
            valid, far, tok1 = (arr(n, [NT]) for n in ("valid", "far", "tok1"))
            chosen, both, scan0, scan1, place = (arr(n, [NT, NX]) for n in ("chosen", "both", "scan0", "scan1", "place"))
            fill, tiles_f, begin_e, end_e, base_e = (arr(n, [NX]) for n in ("fill", "tiles_f", "begin_e", "end_e", "base_e"))
            fill_i, tiles_i = arr("fill_i", [NX], I32), arr("tiles_i", [NX], I32)
            where = [arr(f"where{k}", [NT]) for k in range(2)]
            where_i, tile_i = arr("where_i", [2, NT], I32), arr("tile_i", [2, NT], I32)
            slot_tile, slot_row = arr("slot_tile", [2, NT]), arr("slot_row", [2, NT])
            ended, expert_f = arr("ended", [ST, NX]), arr("expert_f", [ST])
            row_hot, tile_vals = arr("row_hot", [2, P]), arr("tile_vals", [2, 2, ST])
            trash, unused = arr("trash", [1]), arr("unused", [ST])
            p_rank, p_tot, p_slot = ps("p_rank", s4b), ps("p_tot", s4b), ps("p_slot", s4b)
            iotas_ready, gap_ready, ratio_ready = sem("iotas_ready"), sem("gap_ready"), sem("ratio_ready")
            chosen_ready, ranks_ready = sem("chosen_ready"), sem("ranks_ready")
            vals_ready, vals_used = sem("vals_ready"), sem("vals_used")

            with nc.Block() as block:
                @block.gpsimd
                def _(pool):
                    imp = dict(allow_small_or_imprecise_dtypes=True)
                    pool.iota(iota_e[:], [[1, NX]], base=0, channel_multiplier=0, **imp).then_inc(iotas_ready, 1)
                    pool.iota(iota_slot[:], [[1, ST]], base=0, channel_multiplier=0, **imp).then_inc(iotas_ready, 1)
                    pool.iota(trash[:], [[0, 1]], base=N + 1, channel_multiplier=1, **imp).then_inc(iotas_ready, 1)

                @block.scalar
                def _(act):
                    act.wait_ge(gap_ready, 1)
                    nc.scalar.activation(ratio[:], gap[:], ACT.Exp).then_inc(ratio_ready, 1)

                @block.tensor
                def _(pe):
                    pe.wait_ge(chosen_ready, 1)
                    flat = chosen[:].rearrange("p t e -> p (t e)")
                    pe.matmul(p_rank[:, 0:NT * NX], lower[:], flat, start=True, stop=True)
                    pe.matmul(p_tot[:, 0:NT * NX], ones[:], flat, start=True, stop=True).then_inc(ranks_ready, 1)

                    def add_tile(t):
                        for k in range(2):
                            pe.wait_ge(vals_ready, 2 * t + (k + 1))
                            pe.matmul(p_slot[:, 0:2 * ST], row_hot[:, k, :], tile_vals[:, k, :, :].rearrange("p a s -> p (a s)"),
                                      start=(isinstance(t, int) and t + k == 0),
                                      stop=(isinstance(t, int) and t + k == NT)).then_inc(vals_used, 1)

                    add_tile(0)
                    with pe.Fori(1, NT - 1) as t:
                        add_tile(t)
                    add_tile(NT - 1)

                @block.vector
                def _(dve):
                    V = nc.vector
                    grid = [P, NT, NX]

                    def per_tile(ap):
                        return ap.unsqueeze(2).to_broadcast(grid)

                    def per_expert(ap):
                        return ap.unsqueeze(1).to_broadcast(grid)

                    dve.wait_ge(iotas_ready, 3)
                    for k, source in enumerate((logits, rest)):
                        link(dve, V.tensor_reduce(top[k][:], source[:], AX.X, ALU.max))
                        link(dve, V.tensor_tensor(lower_than[:], source[:], per_tile(top[k][:]), ALU.is_lt))
                        link(dve, V.scalar_tensor_tensor(cand[:], lower_than[:], 99.0, per_expert(iota_e[:]), ALU.mult, ALU.add))
                        link(dve, V.tensor_reduce(which[:], cand[:], AX.X, ALU.min))
                        link(dve, V.tensor_tensor(hot_k[k][:], per_expert(iota_e[:]), per_tile(which[:]), ALU.is_equal))
                        if k == 0:
                            link(dve, V.scalar_tensor_tensor(rest[:], hot_k[0][:], -1.0e30, logits[:], ALU.mult, ALU.add))
                    V.tensor_tensor(gap[:], top[1][:], top[0][:], ALU.subtract).then_inc(gap_ready, 1)
                    V.tensor_scalar(valid[:], iota_col[:], float(N), None, ALU.is_lt)
                    V.tensor_scalar(far[:], iota_col[:], float(N), FAR, ALU.is_ge, ALU.mult)
                    V.tensor_scalar(tok1[:], iota_col[:], 1.0, None, ALU.add)
                    link(dve, V.tensor_tensor(both[:], hot_k[0][:], hot_k[1][:], ALU.add))
                    V.tensor_tensor(chosen[:], both[:], per_tile(valid[:]), ALU.mult).then_inc(chosen_ready, 1)
                    dve.wait_ge(ratio_ready, 1)
                    link(dve, V.tensor_scalar(one_more[:], ratio[:], 1.0, None, ALU.add))
                    link(dve, V.reciprocal(wk[:, 0, :], one_more[:]))
                    link(dve, V.tensor_tensor(wk[:, 1, :], wk[:, 0, :], ratio[:], ALU.mult))
                    dve.wait_ge(ranks_ready, 1)
                    link(dve, V.tensor_copy(scan0[:], p_tot[:, 0:NT * NX].rearrange("p (t e) -> p t e", e=NX)))
                    old, new, shift = scan0, scan1, 1
                    while shift < NT:
                        V.tensor_copy(new[:, 0:shift, :], old[:, 0:shift, :])
                        link(dve, V.tensor_tensor(new[:, shift:, :], old[:, shift:, :], old[:, 0:NT - shift, :], ALU.add))
                        old, new, shift = new, old, 2 * shift
                    link(dve, V.tensor_scalar(fill[:], old[:, NT - 1, :], float(P - 1), None, ALU.add))
                    link(dve, V.tensor_copy(fill_i[:], fill[:]))
                    link(dve, V.tensor_scalar(tiles_i[:], fill_i[:], 7, None, ALU.arith_shift_right))
                    link(dve, V.tensor_copy(tiles_f[:], tiles_i[:]))
                    link(dve, V.memset(begin_e[:, 0:1], 0.0))
                    for e in range(1, NX):
                        link(dve, V.tensor_tensor(begin_e[:, e:e + 1], begin_e[:, e - 1:e], tiles_f[:, e - 1:e], ALU.add))
                    V.tensor_scalar(base_e[:], begin_e[:], float(P), None, ALU.mult)
                    link(dve, V.tensor_tensor(end_e[:], begin_e[:], tiles_f[:], ALU.add))
                    link(dve, V.tensor_tensor(ended[:], end_e[:].unsqueeze(1).to_broadcast([P, ST, NX]),
                                              iota_slot[:].unsqueeze(2).to_broadcast([P, ST, NX]), ALU.is_le))
                    link(dve, V.tensor_reduce(expert_f[:], ended[:], AX.X, ALU.add))
                    link(dve, V.tensor_scalar(expert_f[:], expert_f[:], float(NX - 1), None, ALU.min))
                    V.tensor_copy(tile_expert[:], expert_f[:])
                    link(dve, V.tensor_tensor(new[:], old[:], p_tot[:, 0:NT * NX].rearrange("p (t e) -> p t e", e=NX), ALU.subtract))
                    link(dve, V.tensor_tensor(place[:], new[:], p_rank[:, 0:NT * NX].rearrange("p (t e) -> p t e", e=NX), ALU.add))
                    link(dve, V.tensor_tensor(place[:], place[:], per_expert(base_e[:]), ALU.add))
                    for k in range(2):
                        link(dve, V.tensor_tensor(cand[:], place[:], hot_k[k][:], ALU.mult))
                        link(dve, V.tensor_reduce(where[k][:], cand[:], AX.X, ALU.add))
                        link(dve, V.tensor_copy(where_i[:, k, :], where[k][:]))
                        link(dve, V.tensor_scalar(tile_i[:, k, :], where_i[:, k, :], 7, None, ALU.arith_shift_right))
                        link(dve, V.tensor_copy(slot_tile[:, k, :], tile_i[:, k, :]))
                        link(dve, V.scalar_tensor_tensor(slot_row[:, k, :], slot_tile[:, k, :], -float(P), where[k][:], ALU.mult, ALU.add))
                        link(dve, V.tensor_tensor(slot_tile[:, k, :], slot_tile[:, k, :], far[:], ALU.add))

                    def tile_tick(t):
                        for k in range(2):
                            wait_from_first(dve, vals_used, 2 * t + (k - 1))
                            V.tensor_scalar(row_hot[:, k, :], iota_row[:], slot_row[:, k, ds(t, 1)], None, ALU.is_equal)
                            V.tensor_scalar(tile_vals[:, k, 0, :], iota_slot[:], slot_tile[:, k, ds(t, 1)], tok1[:, ds(t, 1)],
                                            ALU.is_equal, ALU.mult)
                            V.tensor_scalar(tile_vals[:, k, 1, :], iota_slot[:], slot_tile[:, k, ds(t, 1)], wk[:, k, ds(t, 1)],
                                            ALU.is_equal, ALU.mult).then_inc(vals_ready, 1)

                    tile_tick(0)
                    with dve.Fori(1, NT) as t:
                        tile_tick(t)
                    dve.wait_ge(vals_used, 2 * NT)
                    V.tensor_scalar(slot_read[:], p_slot[:, 0:ST], -1.0, 0.0, ALU.add, ALU.max)
                    link(dve, V.tensor_scalar(unused[:], p_slot[:, 0:ST], 0.0, trash[:, 0:1], ALU.is_equal, ALU.mult))
                    V.scalar_tensor_tensor(slot_add[:], p_slot[:, 0:ST], -1.0, unused[:], ALU.add, ALU.add)
                    V.tensor_copy(slot_w[:], p_slot[:, ST:2 * ST])

        with ExitStack() as s5:
            HALF = HC // 2
            rows = sb("rows", [P, 2, D], F32, s5)
            xe = sb("xe", [P, KC, P], F32, s5)
            xe_h = sb("xe_h", [P, 2, KC, P], F16, s5)
            xe_l = sb("xe_l", [P, 2, KC, P], F16, s5)
            h32 = sb("h32", [P, 2, HALF * P], F32, s5)
            h_h = sb("h_h", [P, 2, H], F16, s5)
            h_l = sb("h_l", [P, 2, H], F16, s5)
            y_lo = sb("y_lo", [P, D], F32, s5)
            y0 = sb("y0", [P, D], F32, s5)
            y = sb("y", [P, 2, D], F32, s5)
            read_now = sb("read_now", [P, 2], U32, s5)
            add_now = sb("add_now", [P, 2], U32, s5)
            p_x = ps("p_x", s5)
            p_h = [ps(f"p_h{k}", s5) for k in range(2)]
            p_y = [ps(f"p_y5{k}", s5) for k in range(2)]
            read_set, add_set, issue_clear = sem("read_set"), sem("add_set"), sem("issue_clear")
            rows_in = [sem("slot_rows_in0"), sem("slot_rows_in1")]
            y_added = [sem("y_added0"), sem("y_added1")]
            turned, xe_made, xe_hi, xe_ready = sem("turned5"), sem("xe_made"), sem("xe_hi"), sem("xe_ready")
            hidden_made, gelu_done, h_hi, h_ready = sem("hidden_made"), sem("gelu_done"), sem("h_hi"), sem("h_ready")
            y_lo_made = sem("y_lo_made")
            y_made, y_part, y_ready = sem("y_made5"), sem("y_part"), sem("y_ready")
            w1h_f, w1l_f = (w[:].rearrange("p a h -> p (a h)") for w in (w1h, w1l))
            w2_f = w2[:].rearrange("p a q i d -> p (a q i d)")

            def experts_of(engine, lo, n):
                return nc.values_load_multi_w_load_instructions(
                    tile_expert[0:1, ds(lo, n)], engines=(engine,), min_val=0, max_val=NX - 1,
                    skip_runtime_bounds_check_because="clamped on chip")[1]

            def exists(s):
                return not isinstance(s, int) or 0 <= s < ST

            def over_tiles5(eng, engine, tick, lo, n):
                def with_experts(s, half, par):
                    if par == 0:
                        a0 = max(0, s + lo) if isinstance(s, int) else s + lo
                        skip = a0 - (s + lo) if isinstance(s, int) else 0
                        count = n + 1 - skip
                        if isinstance(s, int):
                            count = min(count, ST - a0)
                        nos = [None] * skip + list(experts_of(engine, a0, count))
                        held[0] = nos + [None] * (n + 1 - len(nos))
                    tick(s, half, par, *held[0][par:par + n])

                held = [None]
                over_pairs(eng, ST, with_experts)

            with nc.Block() as block:
                @block.gpsimd
                def _(pool):
                    def gather(s, half, par):
                        if exists(s):
                            pool.wait_ge(read_set, s + 1)
                            wait_from_first(pool, turned, s - 1)
                            pool.sem_inc(issue_clear)
                            pool.indirect_dma_start(
                                out=rows[:, par, :], out_offset=None, in_=xn_table[:, :],
                                in_offset=bass.IndirectOffsetOnAxis(ap=read_now[:, par:par + 1], axis=0),
                            ).then_inc(rows_in[par], 16)

                    def add_out(s, half, par):
                        if exists(s):
                            pool.wait_ge(add_set, s + 1)
                            pool.wait_ge(y_ready, s + 1)
                            if not (isinstance(s, int) and s == 0):
                                pool.wait_ge(y_added[1 - par], 16 * (half + par))
                            pool.sem_inc(issue_clear)
                            pool.indirect_dma_start(
                                out=out[:, :], out_offset=bass.IndirectOffsetOnAxis(ap=add_now[:, par:par + 1], axis=0),
                                in_=y[:, par, :], in_offset=None, compute_op=ALU.add,
                            ).then_inc(y_added[par], 16)

                    def tick(s, half, par):
                        gather(s + 2, half + 1, par)
                        add_out(s - 2, half - 1, par)

                    gather(0, 0, 0)
                    gather(1, 0, 1)
                    over_pairs(pool, ST, tick)
                    add_out(ST - 2, (ST - 2) // 2, (ST - 2) % 2)
                    add_out(ST - 1, (ST - 1) // 2, (ST - 1) % 2)
                    pool.wait_ge(y_added[0], 16 * (ST // 2))
                    pool.wait_ge(y_added[1], 16 * (ST // 2))

                @block.scalar
                def _(act):
                    def set_read(s, half, par):
                        if exists(s):
                            wait_from_first(act, rows_in[par], 16 * half)
                            nc.scalar.activation(read_now[:, par:par + 1], slot_read[:, ds(s, 1)], ACT.Copy).then_inc(read_set, 1)

                    def set_add(s, half, par):
                        if exists(s):
                            wait_from_first(act, y_added[par], 16 * half)
                            nc.scalar.activation(add_now[:, par:par + 1], slot_add[:, ds(s, 1)], ACT.Copy).then_inc(add_set, 1)

                    def x_hi(s, par):
                        if exists(s):
                            act.wait_ge(xe_made, KC * s + KC)
                            nc.scalar.activation(xe_h[:, par, :, :], xe[:], ACT.Copy).then_inc(xe_hi, 1)

                    def tick(s, half, par, expert):
                        set_read(s + 2, half + 1, par)
                        set_add(s - 2, half - 1, par)
                        for k in range(2):
                            if k == 1:
                                x_hi(s + 1, 1 - par)
                            act.wait_ge(hidden_made, 2 * s + (k + 1))
                            wait_from_first(act, h_ready, 2 * s - (1 - k))
                            for q in range(HALF):
                                ins = nc.scalar.activation(
                                    h32[:, k, q * P:(q + 1) * P], p_h[k][:, q * P:(q + 1) * P], ACT.Gelu,
                                    bias=params[:, ds(expert * HC + (B10 + k * HALF + q), 1)], scale=1.0 / W_SCALE)
                            ins.then_inc(gelu_done, 1)

                    set_read(0, 0, 0)
                    set_read(1, 0, 1)
                    x_hi(0, 0)
                    over_tiles5(act, ENG.Activation, tick, 0, 1)
                    set_add(ST - 2, (ST - 2) // 2, (ST - 2) % 2)
                    set_add(ST - 1, (ST - 1) // 2, (ST - 1) % 2)

                @block.tensor
                def _(pe):
                    def turn(s, half, par):
                        if exists(s):
                            pe.wait_ge(rows_in[par], 16 * half + 16)
                            wait_from_first(pe, xe_made, KC * s)
                            for c in range(KC):
                                mm = pe.transpose(p_x[:, c * P:(c + 1) * P], rows[:, par, c * P:(c + 1) * P], ident[:])
                            mm.then_inc(turned, 1)

                    def up(s, par, expert, hc):
                        k, q = divmod(hc, HALF)
                        if q == 0:
                            wait_from_first(pe, gelu_done, 2 * s + (k - 1))
                        for c in range(KC):
                            at = ds(expert * (KC * H) + (c * H + hc * P), P)
                            for n, (wp, xp) in enumerate(((w1h_f, xe_h), (w1h_f, xe_l), (w1l_f, xe_h))):
                                mm = pe.matmul(p_h[k][:, q * P:(q + 1) * P], wp[:, at], xp[:, par, c, :],
                                               start=(c + n == 0), stop=(c == KC - 1 and n == 2))
                        if q == HALF - 1:
                            mm.then_inc(hidden_made, 1)

                    def down(s, par, expert, hc):
                        if hc % HALF == 0:
                            pe.wait_ge(h_ready, 2 * s + (1 + hc // HALF))
                        if hc == 0:
                            wait_from_first(pe, y_part, s - 1)
                        at = expert * (HC * 2 * D) + hc * 2 * D
                        pe.matmul(p_y[par][:, 0:2 * D], h_h[:, par, hc * P:(hc + 1) * P], w2_f[:, ds(at, 2 * D)],
                                  start=(hc == 0), stop=False)
                        mm = pe.matmul(p_y[par][:, 0:D], h_l[:, par, hc * P:(hc + 1) * P], w2_f[:, ds(at, D)],
                                       start=False, stop=(hc == HC - 1))
                        if hc == HC - 1:
                            mm.then_inc(y_made, 1)

                    def tick(s, half, par, before, expert):
                        pe.wait_ge(xe_ready, s + 1)
                        for hc in range(HC):
                            if hc == HALF:
                                turn(s + 1, half + par, 1 - par)
                            up(s, par, expert, hc)
                            if exists(s - 1):
                                down(s - 1, 1 - par, before, hc)

                    turn(0, 0, 0)
                    over_tiles5(pe, ENG.PE, tick, -1, 2)
                    last = experts_of(ENG.PE, ST - 1, 1)
                    for hc in range(HC):
                        down(ST - 1, (ST - 1) % 2, last[0], hc)

                @block.vector
                def _(dve):
                    V = nc.vector

                    def apply_ln(s, par, expert):
                        if exists(s):
                            dve.wait_ge(turned, s + 1)
                            wait_from_first(dve, xe_ready, s)
                            for c in range(KC):
                                V.tensor_scalar(xe[:, c, :], p_x[:, c * P:(c + 1) * P], params[:, ds(expert * KC + (G0 + c), 1)],
                                                params[:, ds(expert * KC + (B0 + c), 1)], ALU.mult, ALU.add).then_inc(xe_made, 1)

                    def x_lo(s, par):
                        if exists(s):
                            dve.wait_ge(xe_hi, s + 1)
                            V.tensor_tensor(xe_l[:, par, :, :], xe[:], xe_h[:, par, :, :], ALU.subtract).then_inc(xe_ready, 1)

                    def weigh(s, half, par, expert):
                        if exists(s):
                            dve.wait_ge(y_made, s + 1)
                            wait_from_first(dve, y_ready, s)
                            V.scalar_tensor_tensor(y_lo[:], p_y[par][:, D:2 * D], 1.0 / W_SCALE,
                                                   b2_rows[:, ds(expert, 1), :].rearrange("p a d -> p (a d)"),
                                                   ALU.mult, ALU.add).then_inc(y_lo_made, 1)
                            dve.wait_ge(y_lo_made, s + 1)
                            V.scalar_tensor_tensor(y0[:], p_y[par][:, 0:D], 1.0 / W_SCALE, y_lo[:],
                                                   ALU.mult, ALU.add).then_inc(y_part, 1)
                            dve.wait_ge(y_part, s + 1)
                            wait_from_first(dve, y_added[par], 16 * half)
                            V.tensor_scalar(y[:, par, :], y0[:], slot_w[:, ds(s, 1)], None, ALU.mult).then_inc(y_ready, 1)

                    def split_hidden(s, par, k):
                        dve.wait_ge(gelu_done, 2 * s + (k + 1))
                        wait_from_first(dve, y_made, s - 1)
                        at = slice(k * HALF * P, (k + 1) * HALF * P)
                        V.tensor_copy(h_h[:, par, at], h32[:, k, :]).then_inc(h_hi, 1)
                        dve.wait_ge(h_hi, 2 * s + (k + 1))
                        V.tensor_tensor(h_l[:, par, at], h32[:, k, :], h_h[:, par, at], ALU.subtract).then_inc(h_ready, 1)

                    def tick(s, half, par, before, expert, after):
                        apply_ln(s + 1, 1 - par, after)
                        split_hidden(s, par, 0)
                        x_lo(s + 1, 1 - par)
                        weigh(s - 1, half - 1 + par, 1 - par, before)
                        split_hidden(s, par, 1)

                    dve.wait_ge(b2_loaded, 16)
                    first = experts_of(ENG.DVE, 0, 1)
                    apply_ln(0, 0, first[0])
                    x_lo(0, 0)
                    over_tiles5(dve, ENG.DVE, tick, -1, 3)
                    last = experts_of(ENG.DVE, ST - 1, 1)
                    weigh(ST - 1, (ST - 1) // 2, (ST - 1) % 2, last[0])

def kernel(**inputs):
    import numpy as np
    import concourse.bacc as bacc
    from concourse.bass_utils import run_bass_kernel_spmd as run

    nc = bacc.Bacc("TRN2", target_bir_lowering=False, num_devices=1)
    arrays, aps = {}, {}
    for name, value in inputs.items():
        value = np.ascontiguousarray(value)
        arrays[f"in_{name}"] = value
        aps[name] = nc.dram_tensor(f"in_{name}", value.shape, mybir.dt.from_np(value.dtype), kind="ExternalInput").ap()
    n, d = inputs["x"].shape
    out = nc.dram_tensor("out_0", (n + P, d), F32, kind="ExternalOutput").ap()
    build(nc, aps, out)
    result = run(nc, [arrays], core_ids=[0]).results[0]["out_0"]
    return result[:n]
```

```python
from contextlib import ExitStack

import concourse.bass as bass
from concourse import mybir

P = 128
F32, F16 = mybir.dt.float32, mybir.dt.float16
I32, U32 = mybir.dt.int32, mybir.dt.uint32
ALU = mybir.AluOpType
ACT = mybir.ActivationFunctionType
AX = mybir.AxisListType
ENG = mybir.EngineType
ds = bass.ds

W_SCALE = 64.0
Y_SCALE = 16.0
INV_SCALE = 16384.0
EPS = 1e-5
FAR = 1.0e6


def ceil_div(a, b):
    return -(-a // b)


def wait_from_first(eng, sem, value):
    if not (isinstance(value, int) and value <= 0):
        eng.wait_ge(sem, value)


def build(nc, a, out):
    N, D = a["x"].shape
    E = a["src"].shape[0]
    R = a["L0_gnn_W"].shape[0]
    NX = a["L0_ffn_Wr"].shape[1]
    H = a["L0_ffn_W1"].shape[2]
    NT = ceil_div(N, P)
    LAST = N - (NT - 1) * P
    ET = ceil_div(E, P)
    EC = ceil_div(ET, P)
    KC = D // P
    HC = H // P
    UNROLL = 8
    COUNT_STEPS = ceil_div(ET + NT - 1, NT)
    GROUPS = ceil_div(ET + NT - 1, UNROLL)
    PAIRS = GROUPS * UNROLL
    PW = max(COUNT_STEPS * NT, PAIRS + UNROLL)
    PW = ceil_div(PW, UNROLL) * UNROLL
    DUMMY = NT
    ST = (2 * N) // P + NX
    assert PW <= 512 and ST % 2 == 0 and KC == 2 and NT % 2 == 1 and D == 256

    x, src, dst, typ = a["x"], a["src"], a["dst"], a["edge_type_8"]
    y_table = nc.dram_tensor("y_table", (NT * P * R, 2 * D), F16).ap()
    xn_table = nc.dram_tensor("xn_table", (NT * P, D), F32).ap()

    with ExitStack() as whole:
        def sem(name):
            return whole.enter_context(nc.semaphore(name))

        def sb(name, shape, dt, ctx=whole):
            return ctx.enter_context(nc.sbuf_tensor(name, shape, dt))

        def ps(name, ctx, shape=(P, 512), dt=F32):
            return ctx.enter_context(nc.psum_tensor(name, list(shape), dt))

        ident = sb("ident", [P, P], F32)
        lower = sb("lower", [P, P], F32)
        ones = sb("ones", [P, P], F32)
        iota_row = sb("iota_row", [P, P], F32)
        iota_col = sb("iota_col", [P, NT], F32)
        params = sb("params", [P, 2 * KC * NX + HC * NX], F32)
        br_row = sb("br_row", [P, NX], F32)
        wr = sb("wr", [P, KC, NX], F32)
        acc = sb("acc", [P, NT + 1, D], F32)
        G0, B0, B10 = 0, KC * NX, 2 * KC * NX

        rows_loaded = sem("rows_loaded")
        consts_ready, steps = sem("consts_ready"), sem("dve_steps")
        done_steps = [0]

        def link(dve, ins):
            done_steps[0] += 1
            ins.then_inc(steps, 1)
            dve.wait_ge(steps, done_steps[0])

        def inverse_of_root(dve, result, root, value):
            link(dve, nc.vector.reciprocal(result[:], root[:]))
            link(dve, nc.vector.tensor_tensor(result[:], result[:], value[:], ALU.mult))
            link(dve, nc.vector.tensor_tensor(root[:], root[:], result[:], ALU.add))
            link(dve, nc.vector.tensor_scalar(root[:], root[:], 0.5, None, ALU.mult))
            link(dve, nc.vector.reciprocal(result[:], root[:]))

        dst_rel = sb("dst_rel", [P, PW], F32)
        row_idx = sb("row_idx", [P, PW], U32)
        blk = sb("blk", [P, PW], I32)
        rel_hot = sb("rel_hot", [P, PW, R], F16)
        iota_h = sb("iota_h", [P, P], F16)
        ident_h = sb("ident_h", [P, P], F16)
        inv_parts = sb("inv_parts", [P, NT + 1, 2, R], F16)

        with ExitStack() as to2:
            xs = sb("xs", [P, NT, D], F32, to2)
            wg32 = sb("wg32", [P, KC, R + 1, D], F32, to2)
            wgh = sb("wgh", [P, KC, (R + 1) * D], F16, to2)
            wgl = sb("wgl", [P, KC, (R + 1) * D], F16, to2)
            bias_row = sb("bias_row", [P, D], F32, to2)
            zeros_h = sb("zeros_h", [P, (NT + 1) * R], F16, to2)

            with ExitStack() as s1:
                dst_i = sb("dst_i", [P, EC, P], I32, s1)
                src_i = sb("src_i", [P, EC, P], I32, s1)
                typ_i = sb("typ_i", [P, EC, P], I32, s1)
                dst_f = sb("dst_f", [P, EC, P], F32, s1)
                seg_f = sb("seg_f", [P, EC, P], F32, s1)
                typ_f = sb("typ_f", [P, EC, P], F32, s1)
                off_f = sb("off_f", [P, EC, P], F32, s1)
                pair_hot = sb("pair_hot", [P, EC, PW], F32, s1)
                before_end = sb("before_end", [P, EC, PW], F32, s1)
                iota_pair = sb("iota_pair", [P, PW], F32, s1)
                tile_no = sb("tile_no", [P, EC], F32, s1)
                first_i = sb("first_i", [P, EC], I32, s1)
                last_i = sb("last_i", [P, EC], I32, s1)
                last_s = sb("last_s", [P, EC], I32, s1)
                last_m = sb("last_m", [P, EC], F32, s1)
                first = sb("first", [P, EC], F32, s1)
                last = sb("last", [P, EC], F32, s1)
                span = sb("span", [P, EC], F32, s1)
                totals = sb("totals", [P, EC], F32, s1)
                carry = sb("carry", [P, EC], F32, s1)
                begin = sb("begin", [P, EC], F32, s1)
                end = sb("end", [P, EC], F32, s1)
                is_last = sb("is_last", [P, EC], F32, s1)
                beyond = sb("beyond", [P, EC], F32, s1)
                begin_v = sb("begin_v", [P, EC], F32, s1)
                end_v = sb("end_v", [P, EC], F32, s1)
                offset = sb("offset", [P, EC], F32, s1)
                blk_f = sb("blk_f", [P, PW], F32, s1)
                blk_raw = sb("blk_raw", [P, PW], F32, s1)
                iota_rel = sb("iota_rel", [P, R], F32, s1)
                stats = sb("stats", [P, NT, 6], F32, s1)
                mv = sb("mv", [P, NT, 2], F32, s1)
                var_eps = sb("var_eps", [P, NT], F32, s1)
                std = sb("std", [P, NT], F32, s1)
                rstd = sb("rstd", [P, NT], F32, s1)
                shift = sb("shift1", [P, NT], F32, s1)
                var_ready, root_ready, shift_ready = sem("var_ready"), sem("root_ready"), sem("shift_ready1")
                raw = sb("raw", [2 * KC * NX + HC * NX, P], F32, s1)
                p_prefix, p_total = ps("p_prefix", s1), ps("p_total", s1)
                p_dst, p_seg = ps("p_dst", s1), ps("p_seg", s1)
                p_typ, p_off = ps("p_typ", s1), ps("p_off", s1)
                p_par = ps("p_par", s1)

                pads_set, edges_loaded = sem("pads_set"), sem("edges_loaded")
                x_loaded, params_loaded = sem("x_loaded"), sem("params_loaded")
                wg_loaded, wgh_ready = sem("wg_loaded"), sem("wgh_ready")
                spans_ready, prefix_ready = sem("spans_ready"), sem("prefix_ready")
                hot_ready, pair_cols_ready = sem("hot_ready"), sem("pair_cols_ready")
                par_turned, ident_base = sem("par_turned"), sem("ident_base")

                FULL_C = E // (P * P)
                FULL_T = E // P - FULL_C * P
                TAIL = E - (E // P) * P

                with nc.Block() as block:
                    @block.sync
                    def _(sp):
                        sp.wait_ge(pads_set, 4)
                        for t, i in ((dst_i, dst), (src_i, src), (typ_i, typ)):
                            sp.dma_start(t[:, 0:FULL_C, :], i[0:FULL_C * P * P].rearrange(
                                "(c p e) -> p c e", c=FULL_C, p=P)).then_inc(edges_loaded, 16)
                            sp.dma_start(t[0:FULL_T, FULL_C, :], i[FULL_C * P * P:(E // P) * P].rearrange(
                                "(p e) -> p e", e=P)).then_inc(edges_loaded, 16)
                            sp.dma_start(t[FULL_T:FULL_T + 1, FULL_C, 0:TAIL], i[(E // P) * P:E].rearrange(
                                "(p e) -> p e", p=1)).then_inc(edges_loaded, 16)
                        sp.dma_start(xs[:, 0:NT - 1, :], x[0:(NT - 1) * P, :].rearrange(
                            "(t p) d -> p t d", p=P)).then_inc(x_loaded, 16)
                        sp.dma_start(xs[0:LAST, NT - 1, :], x[(NT - 1) * P:N, :]).then_inc(x_loaded, 16)
                        for c in range(KC):
                            sp.dma_start(wg32[:, c, 0:R, :], a["L0_gnn_W"][:, c * P:(c + 1) * P, :].rearrange(
                                "r k o -> k r o")).then_inc(wg_loaded, 16)
                            sp.dma_start(wg32[:, c, R, :], a["L0_gnn_W_root"][c * P:(c + 1) * P, :]
                                         ).then_inc(wg_loaded, 16)

                    @block.scalar
                    def _(act):
                        GB = KC * NX
                        act.dma_start(raw[0:GB, :], a["L0_ffn_ln_g"].rearrange("e (c k) -> (e c) k", k=P)
                                      ).then_inc(params_loaded, 16)
                        act.dma_start(raw[GB:2 * GB, :], a["L0_ffn_ln_b"].rearrange("e (c k) -> (e c) k", k=P)
                                      ).then_inc(params_loaded, 16)
                        act.dma_start(raw[2 * GB:, :], a["L0_ffn_b1"].rearrange("e (c k) -> (e c) k", k=P)
                                      ).then_inc(params_loaded, 16)
                        act.dma_start(bias_row[:], a["L0_gnn_bias"].partition_broadcast(P)).then_inc(rows_loaded, 16)
                        act.dma_start(br_row[:], a["L0_ffn_br"].partition_broadcast(P)).then_inc(rows_loaded, 16)
                        act.dma_start(wr[:], a["L0_ffn_Wr"].rearrange("(c k) e -> k c e", k=P)
                                      ).then_inc(rows_loaded, 16)
                        act.wait_ge(wg_loaded, 16 * 2 * KC)
                        for c in range(KC):
                            nc.scalar.activation(wgh[:, c, :], wg32[:, c, :, :].rearrange("p r o -> p (r o)"),
                                                 ACT.Copy, scale=W_SCALE).then_inc(wgh_ready, 1)
                        act.wait_ge(var_ready, 1)
                        nc.scalar.activation(std[:], var_eps[:], ACT.Sqrt).then_inc(root_ready, 1)
                        act.wait_ge(shift_ready, 1)
                        for t in range(NT):
                            nc.scalar.activation(xs[:, t, :], xs[:, t, :], ACT.Identity, bias=shift[:, t:t + 1],
                                                 scale=rstd[:, t:t + 1])

                    @block.gpsimd
                    def _(pool):
                        pool.memset(dst_i[:, EC - 1, :], -1).then_inc(pads_set, 1)
                        pool.memset(src_i[:, EC - 1, :], 0).then_inc(pads_set, 1)
                        pool.memset(typ_i[:, EC - 1, :], 0).then_inc(pads_set, 1)
                        pool.memset(xs[:, NT - 1, :], 0.0).then_inc(pads_set, 1)
                        pool.memset(zeros_h[:], 0.0)
                        pool.memset(ones[:], 1.0).then_inc(ident_base, 1)
                        imp = dict(allow_small_or_imprecise_dtypes=True)
                        pool.iota(iota_row[:], [[1, P]], base=0, channel_multiplier=0, **imp).then_inc(consts_ready, 1)
                        pool.iota(iota_h[:], [[1, P]], base=0, channel_multiplier=0, **imp).then_inc(consts_ready, 1)
                        pool.iota(iota_col[:], [[P, NT]], base=0, channel_multiplier=1, **imp).then_inc(consts_ready, 1)
                        pool.iota(iota_pair[:], [[1, PW]], base=0, channel_multiplier=0, **imp).then_inc(consts_ready, 1)
                        pool.iota(iota_rel[:], [[1, R]], base=0, channel_multiplier=0, **imp).then_inc(consts_ready, 1)
                        pool.iota(tile_no[:], [[P, EC]], base=0, channel_multiplier=1, **imp).then_inc(consts_ready, 1)
                        pool.wait_ge(ident_base, 1)
                        pool.affine_select(out=ident[:], in_=ones[:], compare_op=ALU.is_equal, fill=0.0,
                                           base=0, pattern=[[-1, P]], channel_multiplier=1).then_inc(consts_ready, 1)
                        pool.affine_select(out=ident_h[:], in_=ones[:], compare_op=ALU.is_equal, fill=0.0,
                                           base=0, pattern=[[-1, P]], channel_multiplier=1).then_inc(consts_ready, 1)
                        pool.affine_select(out=lower[:], in_=ones[:], compare_op=ALU.is_gt, fill=0.0,
                                           base=0, pattern=[[1, P]], channel_multiplier=-1).then_inc(consts_ready, 1)

                    @block.vector
                    def _(dve):
                        V = nc.vector
                        V.memset(acc[:, NT, :], 0.0)
                        dve.wait_ge(edges_loaded, 16 * 9)
                        dve.wait_ge(consts_ready, 9)
                        V.tensor_copy(dst_f[:], dst_i[:])
                        V.scalar_tensor_tensor(seg_f[:], src_i[:], float(R), typ_i[:], ALU.mult, ALU.add)
                        V.tensor_copy(typ_f[:], typ_i[:])
                        V.tensor_scalar(first_i[:], dst_i[:, :, 0], 7, None, ALU.arith_shift_right)
                        V.tensor_scalar(is_last[:], tile_no[:], float(ET - 1), FAR, ALU.is_equal, ALU.mult)
                        link(dve, V.tensor_scalar(beyond[:], tile_no[:], float(ET - 1), FAR, ALU.is_gt, ALU.mult))
                        link(dve, V.tensor_reduce(last_m[:], dst_f[:], AX.X, ALU.max))
                        link(dve, V.tensor_copy(last_i[:], last_m[:]))
                        link(dve, V.tensor_scalar(last_s[:], last_i[:], 7, None, ALU.arith_shift_right))
                        V.tensor_copy(first[:], first_i[:])
                        link(dve, V.tensor_copy(last[:], last_s[:]))
                        link(dve, V.scalar_tensor_tensor(span[:], last[:], 1.0, first[:], ALU.add, ALU.subtract))
                        V.engine_nop().then_inc(spans_ready, 1)
                        dve.wait_ge(prefix_ready, 1)
                        V.memset(carry[:, 0:1], 0.0)
                        link(dve, V.tensor_copy(totals[:], p_total[:, 0:EC]))
                        for c in range(1, EC):
                            link(dve, V.tensor_tensor(carry[:, c:c + 1], carry[:, c - 1:c], totals[:, c - 1:c], ALU.add))
                        link(dve, V.tensor_tensor(begin[:], p_prefix[:, 0:EC], carry[:], ALU.add))
                        V.tensor_tensor(begin_v[:], begin[:], beyond[:], ALU.add)
                        V.tensor_tensor(offset[:], first[:], begin[:], ALU.subtract)
                        link(dve, V.tensor_tensor(end[:], begin[:], span[:], ALU.add))
                        link(dve, V.tensor_tensor(end_v[:], end[:], is_last[:], ALU.add))
                        for c in range(EC):
                            V.tensor_scalar(off_f[:, c, :], ones[:], offset[:, c:c + 1], None, ALU.mult)
                            ins = V.tensor_scalar(before_end[:, c, :], iota_pair[:], end_v[:, c:c + 1], None, ALU.is_lt)
                        link(dve, ins)
                        for c in range(EC):
                            V.scalar_tensor_tensor(pair_hot[:, c, :], iota_pair[:], begin_v[:, c:c + 1],
                                                   before_end[:, c, :], ALU.is_ge, ALU.mult).then_inc(hot_ready, 1)
                        dve.wait_ge(x_loaded, 32)
                        for t in range(NT):
                            ins = V.bn_stats(stats[:, t, :], xs[:, t, :])
                        link(dve, ins)
                        for t in range(NT):
                            ins = V.bn_aggr(mv[:, t, :], stats[:, t, :])
                        link(dve, ins)
                        V.tensor_scalar(var_eps[:], mv[:, :, 1], EPS, None, ALU.add).then_inc(var_ready, 1)
                        dve.wait_ge(root_ready, 1)
                        inverse_of_root(dve, rstd, std, var_eps)
                        V.scalar_tensor_tensor(shift[:], mv[:, :, 0], -1.0, rstd[:], ALU.mult, ALU.mult).then_inc(shift_ready, 1)
                        for c in range(KC):
                            dve.wait_ge(wgh_ready, c + 1)
                            V.scalar_tensor_tensor(wgl[:, c, :], wg32[:, c, :, :].rearrange("p r o -> p (r o)"),
                                                   W_SCALE, wgh[:, c, :], ALU.mult, ALU.subtract)
                        dve.wait_ge(par_turned, 1)
                        V.tensor_copy(params[:], p_par[:, 0:params.shape[1]])
                        dve.wait_ge(pair_cols_ready, 4)
                        link(dve, V.tensor_tensor(blk_raw[:], p_off[:, 0:PW], iota_pair[:], ALU.add))
                        link(dve, V.tensor_scalar(blk_f[:], blk_raw[:], float(DUMMY), None, ALU.min))
                        V.tensor_copy(blk[:], blk_f[:])
                        V.scalar_tensor_tensor(dst_rel[:], blk_f[:], -float(P), p_dst[:, 0:PW], ALU.mult, ALU.add)
                        V.tensor_copy(row_idx[:], p_seg[:, 0:PW])
                        V.tensor_tensor(rel_hot[:], p_typ[:, 0:PW].unsqueeze(2).to_broadcast([P, PW, R]),
                                        iota_rel[:].unsqueeze(1).to_broadcast([P, PW, R]), ALU.is_equal)

                    @block.tensor
                    def _(pe):
                        pe.wait_ge(consts_ready, 9)
                        pe.wait_ge(params_loaded, 48)
                        nr = raw.shape[0]
                        pe.transpose(p_par[:, 0:nr], raw[:], ident[0:nr, 0:nr]).then_inc(par_turned, 1)
                        pe.wait_ge(spans_ready, 1)
                        pe.matmul(p_prefix[:, 0:EC], lower[:], span[:], start=True, stop=True)
                        pe.matmul(p_total[:, 0:EC], ones[:], span[:], start=True, stop=True).then_inc(prefix_ready, 1)
                        pe.wait_ge(hot_ready, EC)
                        for t, p in ((off_f, p_off), (dst_f, p_dst), (seg_f, p_seg), (typ_f, p_typ)):
                            for c in range(EC):
                                mm = pe.matmul(p[:, 0:PW], t[:, c, :], pair_hot[:, c, :],
                                               start=(c == 0), stop=(c == EC - 1))
                            mm.then_inc(pair_cols_ready, 1)

            with ExitStack() as s2:
                CS, NY = COUNT_STEPS, R * D // 512
                parts = sb("parts", [P, 2, 2, D], F16, s2)
                xt = sb("xt", [P, 2, 2 * KC * P], F16, s2)
                ystage = sb("ystage", [P, 2, R, 2, D], F16, s2)
                hot = sb("hot", [P, 2, CS, P], F16, s2)
                rel_now = sb("rel_now", [P, 2, CS, R], F16, s2)
                cnt_max = sb("cnt_max", [P, NT + 1, R], F32, s2)
                inv = sb("inv", [P, NT + 1, R], F32, s2)
                p_turn = ps("p_turn", s2, (P, 1024), F16)
                p_y = [ps(f"p_y{q}", s2) for q in range(NY)]
                p_root = ps("p_root", s2)
                p_cnt = ps("p_cnt", s2)
                hi_split, lo_split = sem("hi_split"), sem("lo_split")
                turned, xt_ready = sem("turned"), sem("xt_ready")
                y_made, y_hi, y_lo = sem("y_made"), sem("y_hi"), sem("y_lo")
                y_stored = [sem("y_stored0"), sem("y_stored1")]
                root_made, root_kept = sem("root_made"), sem("root_kept")
                hots_made, rels_set, counts_made = sem("hots_made"), sem("rels_set"), sem("counts_made")
                y_rows = y_table.rearrange("(t p r) d -> t p (r d)", p=P, r=R)

                def tile_of(ap, t):
                    return ap[:, t, :] if isinstance(t, int) else ap[:, ds(t, 1), :].rearrange("p a d -> p (a d)")

                def over_tiles(eng, tick):
                    tick(0, 0, 0)
                    tick(1, 0, 1)
                    with eng.Fori(0, (NT - 5) // 2) as i:
                        tick(2 * i + 2, i + 1, 0)
                        tick(2 * i + 3, i + 1, 1)
                    for t in range(NT - 3, NT):
                        tick(t, t // 2, t % 2)

                def is_tile(t):
                    return not (isinstance(t, int) and t >= NT)

                with nc.Block() as block:
                    @block.tensor
                    def _(pe):
                        def turn(t, par):
                            pe.wait_ge(lo_split, t + 1)
                            wait_from_first(pe, xt_ready, t)
                            for n in range(2 * KC):
                                part, c = divmod(n, KC)
                                mm = pe.transpose(p_turn[:, n * P:(n + 1) * P],
                                                  parts[:, par, part, c * P:(c + 1) * P], ident_h[:])
                            mm.then_inc(turned, 1)

                        def tick(t, half, par):
                            if is_tile(t + 1):
                                turn(t + 1, 1 - par)
                            pe.wait_ge(xt_ready, t + 1)
                            for q in range(NY + 1):
                                lo, hi = q * 512, min((q + 1) * 512, (R + 1) * D)
                                if q < NY:
                                    o = p_y[q][:, :]
                                    wait_from_first(pe, y_lo, NY * t + (q + 1 - NY))
                                else:
                                    o = p_root[:, 0:D]
                                    wait_from_first(pe, root_kept, t)
                                terms = [(xp, wp, c) for c in range(KC) for xp, wp in ((0, wgh), (0, wgl), (1, wgh))]
                                for n, (xp, wp, c) in enumerate(terms):
                                    mm = pe.matmul(o, xt[:, par, (xp * KC + c) * P:(xp * KC + c + 1) * P], wp[:, c, lo:hi],
                                                   start=(n == 0), stop=(n == len(terms) - 1))
                                mm.then_inc(y_made if q < NY else root_made, 1)
                            nos = nc.values_load_multi_w_load_instructions(
                                blk[0:1, ds(t * CS, CS)], engines=(ENG.PE,), min_val=0, max_val=DUMMY,
                                skip_runtime_bounds_check_because="clamped to DUMMY on chip")[1]
                            pe.wait_ge(rels_set, t + 1)
                            pe.wait_ge(hots_made, t + 1)
                            for j in range(CS):
                                mm = pe.matmul(p_cnt[:, ds(nos[j] * R, R)], hot[:, par, j, :], rel_now[:, par, j, :],
                                               start=False, stop=isinstance(t, int) and t * CS + j == NT * CS - 1)
                            mm.then_inc(counts_made, 1)

                        pe.matmul(p_cnt[:, 0:(NT + 1) * R], ident_h[:], zeros_h[:], start=True, stop=False)
                        turn(0, 0)
                        over_tiles(pe, tick)

                    @block.scalar
                    def _(act):
                        def split_hi(t, par):
                            wait_from_first(act, turned, t - 1)
                            nc.scalar.activation(parts[:, par, 0, :], tile_of(xs, t), ACT.Copy).then_inc(hi_split, 1)

                        def keep_turned(t, par):
                            act.wait_ge(turned, t + 1)
                            wait_from_first(act, root_made, t - 1)
                            nc.scalar.activation(xt[:, par, :], p_turn[:, 0:2 * KC * P], ACT.Copy).then_inc(xt_ready, 1)

                        def tick(t, half, par):
                            if is_tile(t + 2):
                                split_hi(t + 2, par)
                            if is_tile(t + 1):
                                keep_turned(t + 1, 1 - par)
                            wait_from_first(act, counts_made, t - 1)
                            nc.scalar.activation(rel_now[:, par, :, :], rel_hot[:, ds(t * CS, CS), :], ACT.Copy
                                                 ).then_inc(rels_set, 1)
                            wait_from_first(act, y_stored[par], 16 * half)
                            for q in range(NY):
                                act.wait_ge(y_made, NY * t + (q + 1))
                                nc.scalar.activation(ystage[:, par, 2 * q:2 * q + 2, 0, :],
                                                     p_y[q][:, :].rearrange("p (r d) -> p r d", d=D),
                                                     ACT.Copy, scale=Y_SCALE / W_SCALE).then_inc(y_hi, 1)

                        split_hi(0, 0)
                        split_hi(1, 1)
                        keep_turned(0, 0)
                        over_tiles(act, tick)

                    @block.sync
                    def _(sp):
                        def store_last():
                            for part in range(2):
                                sp.wait_ge(y_lo, NY * NT - (1 - part) * NY // 2)
                                n = R // 2
                                at = slice(part * n, (part + 1) * n)
                                sp.dma_start(y_rows[NT - 1, :, part * n * 2 * D:(part + 1) * n * 2 * D],
                                             ystage[:, (NT - 1) % 2, at, :, :].rearrange("p r i d -> p (r i d)")
                                             ).then_inc(y_stored[(NT - 1) % 2], 16)

                        def tick(t, half, par):
                            if isinstance(t, int) and t == NT - 1:
                                return store_last()
                            sp.wait_ge(y_lo, NY * t + NY)
                            row = y_rows[t, :, :] if isinstance(t, int) else \
                                y_rows[ds(t, 1), :, :].rearrange("a p d -> (a p) d")
                            sp.dma_start(row, ystage[:, par, :, :, :].rearrange("p r i d -> p (r i d)")
                                         ).then_inc(y_stored[par], 16)

                        over_tiles(sp, tick)
                        sp.wait_ge(y_stored[0], 16 * ((NT + 1) // 2 + 1))
                        sp.wait_ge(y_stored[1], 16 * (NT // 2))

                    @block.vector
                    def _(dve):
                        V = nc.vector

                        def split_lo(t, par):
                            dve.wait_ge(hi_split, t + 1)
                            wait_from_first(dve, turned, t - 1)
                            V.tensor_tensor(parts[:, par, 1, :], tile_of(xs, t), parts[:, par, 0, :],
                                            ALU.subtract).then_inc(lo_split, 1)

                        def tick(t, half, par):
                            if is_tile(t + 2):
                                split_lo(t + 2, par)
                            wait_from_first(dve, counts_made, t - 1)
                            V.tensor_tensor(hot[:, par, :, :], iota_h[:].unsqueeze(1).to_broadcast([P, CS, P]),
                                            dst_rel[:, ds(t * CS, CS)].unsqueeze(2).to_broadcast([P, CS, P]),
                                            ALU.is_equal).then_inc(hots_made, 1)
                            for q in range(NY):
                                dve.wait_ge(y_hi, NY * t + (q + 1))
                                V.scalar_tensor_tensor(ystage[:, par, 2 * q:2 * q + 2, 1, :],
                                                       p_y[q][:, :].rearrange("p (r d) -> p r d", d=D), Y_SCALE / W_SCALE,
                                                       ystage[:, par, 2 * q:2 * q + 2, 0, :],
                                                       ALU.mult, ALU.subtract).then_inc(y_lo, 1)
                            dve.wait_ge(root_made, t + 1)
                            V.scalar_tensor_tensor(tile_of(acc, t), p_root[:, 0:D], 1.0 / W_SCALE, bias_row[:],
                                                   ALU.mult, ALU.add).then_inc(root_kept, 1)

                        dve.wait_ge(rows_loaded, 48)
                        split_lo(0, 0)
                        split_lo(1, 1)
                        over_tiles(dve, tick)
                        dve.wait_ge(counts_made, NT)
                        link(dve, V.tensor_scalar(cnt_max[:], p_cnt[:, 0:(NT + 1) * R].rearrange("p (t r) -> p t r", r=R),
                                                  1.0, 1.0 / INV_SCALE, ALU.max, ALU.mult))
                        link(dve, V.reciprocal(inv[:], cnt_max[:]))
                        link(dve, V.tensor_copy(inv_parts[:, :, 0, :], inv[:]))
                        V.tensor_tensor(inv_parts[:, :, 1, :], inv[:], inv_parts[:, :, 0, :], ALU.subtract)
        w1h = sb("w1h", [P, KC * NX, H], F16)
        w1l = sb("w1l", [P, KC * NX, H], F16)
        w2 = sb("w2", [P, 2 * NX, HC // 2, 2, D], F16)
        with ExitStack() as s3:
            U = UNROLL
            PIECE = H // 2
            wstage = [sb(f"wstage{k}", [P, PIECE], F32, s3) for k in range(2)]
            gathered = sb("gathered", [P, 2, U, 2, D], F16, s3)
            idx_now = sb("idx_now", [P, 2, U], U32, s3)
            hot = sb("hot3", [P, 2, U, P], F16, s3)
            hot_t = sb("hot_t", [P, 2, U * P], F16, s3)
            hot_w = sb("hot_w", [P, 2, 2, U, P], F16, s3)
            picked = sb("picked", [P, U, 2, R], F32, s3)
            weight = sb("weight", [P, 2, U, 2], F32, s3)
            p_hot = [ps(f"p_hot{k}", s3, (P, 1024), F16) for k in range(2)]
            p_inv = [ps(f"p_inv{k}", s3) for k in range(2)]
            p_sum = [ps(f"p_sum{k}", s3) for k in range(4)]
            idx_set, hots3, hots_turned, hots_kept = sem("idx_set"), sem("hots3"), sem("hots_turned"), sem("hots_kept")
            inv_found, picks_made, weighed = sem("inv_found"), sem("picks_made"), sem("weighed")
            hots_hi, hots_lo = sem("hots_hi"), sem("hots_lo")
            summed, added = sem("summed"), sem("added")
            rows_in = [[sem(f"edge_rows_in{par}{h}") for h in range(2)] for par in range(2)]
            w_loaded = [sem("w_piece0_loaded"), sem("w_piece1_loaded")]
            w_hi, w_lo = sem("w_hi"), sem("w_lo")
            gather_clear = sem("gather_clear")
            w1_src = a["L0_ffn_W1"].rearrange("e (c k) h -> (e c) k h", k=P)
            w2_src = a["L0_ffn_W2"].rearrange("e (f q k) d -> (e f) k q d", f=2, k=P)
            UNITS = KC * NX

            def over_groups(eng, tick):
                for g in range(4):
                    tick(g, g // 2, g % 2, None, None)
                for kind in range(2):
                    with eng.Fori(0, UNITS // 2) as i:
                        for par in range(2):
                            tick(2 * i + (4 + kind * UNITS + par), i + (2 + kind * UNITS // 2), par, kind, 2 * i + par)
                with eng.Fori(2 + UNITS, GROUPS // 2) as i:
                    for par in range(2):
                        tick(2 * i + par, i, par, None, None)
                for g in range(GROUPS, GROUPS + 2):
                    tick(g, g // 2, g % 2, None, None)

            def is_group(g):
                return not isinstance(g, int) or 0 <= g < GROUPS

            def blocks(g, engine):
                return nc.values_load_multi_w_load_instructions(
                    blk[0:1, ds(g * U, U)], engines=(engine,), min_val=0, max_val=DUMMY,
                    skip_runtime_bounds_check_because="clamped to DUMMY on chip")[1]

            def w_part(kind, i, piece, part):
                if kind == 0:
                    return (w1h, w1l)[part][:, ds(i, 1), piece * PIECE:(piece + 1) * PIECE].rearrange("p a n -> p (a n)")
                q = HC // 4
                return w2[:, ds(i, 1), piece * q:(piece + 1) * q, part, :].rearrange("p a q d -> p (a q) d")

            def staged(kind, piece):
                return wstage[piece][:] if kind == 0 else wstage[piece][:].rearrange("p (q d) -> p q d", d=D)

            with nc.Block() as block:
                @block.sync
                def _(sp):
                    def unit(kind, i):
                        for piece in range(2):
                            wait_from_first(sp, w_lo, 2 * (i + kind * UNITS) + (piece - 1))
                            if kind == 0:
                                source = w1_src[ds(i, 1), :, piece * PIECE:(piece + 1) * PIECE].rearrange("a k h -> (a k) h")
                            else:
                                q = HC // 4
                                source = w2_src[ds(i, 1), :, piece * q:(piece + 1) * q, :].rearrange("a k q d -> (a k) q d")
                            sp.dma_start(staged(kind, piece), source).then_inc(w_loaded[piece], 16)

                    unit(0, 0)
                    with sp.Fori(1, UNITS) as i:
                        unit(0, i)
                    with sp.Fori(0, UNITS) as i:
                        unit(1, i)

                @block.gpsimd
                def _(pool):
                    def tick(g, half, par, kind, i):
                        if is_group(g):
                            pool.wait_ge(idx_set, g + 1)
                            for j in range(U):
                                if j % 2 == 0:
                                    wait_from_first(pool, summed, g * U + (j + 2 - 2 * U))
                                    pool.sem_inc(gather_clear)
                                pool.indirect_dma_start(
                                    out=gathered[:, par, j, :, :].rearrange("p i d -> p (i d)"), out_offset=None,
                                    in_=y_table[:, :], in_offset=bass.IndirectOffsetOnAxis(ap=idx_now[:, par, j:j + 1], axis=0),
                                ).then_inc(rows_in[par][j // (U // 2)], 16)

                    over_groups(pool, tick)

                @block.scalar
                def _(act):
                    def set_idx(g, half, par):
                        if is_group(g):
                            for h in range(2):
                                wait_from_first(act, rows_in[par][h], 8 * U * half)
                            nc.scalar.activation(idx_now[:, par, :], row_idx[:, ds(g * U, U)], ACT.Copy).then_inc(idx_set, 1)

                    def keep_turned(g, par):
                        if is_group(g):
                            act.wait_ge(hots_turned, g + 1)
                            wait_from_first(act, inv_found, g - 1)
                            nc.scalar.activation(hot_t[:, par, :], p_hot[par][:, :], ACT.Copy).then_inc(hots_kept, 1)

                    def hot_hi(g, par):
                        if is_group(g):
                            act.wait_ge(weighed, g + 1)
                            wait_from_first(act, summed, g * U - U)
                            for j in range(U):
                                ins = nc.scalar.activation(hot_w[:, par, 0, j, :], hot[:, par, j, :], ACT.Copy,
                                                           scale=weight[:, par, j, 0:1])
                            ins.then_inc(hots_hi, 1)

                    def w_hi_part(kind, i, piece):
                        if kind is not None:
                            act.wait_ge(w_loaded[piece], 16 * (i + kind * UNITS) + 16)
                            nc.scalar.activation(w_part(kind, i, piece, 0), staged(kind, piece),
                                                 ACT.Copy, scale=W_SCALE).then_inc(w_hi, 1)

                    def tick(g, half, par, kind, i):
                        if not isinstance(g, int) or g >= 2:
                            set_idx(g, half, par)
                        w_hi_part(kind, i, 0)
                        hot_hi(g - 1, 1 - par)
                        keep_turned(g, par)
                        w_hi_part(kind, i, 1)

                    set_idx(0, 0, 0)
                    set_idx(1, 0, 1)
                    over_groups(act, tick)

                @block.tensor
                def _(pe):
                    def turn(g, par):
                        if is_group(g):
                            pe.wait_ge(hots3, 4 * g + 4)
                            wait_from_first(pe, hots_kept, g - 1)
                            for j in range(U):
                                mm = pe.transpose(p_hot[par][:, j * P:(j + 1) * P], hot[:, par, j, :], ident_h[:])
                            mm.then_inc(hots_turned, 1)

                    def lookup(g, par):
                        if is_group(g):
                            nos = blocks(g, ENG.PE)
                            pe.wait_ge(hots_kept, g + 1)
                            wait_from_first(pe, picks_made, g - 1)
                            for j in range(U):
                                mm = pe.matmul(p_inv[par][:, j * 2 * R:(j + 1) * 2 * R], hot_t[:, par, j * P:(j + 1) * P],
                                               inv_parts[:, ds(nos[j], 1), :, :].rearrange("p a i r -> p (a i r)"),
                                               start=True, stop=True)
                            mm.then_inc(inv_found, 1)

                    def sum_pairs(g, half, par, js):
                        if is_group(g):
                            if js[0] == 0:
                                pe.wait_ge(hots_hi, g + 1)
                                pe.wait_ge(hots_lo, 4 * g + 4)
                            pe.wait_ge(rows_in[par][js[0] // (U // 2)], 8 * U * half + 8 * U)
                            for j in js:
                                wait_from_first(pe, added, g * U + (j - 3))
                                for n, (hp, yp) in enumerate(((0, 0), (0, 1), (1, 0))):
                                    mm = pe.matmul(p_sum[j % 4][:, 0:D], hot_w[:, par, hp, j, :], gathered[:, par, j, yp, :],
                                                   start=(n == 0), stop=(n == 2))
                                mm.then_inc(summed, 1)

                    def tick(g, half, par, kind, i):
                        sum_pairs(g - 2, half - 1, par, range(0, U // 2))
                        turn(g, par)
                        sum_pairs(g - 2, half - 1, par, range(U // 2, U))
                        lookup(g, par)

                    over_groups(pe, tick)

                @block.vector
                def _(dve):
                    V = nc.vector

                    def add(g, j, nos):
                        if is_group(g):
                            dve.wait_ge(summed, g * U + (j + 1))
                            wait_from_first(dve, added, g * U + j)
                            here = acc[:, ds(nos[j], 1), :].rearrange("p a d -> p (a d)")
                            V.scalar_tensor_tensor(here, p_sum[j % 4][:, 0:D], 1.0 / (Y_SCALE * INV_SCALE), here,
                                                   ALU.mult, ALU.add).then_inc(added, 1)

                    QUARTER = U // 4

                    def one_hots(g, par, quarter):
                        if is_group(g):
                            if quarter == 0:
                                wait_from_first(dve, hots_hi, g - 1)
                                wait_from_first(dve, hots_lo, 4 * g - 4)
                            at = slice(quarter * QUARTER, (quarter + 1) * QUARTER)
                            V.tensor_tensor(hot[:, par, at, :], iota_h[:].unsqueeze(1).to_broadcast([P, QUARTER, P]),
                                            dst_rel[:, ds(g * U + at.start, QUARTER)].unsqueeze(2).to_broadcast([P, QUARTER, P]),
                                            ALU.is_equal).then_inc(hots3, 1)

                    def pick(g, par):
                        if is_group(g):
                            dve.wait_ge(inv_found, g + 1)
                            wait_from_first(dve, weighed, g)
                            V.tensor_tensor(picked[:], p_inv[par][:, 0:U * 2 * R].rearrange("p (u i r) -> p u i r", u=U, r=R),
                                            rel_hot[:, ds(g * U, U), :].unsqueeze(2).to_broadcast([P, U, 2, R]),
                                            ALU.mult).then_inc(picks_made, 1)

                    def weigh(g, par):
                        if is_group(g):
                            dve.wait_ge(picks_made, g + 1)
                            V.tensor_reduce(weight[:, par, :, :], picked[:], AX.X, ALU.add).then_inc(weighed, 1)

                    def hot_lo(g, par, quarter):
                        if is_group(g):
                            if quarter == 0:
                                dve.wait_ge(weighed, g + 1)
                                wait_from_first(dve, summed, g * U - U)
                            at = slice(quarter * QUARTER, (quarter + 1) * QUARTER)
                            V.tensor_tensor(hot_w[:, par, 1, at, :], hot[:, par, at, :],
                                            weight[:, par, at, 1].unsqueeze(2).to_broadcast([P, QUARTER, P]),
                                            ALU.mult).then_inc(hots_lo, 1)

                    def w_lo_part(kind, i, piece):
                        if kind is not None:
                            dve.wait_ge(w_hi, 2 * (i + kind * UNITS) + (piece + 1))
                            V.scalar_tensor_tensor(w_part(kind, i, piece, 1), staged(kind, piece), W_SCALE,
                                                   w_part(kind, i, piece, 0), ALU.mult, ALU.subtract).then_inc(w_lo, 1)

                    def tick(g, half, par, kind, i):
                        nos = blocks(g - 2, ENG.DVE) if is_group(g - 2) else None
                        one_hots(g, par, 0)
                        add(g - 2, 0, nos)
                        pick(g - 1, 1 - par)
                        one_hots(g, par, 1)
                        add(g - 2, 1, nos)
                        weigh(g - 1, 1 - par)
                        one_hots(g, par, 2)
                        add(g - 2, 2, nos)
                        one_hots(g, par, 3)
                        for j in range(3, 7):
                            add(g - 2, j, nos)
                            hot_lo(g - 1, 1 - par, j - 3)
                            if j == 4:
                                w_lo_part(kind, i, 0)
                        add(g - 2, 7, nos)
                        w_lo_part(kind, i, 1)

                    over_groups(dve, tick)

        logits = sb("logits", [P, NT, NX], F32)
        slot_read = sb("slot_read", [P, ST], F32)
        slot_add = sb("slot_add", [P, ST], F32)
        slot_w = sb("slot_w", [P, ST], F32)
        tile_expert = sb("tile_expert", [P, ST], I32)
        b2_rows = sb("b2_rows", [P, NX, D], F32)
        b2_loaded = sem("b2_loaded")
        TG = 5
        NG = NT // TG
        assert NT == TG * NG and NG % 2 == 1 and NG >= 3

        def row_group(t, n, ap):
            return ap[ds(t * P, n * P), :].rearrange("(t p) d -> p t d", p=P)

        with ExitStack() as s4:
            x_in = sb("x_in", [P, 2, TG, D], F32, s4)
            xr = sb("xr", [P, 2, TG, D], F32, s4)
            xn = sb("xn", [P, TG, D], F32, s4)
            xr_t = sb("xr_t", [P, 2, D], F32, s4)
            stats = sb("stats4", [P, TG, 6], F32, s4)
            mv = sb("mv4", [P, TG, 2], F32, s4)
            var_eps, std, rstd = (sb(n, [P, 2, TG], F32, s4) for n in ("var_eps4", "std4", "rstd4"))
            shift = sb("shift", [P, TG], F32, s4)
            total, squares = sb("total", [P, TG], F32, s4), sb("squares", [P, TG], F32, s4)
            mean2, mean2_sq, var2 = (sb(n, [P, TG], F32, s4) for n in ("mean2", "mean2_sq", "var2"))
            squared = dst_rel[:, 0:D]
            p_turn = [ps(f"p_turn4{k}", s4) for k in range(2)]
            p_logit = [ps(f"p_logit{k}", s4) for k in range(2)]
            x_in_loaded = [sem("x_in_loaded0"), sem("x_in_loaded1")]
            x1_ready, x1_stored, xn_ready, xn_stored = sem("x1_ready"), sem("x1_stored"), sem("xn_ready"), sem("xn_stored")
            var_ready, root_ready, shift_ready = sem("var_ready4"), sem("root_ready4"), sem("shift_ready")
            xr_ready, squared_steps = sem("xr_ready"), sem("squared_steps")
            turned, kept, tile_logit, logit_kept = sem("turned4"), sem("kept4"), sem("tile_logit"), sem("logit_kept")

            with nc.Block() as block:
                @block.sync
                def _(sp):
                    def load(g):
                        par = g % 2
                        if g == NG - 1:
                            sp.dma_start(x_in[:, par, 0:TG - 1, :], row_group(g * TG, TG - 1, x)).then_inc(x_in_loaded[par], 16)
                            sp.dma_start(x_in[0:LAST, par, TG - 1, :], x[(NT - 1) * P:N, :]).then_inc(x_in_loaded[par], 16)
                        else:
                            sp.dma_start(x_in[:, par, :, :], row_group(g * TG, TG, x)).then_inc(x_in_loaded[par], 16)

                    load(0)
                    load(1)
                    sp.dma_start(b2_rows[:], a["L0_ffn_b2"].partition_broadcast(P)).then_inc(b2_loaded, 16)
                    for g in range(NG + 1):
                        if g < NG:
                            sp.wait_ge(x1_ready, g + 1)
                            if g + 2 < NG:
                                load(g + 2)
                            sp.dma_start(row_group(g * TG, TG, out), acc[:, g * TG:(g + 1) * TG, :]).then_inc(x1_stored, 16)
                        if g > 0:
                            sp.wait_ge(xn_ready, g)
                            sp.dma_start(row_group((g - 1) * TG, TG, xn_table), xn[:]).then_inc(xn_stored, 16)
                    sp.dma_start(out[NT * P:N + P, :], acc[0:N + P - NT * P, NT, :]).then_inc(x1_stored, 16)

                @block.vector
                def _(dve):
                    V = nc.vector
                    link(dve, V.memset(var_eps[:, 1, :], 1.0))
                    for g in range(NG + 1):
                        if g < NG:
                            nodes = acc[:, g * TG:(g + 1) * TG, :]
                            dve.wait_ge(x_in_loaded[g % 2], 16 * (g // 2) + (32 if g == NG - 1 else 16))
                            V.scalar_tensor_tensor(nodes, nodes, 0.0, x_in[:, g % 2, :, :], ALU.max, ALU.add).then_inc(x1_ready, 1)
                            dve.wait_ge(x1_ready, g + 1)
                            for t in range(TG):
                                ins = V.bn_stats(stats[:, t, :], nodes[:, t, :])
                            link(dve, ins)
                            for t in range(TG):
                                ins = V.bn_aggr(mv[:, t, :], stats[:, t, :])
                            link(dve, ins)
                            last = V.tensor_scalar(var_eps[:, 0, :], mv[:, :, 1], EPS, None, ALU.add)
                        if g > 0:
                            dve.wait_ge(squared_steps, TG * g)
                            wait_from_first(dve, xn_ready, g - 1)
                            link(dve, V.tensor_scalar(mean2[:], total[:], 1.0 / D, None, ALU.mult))
                            link(dve, V.tensor_tensor(mean2_sq[:], mean2[:], mean2[:], ALU.mult))
                            link(dve, V.scalar_tensor_tensor(var2[:], squares[:], 1.0 / D, mean2_sq[:], ALU.mult, ALU.subtract))
                            last = V.tensor_scalar(var_eps[:, 1, :], var2[:], EPS, None, ALU.add)
                        last.then_inc(var_ready, 1)
                        dve.wait_ge(root_ready, g + 1)
                        inverse_of_root(dve, rstd, std, var_eps)
                        if g < NG:
                            V.scalar_tensor_tensor(shift[:], mv[:, :, 0], -1.0, rstd[:, 0, :], ALU.mult, ALU.mult).then_inc(shift_ready, 1)
                        if g > 0:
                            wait_from_first(dve, xn_stored, 16 * (g - 1))
                            for t in range(TG):
                                ins = V.tensor_scalar(xn[:, t, :], xr[:, (g - 1) % 2, t, :], mean2[:, t:t + 1],
                                                      rstd[:, 1, t:t + 1], ALU.subtract, ALU.mult)
                            ins.then_inc(xn_ready, 1)
                            dve.wait_ge(tile_logit, TG * g)
                            V.tensor_tensor(logits[:, (g - 1) * TG:g * TG, :],
                                            p_logit[(g - 1) % 2][:, 0:TG * NX].rearrange("p (t e) -> p t e", e=NX),
                                            br_row[:].unsqueeze(1).to_broadcast([P, TG, NX]), ALU.add).then_inc(logit_kept, 1)

                @block.scalar
                def _(act):
                    EARLY = 2

                    def keep(g, t):
                        act.wait_ge(turned, TG * g + (t + 1))
                        if t < 2:
                            wait_from_first(act, tile_logit, TG * g)
                        else:
                            act.wait_ge(tile_logit, TG * g + (t - 1))
                        nc.scalar.activation(xr_t[:, t % 2, :], p_turn[t % 2][:, 0:D], ACT.Copy).then_inc(kept, 1)

                    for g in range(NG + 1):
                        act.wait_ge(var_ready, g + 1)
                        nc.scalar.activation(std[:], var_eps[:], ACT.Sqrt).then_inc(root_ready, 1)
                        if g > 0:
                            for t in range(EARLY, TG):
                                keep(g - 1, t)
                        if g == NG:
                            break
                        act.wait_ge(shift_ready, g + 1)
                        for t in range(TG):
                            nc.scalar.activation(xr[:, g % 2, t, :], acc[:, g * TG + t, :], ACT.Identity, bias=shift[:, t:t + 1],
                                                 scale=rstd[:, 0, t:t + 1], accum_out=total[:, t:t + 1]).then_inc(xr_ready, 1)
                        for t in range(TG):
                            act.wait_ge(xr_ready, TG * g + (t + 1))
                            wait_from_first(act, squared_steps, TG * g + t)
                            nc.scalar.activation(squared, xr[:, g % 2, t, :], ACT.Square,
                                                 accum_out=squares[:, t:t + 1]).then_inc(squared_steps, 1)
                            if t < EARLY:
                                keep(g, t)

                @block.tensor
                def _(pe):
                    pe.wait_ge(rows_loaded, 48)
                    for g in range(NG):
                        def turn(t):
                            pe.wait_ge(xr_ready, TG * g + (t + 1))
                            if t < 2:
                                wait_from_first(pe, kept, TG * g)
                            else:
                                pe.wait_ge(kept, TG * g + (t - 1))
                            for c in range(KC):
                                mm = pe.transpose(p_turn[t % 2][:, c * P:(c + 1) * P], xr[:, g % 2, t, c * P:(c + 1) * P], ident[:])
                            mm.then_inc(turned, 1)

                        wait_from_first(pe, logit_kept, g - 1)
                        turn(0)
                        for t in range(TG):
                            if t + 1 < TG:
                                turn(t + 1)
                            pe.wait_ge(kept, TG * g + (t + 1))
                            for c in range(KC):
                                mm = pe.matmul(p_logit[g % 2][:, t * NX:(t + 1) * NX], xr_t[:, t % 2, c * P:(c + 1) * P],
                                               wr[:, c, :], start=(c == 0), stop=(c == KC - 1))
                            mm.then_inc(tile_logit, 1)

        with ExitStack() as s4b:
            def arr(name, shape, dt=F32):
                return sb(name, [P] + list(shape), dt, s4b)

            iota_e, iota_slot = arr("iota_e", [NX]), arr("iota_slot", [ST])
            hot_k = arr("hot_k", [2, NT, NX])
            top = [arr(f"top{k}", [NT]) for k in range(2)]
            lower_than, cand, rest = (arr(n, [NT, NX]) for n in ("lower_than", "cand", "rest"))
            which, gap, ratio, one_more = (arr(n, [NT]) for n in ("which", "gap", "ratio", "one_more"))
            wk = arr("wk", [2, NT])
            valid, far, tok1 = (arr(n, [NT]) for n in ("valid", "far", "tok1"))
            chosen, both, scan0, scan1, place = (arr(n, [NT, NX]) for n in ("chosen", "both", "scan0", "scan1", "place"))
            fill, tiles_f, begin_e, end_e, base_e = (arr(n, [NX]) for n in ("fill", "tiles_f", "begin_e", "end_e", "base_e"))
            fill_i, tiles_i = arr("fill_i", [NX], I32), arr("tiles_i", [NX], I32)
            where, place_k = arr("where", [2, NT]), arr("place_k", [2, NT, NX])
            where_i, tile_i = arr("where_i", [2, NT], I32), arr("tile_i", [2, NT], I32)
            slot_tile, slot_row = arr("slot_tile", [2, NT]), arr("slot_row", [2, NT])
            ended, expert_f = arr("ended", [ST, NX]), arr("expert_f", [ST])
            row_hot, tile_hot = arr("row_hot", [2, TG, P]), arr("tile_hot", [2, TG, ST])
            tile_vals = arr("tile_vals", [2, TG, 2, ST])
            trash, unused = arr("trash", [1]), arr("unused", [ST])
            p_rank, p_tot, p_slot = ps("p_rank", s4b), ps("p_tot", s4b), ps("p_slot", s4b)
            iotas_ready, gap_ready, ratio_ready = sem("iotas_ready"), sem("gap_ready"), sem("ratio_ready")
            chosen_ready, ranks_ready = sem("chosen_ready"), sem("ranks_ready")
            tile_hots, token_vals, weight_vals, vals_used = (
                sem(n) for n in ("tile_hots", "token_vals", "weight_vals", "vals_used"))

            with nc.Block() as block:
                @block.sync
                def _(sp):
                    sp.wait_ge(x1_stored, 16 * (NG + 1))
                    sp.wait_ge(xn_stored, 16 * NG)

                @block.gpsimd
                def _(pool):
                    imp = dict(allow_small_or_imprecise_dtypes=True)
                    pool.iota(iota_e[:], [[1, NX]], base=0, channel_multiplier=0, **imp).then_inc(iotas_ready, 1)
                    pool.iota(iota_slot[:], [[1, ST]], base=0, channel_multiplier=0, **imp).then_inc(iotas_ready, 1)
                    pool.iota(trash[:], [[0, 1]], base=N + 1, channel_multiplier=1, **imp).then_inc(iotas_ready, 1)
                    for u in range(2 * NG):
                        k, tiles = u % 2, slice(u // 2 * TG, (u // 2 + 1) * TG)
                        pool.wait_ge(tile_hots, u + 1)
                        pool.tensor_tensor(tile_vals[:, k, :, 0, :], tile_hot[:, k, :, :],
                                           tok1[:, tiles].unsqueeze(2).to_broadcast([P, TG, ST]),
                                           ALU.mult).then_inc(token_vals, 1)

                @block.scalar
                def _(act):
                    act.wait_ge(gap_ready, 1)
                    nc.scalar.activation(ratio[:], gap[:], ACT.Exp).then_inc(ratio_ready, 1)

                @block.tensor
                def _(pe):
                    pe.wait_ge(chosen_ready, 1)
                    flat = chosen[:].rearrange("p t e -> p (t e)")
                    pe.matmul(p_rank[:, 0:NT * NX], lower[:], flat, start=True, stop=True)
                    pe.matmul(p_tot[:, 0:NT * NX], ones[:], flat, start=True, stop=True).then_inc(ranks_ready, 1)

                    for u in range(2 * NG):
                        pe.wait_ge(token_vals, u + 1)
                        pe.wait_ge(weight_vals, u + 1)
                        for t in range(TG):
                            mm = pe.matmul(p_slot[:, 0:2 * ST], row_hot[:, u % 2, t, :],
                                           tile_vals[:, u % 2, t, :, :].rearrange("p a s -> p (a s)"),
                                           start=(u + t == 0), stop=(u == 2 * NG - 1 and t == TG - 1))
                        mm.then_inc(vals_used, 1)

                @block.vector
                def _(dve):
                    V = nc.vector
                    grid = [P, NT, NX]

                    def per_tile(ap):
                        return ap.unsqueeze(2).to_broadcast(grid)

                    def per_expert(ap):
                        return ap.unsqueeze(1).to_broadcast(grid)

                    dve.wait_ge(iotas_ready, 3)
                    for k, source in enumerate((logits, rest)):
                        link(dve, V.tensor_reduce(top[k][:], source[:], AX.X, ALU.max))
                        link(dve, V.tensor_tensor(lower_than[:], source[:], per_tile(top[k][:]), ALU.is_lt))
                        link(dve, V.scalar_tensor_tensor(cand[:], lower_than[:], 99.0, per_expert(iota_e[:]), ALU.mult, ALU.add))
                        link(dve, V.tensor_reduce(which[:], cand[:], AX.X, ALU.min))
                        link(dve, V.tensor_tensor(hot_k[:, k, :, :], per_expert(iota_e[:]), per_tile(which[:]), ALU.is_equal))
                        if k == 0:
                            link(dve, V.scalar_tensor_tensor(rest[:], hot_k[:, 0, :, :], -1.0e30, logits[:], ALU.mult, ALU.add))
                    V.tensor_tensor(gap[:], top[1][:], top[0][:], ALU.subtract).then_inc(gap_ready, 1)
                    V.tensor_scalar(valid[:], iota_col[:], float(N), None, ALU.is_lt)
                    V.tensor_scalar(far[:], iota_col[:], float(N), FAR, ALU.is_ge, ALU.mult)
                    V.tensor_scalar(tok1[:], iota_col[:], 1.0, None, ALU.add)
                    link(dve, V.tensor_tensor(both[:], hot_k[:, 0, :, :], hot_k[:, 1, :, :], ALU.add))
                    V.tensor_tensor(chosen[:], both[:], per_tile(valid[:]), ALU.mult).then_inc(chosen_ready, 1)
                    dve.wait_ge(ratio_ready, 1)
                    link(dve, V.tensor_scalar(one_more[:], ratio[:], 1.0, None, ALU.add))
                    link(dve, V.reciprocal(wk[:, 0, :], one_more[:]))
                    link(dve, V.tensor_tensor(wk[:, 1, :], wk[:, 0, :], ratio[:], ALU.mult))
                    dve.wait_ge(ranks_ready, 1)
                    link(dve, V.tensor_copy(scan0[:], p_tot[:, 0:NT * NX].rearrange("p (t e) -> p t e", e=NX)))
                    old, new, shift = scan0, scan1, 1
                    while shift < NT:
                        V.tensor_copy(new[:, 0:shift, :], old[:, 0:shift, :])
                        link(dve, V.tensor_tensor(new[:, shift:, :], old[:, shift:, :], old[:, 0:NT - shift, :], ALU.add))
                        old, new, shift = new, old, 2 * shift
                    link(dve, V.tensor_scalar(fill[:], old[:, NT - 1, :], float(P - 1), None, ALU.add))
                    link(dve, V.tensor_copy(fill_i[:], fill[:]))
                    link(dve, V.tensor_scalar(tiles_i[:], fill_i[:], 7, None, ALU.arith_shift_right))
                    link(dve, V.tensor_copy(tiles_f[:], tiles_i[:]))
                    link(dve, V.memset(begin_e[:, 0:1], 0.0))
                    for e in range(1, NX):
                        link(dve, V.tensor_tensor(begin_e[:, e:e + 1], begin_e[:, e - 1:e], tiles_f[:, e - 1:e], ALU.add))
                    V.tensor_scalar(base_e[:], begin_e[:], float(P), None, ALU.mult)
                    link(dve, V.tensor_tensor(end_e[:], begin_e[:], tiles_f[:], ALU.add))
                    link(dve, V.tensor_tensor(ended[:], end_e[:].unsqueeze(1).to_broadcast([P, ST, NX]),
                                              iota_slot[:].unsqueeze(2).to_broadcast([P, ST, NX]), ALU.is_le))
                    link(dve, V.tensor_reduce(expert_f[:], ended[:], AX.X, ALU.add))
                    link(dve, V.tensor_scalar(expert_f[:], expert_f[:], float(NX - 1), None, ALU.min))
                    V.tensor_copy(tile_expert[:], expert_f[:])
                    link(dve, V.tensor_tensor(new[:], old[:], p_tot[:, 0:NT * NX].rearrange("p (t e) -> p t e", e=NX), ALU.subtract))
                    link(dve, V.tensor_tensor(place[:], new[:], p_rank[:, 0:NT * NX].rearrange("p (t e) -> p t e", e=NX), ALU.add))
                    link(dve, V.tensor_tensor(place[:], place[:], per_expert(base_e[:]), ALU.add))
                    link(dve, V.tensor_tensor(place_k[:], place[:].unsqueeze(1).to_broadcast([P, 2, NT, NX]), hot_k[:], ALU.mult))
                    link(dve, V.tensor_reduce(where[:], place_k[:], AX.X, ALU.add))
                    link(dve, V.tensor_copy(where_i[:], where[:]))
                    link(dve, V.tensor_scalar(tile_i[:], where_i[:], 7, None, ALU.arith_shift_right))
                    link(dve, V.tensor_copy(slot_tile[:], tile_i[:]))
                    link(dve, V.scalar_tensor_tensor(slot_row[:], slot_tile[:], -float(P), where[:], ALU.mult, ALU.add))
                    link(dve, V.tensor_tensor(slot_tile[:], slot_tile[:], far[:].unsqueeze(1).to_broadcast([P, 2, NT]), ALU.add))
                    dve.wait_ge(xn_stored, 16 * NG)
                    for u in range(2 * NG):
                        k, tiles = u % 2, slice(u // 2 * TG, (u // 2 + 1) * TG)
                        wait_from_first(dve, vals_used, u - 1)
                        V.tensor_tensor(tile_hot[:, k, :, :], iota_slot[:].unsqueeze(1).to_broadcast([P, TG, ST]),
                                        slot_tile[:, k, tiles].unsqueeze(2).to_broadcast([P, TG, ST]),
                                        ALU.is_equal).then_inc(tile_hots, 1)
                        V.tensor_tensor(row_hot[:, k, :, :], iota_row[:].unsqueeze(1).to_broadcast([P, TG, P]),
                                        slot_row[:, k, tiles].unsqueeze(2).to_broadcast([P, TG, P]), ALU.is_equal)
                        dve.wait_ge(tile_hots, u + 1)
                        V.tensor_tensor(tile_vals[:, k, :, 1, :], tile_hot[:, k, :, :],
                                        wk[:, k, tiles].unsqueeze(2).to_broadcast([P, TG, ST]), ALU.mult).then_inc(weight_vals, 1)
                    dve.wait_ge(vals_used, 2 * NG)
                    V.tensor_scalar(slot_read[:], p_slot[:, 0:ST], -1.0, 0.0, ALU.add, ALU.max)
                    link(dve, V.tensor_scalar(unused[:], p_slot[:, 0:ST], 0.0, trash[:, 0:1], ALU.is_equal, ALU.mult))
                    V.scalar_tensor_tensor(slot_add[:], p_slot[:, 0:ST], -1.0, unused[:], ALU.add, ALU.add)
                    V.tensor_copy(slot_w[:], p_slot[:, ST:2 * ST])

        with ExitStack() as s5:
            HALF = HC // 2
            SU = 4
            assert (ST - 4) % SU == 0
            rows = sb("rows", [P, 2, D], F32, s5)
            xe = sb("xe", [P, KC, P], F32, s5)
            xe_h = sb("xe_h", [P, 2, KC, P], F16, s5)
            xe_l = sb("xe_l", [P, 2, KC, P], F16, s5)
            h32 = sb("h32", [P, 2, HALF * P], F32, s5)
            h_h = sb("h_h", [P, 2, H], F16, s5)
            h_l = sb("h_l", [P, 2, H], F16, s5)
            y_lo = sb("y_lo", [P, D], F32, s5)
            y0 = sb("y0", [P, D], F32, s5)
            y = sb("y", [P, 2, D], F32, s5)
            read_now = sb("read_now", [P, 2], U32, s5)
            add_now = sb("add_now", [P, 2], U32, s5)
            p_x = ps("p_x", s5)
            p_h = [ps(f"p_h{k}", s5) for k in range(2)]
            p_y = [ps(f"p_y5{k}", s5) for k in range(2)]
            read_set, add_set, issue_clear = sem("read_set"), sem("add_set"), sem("issue_clear")
            rows_in = [sem("slot_rows_in0"), sem("slot_rows_in1")]
            y_added = [sem("y_added0"), sem("y_added1")]
            turned, xe_made, xe_hi, xe_ready = sem("turned5"), sem("xe_made"), sem("xe_hi"), sem("xe_ready")
            hidden_made, gelu_done, h_hi, h_ready = sem("hidden_made"), sem("gelu_done"), sem("h_hi"), sem("h_ready")
            y_lo_made = sem("y_lo_made")
            y_made, y_part, y_ready = sem("y_made5"), sem("y_part"), sem("y_ready")
            w1h_f, w1l_f = (w[:].rearrange("p a h -> p (a h)") for w in (w1h, w1l))
            w2_f = w2[:].rearrange("p a q i d -> p (a q i d)")

            def experts_of(engine, lo, n):
                return nc.values_load_multi_w_load_instructions(
                    tile_expert[0:1, ds(lo, n)], engines=(engine,), min_val=0, max_val=NX - 1,
                    skip_runtime_bounds_check_because="clamped on chip")[1]

            def exists(s):
                return not isinstance(s, int) or 0 <= s < ST

            def over_slots(eng, tick):
                def unit(s, half, n):
                    for u in range(n):
                        tick(s + u, half + u // 2, u % 2, n, u)

                unit(0, 0, 2)
                with eng.Fori(0, (ST - 4) // SU) as i:
                    unit(SU * i + 2, (SU // 2) * i + 1, SU)
                unit(ST - 2, ST // 2 - 1, 2)

            def over_tiles5(eng, engine, tick, lo, n):
                def with_experts(s, half, par, size, u):
                    if u == 0:
                        first, end = s + lo, s + lo + size + n - 1
                        if isinstance(s, int):
                            held[0] = [None] * max(0, -first) + list(experts_of(
                                engine, max(0, first), min(end, ST) - max(0, first))) + [None] * max(0, end - ST)
                        else:
                            held[0] = experts_of(engine, first, size + n - 1)
                    tick(s, half, par, *held[0][u:u + n])

                held = [None]
                over_slots(eng, with_experts)

            with nc.Block() as block:
                @block.gpsimd
                def _(pool):
                    def gather(s, half, par):
                        if exists(s):
                            pool.wait_ge(read_set, s + 1)
                            wait_from_first(pool, turned, s - 1)
                            pool.sem_inc(issue_clear)
                            pool.indirect_dma_start(
                                out=rows[:, par, :], out_offset=None, in_=xn_table[:, :],
                                in_offset=bass.IndirectOffsetOnAxis(ap=read_now[:, par:par + 1], axis=0),
                            ).then_inc(rows_in[par], 16)

                    def add_out(s, half, par):
                        if exists(s):
                            pool.wait_ge(add_set, s + 1)
                            pool.wait_ge(y_ready, s + 1)
                            if not (isinstance(s, int) and s == 0):
                                pool.wait_ge(y_added[1 - par], 16 * (half + par))
                            pool.sem_inc(issue_clear)
                            pool.indirect_dma_start(
                                out=out[:, :], out_offset=bass.IndirectOffsetOnAxis(ap=add_now[:, par:par + 1], axis=0),
                                in_=y[:, par, :], in_offset=None, compute_op=ALU.add,
                            ).then_inc(y_added[par], 16)

                    def tick(s, half, par, size, u):
                        gather(s + 2, half + 1, par)
                        add_out(s - 2, half - 1, par)

                    gather(0, 0, 0)
                    gather(1, 0, 1)
                    over_slots(pool, tick)
                    add_out(ST - 2, (ST - 2) // 2, (ST - 2) % 2)
                    add_out(ST - 1, (ST - 1) // 2, (ST - 1) % 2)
                    pool.wait_ge(y_added[0], 16 * (ST // 2))
                    pool.wait_ge(y_added[1], 16 * (ST // 2))

                @block.scalar
                def _(act):
                    def set_read(s, half, par):
                        if exists(s):
                            wait_from_first(act, rows_in[par], 16 * half)
                            nc.scalar.activation(read_now[:, par:par + 1], slot_read[:, ds(s, 1)], ACT.Copy).then_inc(read_set, 1)

                    def set_add(s, half, par):
                        if exists(s):
                            wait_from_first(act, y_added[par], 16 * half)
                            nc.scalar.activation(add_now[:, par:par + 1], slot_add[:, ds(s, 1)], ACT.Copy).then_inc(add_set, 1)

                    def x_hi(s, par):
                        if exists(s):
                            act.wait_ge(xe_made, KC * s + KC)
                            nc.scalar.activation(xe_h[:, par, :, :], xe[:], ACT.Copy).then_inc(xe_hi, 1)

                    def tick(s, half, par, expert):
                        set_read(s + 2, half + 1, par)
                        set_add(s - 2, half - 1, par)
                        for k in range(2):
                            act.wait_ge(hidden_made, 2 * s + (k + 1))
                            wait_from_first(act, h_ready, 2 * s - (1 - k))
                            for q in range(HALF):
                                ins = nc.scalar.activation(
                                    h32[:, k, q * P:(q + 1) * P], p_h[k][:, q * P:(q + 1) * P], ACT.Gelu,
                                    bias=params[:, ds(expert * HC + (B10 + k * HALF + q), 1)], scale=1.0 / W_SCALE)
                            ins.then_inc(gelu_done, 1)
                            if k == 0:
                                x_hi(s + 1, 1 - par)
                            act.wait_ge(gelu_done, 2 * s + (k + 1))
                            wait_from_first(act, y_made, s - 1)
                            nc.scalar.activation(h_h[:, par, k * HALF * P:(k + 1) * HALF * P], h32[:, k, :], ACT.Copy).then_inc(h_hi, 1)

                    set_read(0, 0, 0)
                    set_read(1, 0, 1)
                    x_hi(0, 0)
                    over_tiles5(act, ENG.Activation, tick, 0, 1)
                    set_add(ST - 2, (ST - 2) // 2, (ST - 2) % 2)
                    set_add(ST - 1, (ST - 1) // 2, (ST - 1) % 2)

                @block.tensor
                def _(pe):
                    def turn(s, half, par):
                        if exists(s):
                            pe.wait_ge(rows_in[par], 16 * half + 16)
                            for c in range(KC):
                                mm = pe.transpose(p_x[:, c * P:(c + 1) * P], rows[:, par, c * P:(c + 1) * P], ident[:])
                            mm.then_inc(turned, 1)

                    def up(s, par, expert, hc):
                        k, q = divmod(hc, HALF)
                        if hc == 0:
                            wait_from_first(pe, gelu_done, 2 * s - 1)
                        if hc == HALF:
                            wait_from_first(pe, h_ready, 2 * s)
                        for c in range(KC):
                            at = ds(expert * (KC * H) + (c * H + hc * P), P)
                            for n, (wp, xp) in enumerate(((w1h_f, xe_h), (w1h_f, xe_l), (w1l_f, xe_h))):
                                mm = pe.matmul(p_h[k][:, q * P:(q + 1) * P], wp[:, at], xp[:, par, c, :],
                                               start=(c + n == 0), stop=(c == KC - 1 and n == 2))
                        if q == HALF - 1:
                            mm.then_inc(hidden_made, 1)

                    def down(s, par, expert, hc):
                        if hc == 0:
                            pe.wait_ge(h_ready, 2 * s + 1)
                            wait_from_first(pe, y_part, s - 1)
                        at = expert * (HC * 2 * D) + hc * 2 * D
                        pe.matmul(p_y[par][:, 0:2 * D], h_h[:, par, hc * P:(hc + 1) * P], w2_f[:, ds(at, 2 * D)],
                                  start=(hc == 0), stop=False)
                        mm = pe.matmul(p_y[par][:, 0:D], h_l[:, par, hc * P:(hc + 1) * P], w2_f[:, ds(at, D)],
                                       start=False, stop=(hc == HC - 1))
                        if hc == HC - 1:
                            mm.then_inc(y_made, 1)

                    def tick(s, half, par, before, expert):
                        pe.wait_ge(xe_ready, s + 1)
                        for hc in range(HC):
                            if hc == HALF // 2:
                                turn(s + 1, half + par, 1 - par)
                            up(s, par, expert, hc)
                            if exists(s - 1):
                                down(s - 1, 1 - par, before, hc)

                    turn(0, 0, 0)
                    over_tiles5(pe, ENG.PE, tick, -1, 2)
                    last = experts_of(ENG.PE, ST - 1, 1)
                    pe.wait_ge(h_ready, 2 * ST)
                    for hc in range(HC):
                        down(ST - 1, (ST - 1) % 2, last[0], hc)

                @block.vector
                def _(dve):
                    V = nc.vector

                    def apply_ln(s, par, expert):
                        if exists(s):
                            dve.wait_ge(turned, s + 1)
                            wait_from_first(dve, xe_ready, s)
                            for c in range(KC):
                                V.tensor_scalar(xe[:, c, :], p_x[:, c * P:(c + 1) * P], params[:, ds(expert * KC + (G0 + c), 1)],
                                                params[:, ds(expert * KC + (B0 + c), 1)], ALU.mult, ALU.add).then_inc(xe_made, 1)

                    def x_lo(s, par):
                        if exists(s):
                            dve.wait_ge(xe_hi, s + 1)
                            V.tensor_tensor(xe_l[:, par, :, :], xe[:], xe_h[:, par, :, :], ALU.subtract).then_inc(xe_ready, 1)

                    def weigh(s, half, par, expert):
                        if exists(s):
                            dve.wait_ge(y_made, s + 1)
                            wait_from_first(dve, y_ready, s)
                            V.scalar_tensor_tensor(y_lo[:], p_y[par][:, D:2 * D], 1.0 / W_SCALE,
                                                   b2_rows[:, ds(expert, 1), :].rearrange("p a d -> p (a d)"),
                                                   ALU.mult, ALU.add).then_inc(y_lo_made, 1)
                            dve.wait_ge(y_lo_made, s + 1)
                            V.scalar_tensor_tensor(y0[:], p_y[par][:, 0:D], 1.0 / W_SCALE, y_lo[:],
                                                   ALU.mult, ALU.add).then_inc(y_part, 1)
                            dve.wait_ge(y_part, s + 1)
                            wait_from_first(dve, y_added[par], 16 * half)
                            V.tensor_scalar(y[:, par, :], y0[:], slot_w[:, ds(s, 1)], None, ALU.mult).then_inc(y_ready, 1)

                    def hidden_lo(s, par, k):
                        dve.wait_ge(h_hi, 2 * s + (k + 1))
                        at = slice(k * HALF * P, (k + 1) * HALF * P)
                        V.tensor_tensor(h_l[:, par, at], h32[:, k, :], h_h[:, par, at], ALU.subtract).then_inc(h_ready, 1)

                    def tick(s, half, par, before, expert, after):
                        apply_ln(s + 1, 1 - par, after)
                        x_lo(s + 1, 1 - par)
                        hidden_lo(s, par, 0)
                        weigh(s - 1, half - 1 + par, 1 - par, before)
                        hidden_lo(s, par, 1)

                    dve.wait_ge(b2_loaded, 16)
                    first = experts_of(ENG.DVE, 0, 1)
                    apply_ln(0, 0, first[0])
                    x_lo(0, 0)
                    over_tiles5(dve, ENG.DVE, tick, -1, 3)
                    last = experts_of(ENG.DVE, ST - 1, 1)
                    weigh(ST - 1, (ST - 1) // 2, (ST - 1) % 2, last[0])

def kernel(**inputs):
    import numpy as np
    import concourse.bacc as bacc
    from concourse.bass_utils import run_bass_kernel_spmd as run

    nc = bacc.Bacc("TRN2", target_bir_lowering=False, num_devices=1)
    arrays, aps = {}, {}
    for name, value in inputs.items():
        value = np.ascontiguousarray(value)
        arrays[f"in_{name}"] = value
        aps[name] = nc.dram_tensor(f"in_{name}", value.shape, mybir.dt.from_np(value.dtype), kind="ExternalInput").ap()
    n, d = inputs["x"].shape
    out = nc.dram_tensor("out_0", (n + P, d), F32, kind="ExternalOutput").ap()
    build(nc, aps, out)
    result = run(nc, [arrays], core_ids=[0]).results[0]["out_0"]
    return result[:n]
```
